# Optimizing a Trainium2 kernel written in Bass

```python
import numpy as np
import jax
import jax.numpy as jnp

def _softmax(x, axis=-1):
    return jax.nn.softmax(x, axis=axis)

def _gelu(x):
    return jax.nn.gelu(x, approximate=True)

def _silu(x):
    return jax.nn.silu(x)

def _sigmoid(x):
    return jax.nn.sigmoid(x)

def _layernorm(x, axis=-1, eps=1e-05):
    m = jnp.mean(x, axis=axis, keepdims=True)
    v = jnp.var(x, axis=axis, keepdims=True)
    return (x - m) / jnp.sqrt(v + eps)

def _scatter_add(tgt, idx, src, axis=0):
    return tgt.at[idx].add(src)

def _segment_sum(src, seg, n):
    return jax.ops.segment_sum(src, seg, n)
kernel_name = 'mk_perceiver_d1_seqx_r4_c825d0'

def setup_inputs(seed: int=0):
    np.random.seed(seed)
    _w = jnp.asarray

    def _rec_inputs():
        import jax
        import jax.numpy as jnp
        _rk = jax.random.key(seed)
        x = 7.22e-05 + 1 * jax.random.normal(jax.random.fold_in(_rk, 1), (32, 32, 1024), jnp.float32)
        _lenS = 32 - jax.random.randint(jax.random.fold_in(_rk, 7), (32,), 0, max(1, 32 // 4) + 1, jnp.int32)
        _lenS2 = 257 - jax.random.randint(jax.random.fold_in(_rk, 8), (32,), 0, max(1, 257 // 4) + 1, jnp.int32)
        _ctx_4096P = jax.random.normal(jax.random.fold_in(_rk, 11), (32, 16, 1024), jnp.float32)
        _ctx_4096c = jax.random.dirichlet(jax.random.fold_in(_rk, 511), 0.3 * jnp.ones((16,), jnp.float32), (32, 257))
        _ctx_4096t = jnp.einsum('bsk,bkd->bsd', _ctx_4096c, _ctx_4096P)
        _ctx_4096t = _ctx_4096t * jax.lax.rsqrt(jnp.mean(jnp.square(_ctx_4096t)) + 1e-12) * 0.953939
        ctx_4096 = 4.13588e-05 + 0.999923 * (_ctx_4096t + 0.3 * jax.random.normal(jax.random.fold_in(_rk, 611), (32, 257, 1024), jnp.float32))
        return (x, ctx_4096)
    x, ctx_4096 = _rec_inputs()

    def _L0_xattn_setup():
        import jax, jax.numpy as jnp
        import numpy as np
        DIM = 1024
        NUM_HEADS = 32
        NUM_KV_HEADS = 8
        HEAD_DIM = DIM // NUM_HEADS
        KV_DIM = DIM // (NUM_HEADS // NUM_KV_HEADS)
        B, S = (1, 512)
        key = jax.random.key(seed)
        ks = jax.random.split(key, 7)
        w_scale = DIM ** (-0.5)
        return {'query': jax.random.normal(ks[0], (B, S, DIM), jnp.float32), 'key': jax.random.normal(ks[1], (B, S, DIM), jnp.float32), 'value': jax.random.normal(ks[2], (B, S, DIM), jnp.float32), 'Wq': jax.random.normal(ks[3], (DIM, DIM), jnp.float32) * w_scale, 'Wk': jax.random.normal(ks[4], (DIM, KV_DIM), jnp.float32) * w_scale, 'Wv': jax.random.normal(ks[5], (DIM, KV_DIM), jnp.float32) * w_scale, 'Wo': jax.random.normal(ks[6], (DIM, DIM), jnp.float32) * w_scale}
    _L0_xattn_all = _L0_xattn_setup()
    _L0_xattn_in = {k: v for k, v in _L0_xattn_all.items() if k in ('Wq', 'Wk', 'Wv', 'Wo')}
    del _L0_xattn_all

    def _L0_attn_setup():
        import jax, jax.numpy as jnp
        import numpy as np
        B, C, L = (32, 128, 1024)
        key = jax.random.key(seed)
        k1, = jax.random.split(key, 1)
        minibatch = jax.random.normal(k1, (B, C, L), dtype=jnp.float32)
        eta = jnp.zeros((1,), dtype=jnp.float32)
        return {'minibatch': minibatch, 'eta': eta}
    _L0_attn_all = _L0_attn_setup()
    _L0_attn_in = {k: v for k, v in _L0_attn_all.items() if k in ('eta',)}
    del _L0_attn_all

    def _L0_ffn_setup():
        import jax, jax.numpy as jnp
        import numpy as np
        TOP_K = 2
        key = jax.random.key(seed)
        k1, k2, k3 = jax.random.split(key, 3)
        B, S, H, O, E = (2048, 1, 1024, 1024, 8)
        x = jax.random.normal(k1, (B, S, H), dtype=jnp.float32)
        gate_w = jax.random.normal(k2, (H, E), dtype=jnp.float32) * 0.02
        expert_w = jax.random.normal(k3, (E, H, O), dtype=jnp.float32) * 0.02
        return {'x': x, 'gate_w': gate_w, 'expert_w': expert_w}
    _L0_ffn_all = _L0_ffn_setup()
    _L0_ffn_in = {k: v for k, v in _L0_ffn_all.items() if k in ('gate_w', 'expert_w')}
    del _L0_ffn_all
    return {'x': x, 'ctx_4096': ctx_4096, 'L0_xattn_Wq': _L0_xattn_in['Wq'], 'L0_xattn_Wk': _L0_xattn_in['Wk'], 'L0_xattn_Wv': _L0_xattn_in['Wv'], 'L0_xattn_Wo': _L0_xattn_in['Wo'], 'L0_attn_eta': _L0_attn_in['eta'], 'L0_ffn_gate_w': _L0_ffn_in['gate_w'], 'L0_ffn_expert_w': _L0_ffn_in['expert_w']}

def reference(x, ctx_4096, L0_xattn_Wq, L0_xattn_Wk, L0_xattn_Wv, L0_xattn_Wo, L0_attn_eta, L0_ffn_gate_w, L0_ffn_expert_w):
    import jax
    import jax.numpy as jnp

    def _L0_xattn_ref(query, key, value, Wq, Wk, Wv, Wo):
        import jax, jax.numpy as jnp
        import numpy as np
        DIM = 1024
        NUM_HEADS = 32
        NUM_KV_HEADS = 8
        HEAD_DIM = DIM // NUM_HEADS
        KV_DIM = DIM // (NUM_HEADS // NUM_KV_HEADS)
        B, S = (1, 512)
        b, sq, _ = query.shape
        _, sk, _ = key.shape
        rep = NUM_HEADS // NUM_KV_HEADS
        q = (query @ Wq).reshape(b, sq, NUM_HEADS, HEAD_DIM).transpose(0, 2, 1, 3)
        k = (key @ Wk).reshape(b, sk, NUM_KV_HEADS, HEAD_DIM).transpose(0, 2, 1, 3)
        v = (value @ Wv).reshape(b, sk, NUM_KV_HEADS, HEAD_DIM).transpose(0, 2, 1, 3)
        k = jnp.repeat(k, rep, axis=1)
        v = jnp.repeat(v, rep, axis=1)
        scale = HEAD_DIM ** (-0.5)
        scores = jnp.einsum('bhqd,bhkd->bhqk', q, k) * scale
        probs = jax.nn.softmax(scores, axis=-1)
        out = jnp.einsum('bhqk,bhkd->bhqd', probs, v)
        out = out.transpose(0, 2, 1, 3).reshape(b, sq, DIM)
        return out @ Wo

    def _L0_attn_ref(minibatch, eta):
        import jax, jax.numpy as jnp
        import numpy as np
        B, C, L = (32, 128, 1024)
        logits = jnp.einsum('bcl,bdl->bcd', minibatch, minibatch)
        logits_new = jnp.max(logits, axis=-1, keepdims=True) - logits
        probs = jax.nn.softmax(logits_new, axis=-1)
        read = jnp.einsum('bcd,bdl->bcl', probs, minibatch)
        return eta * read + minibatch

    def _L0_ffn_ref(x, gate_w, expert_w):
        import jax, jax.numpy as jnp
        import numpy as np
        TOP_K = 2
        E = gate_w.shape[-1]
        logits = jnp.einsum('bsh,he->bse', x, gate_w)
        topv, topi = jax.lax.top_k(logits, TOP_K)
        w = jax.nn.softmax(topv, axis=-1)
        onehot = jax.nn.one_hot(topi, E, dtype=x.dtype)
        w_e = jnp.einsum('bske,bsk->bse', onehot, w)
        out = jnp.einsum('bsh,eho,bse->bso', x, expert_w, w_e)
        return out
    x = x + _L0_xattn_ref(_layernorm(x, axis=-1), ctx_4096, ctx_4096, L0_xattn_Wq, L0_xattn_Wk, L0_xattn_Wv, L0_xattn_Wo)
    x = x + _L0_attn_ref(_layernorm(x, axis=-1), L0_attn_eta)
    x = x + _L0_ffn_ref(_layernorm(x, axis=-1), L0_ffn_gate_w, L0_ffn_expert_w)
    return x

_drawn_inputs = setup_inputs


def setup_inputs(seed=0):
    import zlib

    import numpy as np

    out = dict(_drawn_inputs(seed))
    spreads = {}
    factors = {}
    for name, (base, spread) in spreads.items():
        noise = np.random.default_rng([zlib.crc32(name.encode()), seed]).standard_normal(out[name].shape)
        drawn = base * np.exp(spread * noise) if base else spread * noise
        out[name] = jnp.asarray(drawn.astype(out[name].dtype))
    for name, factor in factors.items():
        out[name] = (out[name] * factor).astype(out[name].dtype)
    return out
```

```python
from contextlib import ExitStack

import concourse.bass as bass
from concourse import mybir

ALU = mybir.AluOpType
ACT = mybir.ActivationFunctionType
AXX = mybir.AxisListType.X
F32 = mybir.dt.float32
F32R = mybir.dt.float32r
U32 = mybir.dt.uint32
I32 = mybir.dt.int32

P = 128
B = 32
SQ = 32
SK = 257
D = 1024
KC = D // P
NH, NG, DH = 32, 8, 32
REP = NH // NG
KV = NG * DH
NT = B * SQ // P
BT = P // SQ
SCALE = DH ** -0.5
EPS = 1e-5
E = 8
SKP = SK + 1
PASSES = ((0, 0), (0, 1), (1, 0))


def pipelined(eng, n, step, head=1, tail=1):
    assert head % 2 == 1
    pairs = (n - head - tail) // 2
    for t in range(head):
        step(t, t % 2)
    with eng.Fori(0, pairs) as i:
        step(2 * i + head, head % 2)
        step(2 * i + head + 1, (head + 1) % 2)
    for t in range(head + 2 * pairs, n):
        step(t, t % 2)


def wait_apart(eng, sem, value, passed):
    eng.wait_ge(sem, value)
    if not known(value):
        eng.sem_inc(passed, 1)


def known(t):
    return isinstance(t, int)


class Norm:

    def __init__(self, nc, ctx, name):
        self.stats = ctx.enter_context(nc.sbuf_tensor(name + "_stats", [P, 2, 6], F32))
        self.mean_var = ctx.enter_context(nc.sbuf_tensor(name + "_mean_var", [P, 2], F32))
        self.rstd = ctx.enter_context(nc.sbuf_tensor(name + "_rstd", [P, 1], F32))
        self.var_eps = ctx.enter_context(nc.sbuf_tensor(name + "_var_eps", [P, 1], F32))
        self.minus_half = ctx.enter_context(nc.sbuf_tensor(name + "_minus_half", [P, 1], F32))
        self.eps_added = ctx.enter_context(nc.semaphore(name + "_eps_added"))
        self.passed = ctx.enter_context(nc.semaphore(name + "_passed"))
        self.stats_ready = ctx.enter_context(nc.semaphore(name + "_stats_ready"))
        self.var_ready = ctx.enter_context(nc.semaphore(name + "_var_ready"))
        self.rstd_ready = ctx.enter_context(nc.semaphore(name + "_rstd_ready"))

    def on_vector(self, dve, t, out, src):
        for h in range(2):
            dve.bn_stats(self.stats[:, h, :], src[:, h * 512:(h + 1) * 512]).then_inc(self.stats_ready, 1)
        wait_apart(dve, self.stats_ready, 2 * t + 2, self.passed)
        dve.bn_aggr(self.mean_var[:, :], self.stats[:, :, :].rearrange("p a b -> p (a b)")).then_inc(self.var_ready, 1)
        dve.wait_ge(self.rstd_ready, t + 1)
        return dve.tensor_scalar(out, src, self.mean_var[:, 0:1], self.rstd[:, 0:1], ALU.subtract, ALU.mult)

    def start_gpsimd(self, pool):
        pool.memset(self.minus_half[:, :], -0.5).then_inc(self.eps_added, 1)
        pool.wait_ge(self.eps_added, 1)

    def on_gpsimd(self, pool, t):
        wait_apart(pool, self.var_ready, t + 1, self.passed)
        pool.tensor_scalar(self.var_eps[:, :], self.mean_var[:, 1:2], EPS, None, ALU.add).then_inc(self.eps_added, 1)
        pool.wait_ge(self.eps_added, t + 2)
        pool.tensor_tensor(self.rstd[:, :], self.var_eps[:, :], self.minus_half[:, :], ALU.pow).then_inc(self.rstd_ready, 1)


def queries(nc, ident, banks, chunk_loaded, x, wq, wk, wv, q_dram, wq_raw, wkv):
    with ExitStack() as ctx:
        sb = lambda *a: ctx.enter_context(nc.sbuf_tensor(*a))
        sem = lambda n: ctx.enter_context(nc.semaphore(n))
        wkv_raw = sb("wkv_raw", [P, KC, 2 * KV], F32)
        wq_s = [sb("wq_h", [P, KC, D], F32R), sb("wq_l", [P, KC, D], F32R)]
        x_in = sb("x_in", [P, 2, D], F32)
        xn = sb("xn", [P, 2, D], F32)
        xT = [sb("xT_h", [P, 2, D], F32R), sb("xT_l", [P, 2, D], F32R)]
        q_sb = sb("q_sb", [P, 2, D], F32)
        qT = [sb("qT_h", [P, 2, D], F32R), sb("qT_l", [P, 2, D], F32R)]
        norm = Norm(nc, ctx, "norm1")
        xT_ps = banks[0:2]
        q_ps = [banks[2:4], banks[4:6]]
        qT_ps = banks[6:8]

        x_loaded = [sem("x_loaded0"), sem("x_loaded1")]
        wkv_loaded = [sem("wk_loaded"), sem("wv_loaded")]
        ident_zero, ident_ready = sem("ident_zero"), sem("ident_ready")
        wq_h_ready, wq_ready = sem("wq_h_ready"), sem("wq_ready")
        wkv_h_ready, wkv_l_ready = sem("wkv_h_ready"), sem("wkv_l_ready")
        xn_ready, xT_done, xT_h_ready, xT_l_ready = sem("xn_ready"), sem("xT_done"), sem("xT_h_ready"), sem("xT_l_ready")
        q_done, q_copied, qT_done, qT_h_ready, qT_l_ready = (
            sem("q_done"), sem("q_copied"), sem("qT_done"), sem("qT_h_ready"), sem("qT_l_ready"))
        q_stored = [sem("q_stored0"), sem("q_stored1")]

        by_batch = lambda ap: ap.rearrange("p (b m q) -> p m b q", b=BT, q=SQ)

        block = ctx.enter_context(nc.Block())

        @block.sync
        def _(sp):
            def load_x(t, par):
                sp.dma_start(x_in[:, par, :], x[bass.ts(t, P), :]).then_inc(x_loaded[par], 16)
            load_x(0, 0)
            for c in range(KC):
                sp.dma_start(wq_raw[:, c, :], wq[c * P:(c + 1) * P, :]).then_inc(chunk_loaded[c], 16)
                if c == 0:
                    load_x(1, 1)
            for n, w in enumerate((wk, wv)):
                sp.dma_start(wkv_raw[:, :, n * KV:(n + 1) * KV], w.rearrange("(c p) n -> p c n", p=P)).then_inc(wkv_loaded[n], 16)

            def step(t, par):
                if not known(t) or t + 2 < NT:
                    sp.wait_ge(xn_ready, t + 1)
                    load_x(t + 2, par)
            pipelined(sp, NT, step, tail=3)
            for par in range(2):
                sp.wait_ge(q_stored[par], 32 * NT // 2)

        @block.gpsimd
        def _(pool):
            pool.memset(ident[:, :], 0.0).then_inc(ident_zero, 1)
            pool.wait_ge(ident_zero, 1)
            pool.affine_select(out=ident[:, :], in_=ident[:, :], compare_op=ALU.not_equal, fill=1.0, base=0,
                               pattern=[[-1, P]], channel_multiplier=1).then_inc(ident_ready, 1)
            norm.start_gpsimd(pool)
            pipelined(pool, NT, lambda t, par: norm.on_gpsimd(pool, t))

        @block.scalar
        def _(act):
            def xT_high(t, par):
                if not known(t) or t >= 2:
                    act.wait_ge(q_done, 2 * t - 2)
                for h in range(2):
                    act.wait_ge(xT_done, 2 * t + h + 1)
                    act.activation(xT[0][:, par, h * 512:(h + 1) * 512], xT_ps[h][:, :], ACT.Copy).then_inc(xT_h_ready, 1)
            xT_high(0, 0)
            for c in range(KC):
                act.wait_ge(chunk_loaded[c], 16)
                act.activation(wq_s[0][:, c, :], wq_raw[:, c, :], ACT.Copy).then_inc(wq_h_ready, 1)

            def step(t, par):
                if not known(t) or t + 1 < NT:
                    xT_high(t + 1, 1 - par)
                if known(t) and t == 0:
                    for n in range(2):
                        act.wait_ge(wkv_loaded[n], 16)
                    for c in range(KC):
                        act.activation(wkv[0][:, c, :], wkv_raw[:, c, :], ACT.Copy).then_inc(wkv_h_ready, 1)
                for h in range(2):
                    act.wait_ge(q_done, 2 * t + h + 1)
                    if h == 0 and (not known(t) or t >= 2):
                        act.wait_ge(qT_done, 2 * t - 2)
                    act.activation(q_sb[:, par, h * 512:(h + 1) * 512], q_ps[par][h][:, :], ACT.Copy).then_inc(q_copied, 1)
                if not known(t) or t >= 1:
                    qT_high(t - 1, 1 - par)
                if not known(t) or t >= 2:
                    store_q(t - 2, par)

            def store_q(t, par):
                act.wait_ge(qT_l_ready, t + 1)
                for part in range(2):
                    act.dma_start(q_dram[part, bass.ds(t, 1)].rearrange("a p n -> p (a n)"),
                                  qT[part][:, par, :].bitcast(F32)).then_inc(q_stored[par], 16)

            def qT_high(t, par):
                if not known(t) or t >= 2:
                    act.wait_ge(q_stored[par], (t - par) * 16)
                for h in range(2):
                    act.wait_ge(qT_done, 2 * t + h + 1)
                    o = act.activation(by_batch(qT[0][:, par, :])[:, 4 * h:4 * h + 4],
                                       qT_ps[h][:, :].rearrange("p (m b q) -> p m b q", m=4, q=SQ), ACT.Copy, scale=SCALE)
                    if h == 1:
                        o.then_inc(qT_h_ready, 1)
            pipelined(act, NT, step, head=3)
            store_q(6, 0)
            qT_high(7, 1)
            store_q(7, 1)

        @block.vector
        def _(dve):
            def normalize(t, par):
                dve.wait_ge(x_loaded[par], (t - par) * 8 + 16)
                if not known(t) or t >= 2:
                    dve.wait_ge(xT_done, 2 * t - 2)
                norm.on_vector(dve, t, xn[:, par, :], x_in[:, par, :]).then_inc(xn_ready, 1)

            def xT_low(t, par):
                for h in range(2):
                    dve.wait_ge(xT_h_ready, 2 * t + h + 1)
                    dve.tensor_tensor(xT[1][:, par, h * 512:(h + 1) * 512], xT_ps[h][:, :],
                                      xT[0][:, par, h * 512:(h + 1) * 512].bitcast(F32), ALU.subtract).then_inc(xT_l_ready, 1)

            def qT_low(t, par):
                if not known(t) or t >= 2:
                    dve.wait_ge(q_stored[par], (t - par) * 16)
                dve.wait_ge(qT_h_ready, t + 1)
                for h in range(2):
                    for m in range(4):
                        o = dve.scalar_tensor_tensor(out=by_batch(qT[1][:, par, :])[:, 4 * h + m],
                                                     in0=qT_ps[h][:, m * P:(m + 1) * P].rearrange("p (b q) -> p b q", q=SQ),
                                                     scalar=SCALE, in1=by_batch(qT[0][:, par, :])[:, 4 * h + m].bitcast(F32),
                                                     op0=ALU.mult, op1=ALU.subtract)
                o.then_inc(qT_l_ready, 1)

            normalize(0, 0)
            normalize(1, 1)
            xT_low(0, 0)
            for c in range(KC):
                dve.wait_ge(wq_h_ready, c + 1)
                dve.tensor_tensor(wq_s[1][:, c, :], wq_raw[:, c, :], wq_s[0][:, c, :].bitcast(F32), ALU.subtract).then_inc(wq_ready, 1)

            def step(t, par):
                if not known(t) or t + 1 < NT:
                    if not known(t) or t >= 1:
                        normalize(t + 1, 1 - par)
                    xT_low(t + 1, 1 - par)
                if known(t) and t == 0:
                    dve.wait_ge(wkv_h_ready, KC)
                    for c in range(KC):
                        dve.tensor_tensor(wkv[1][:, c, :], wkv_raw[:, c, :], wkv[0][:, c, :].bitcast(F32),
                                          ALU.subtract).then_inc(wkv_l_ready, 1)
                if not known(t) or t >= 1:
                    qT_low(t - 1, 1 - par)
            pipelined(dve, NT, step, head=3)
            qT_low(7, 1)

        @block.tensor
        def _(pe):
            def transpose_x(t, par):
                pe.wait_ge(xn_ready, t + 1)
                for k in range(KC):
                    if k % 4 == 0 and (not known(t) or t >= 1):
                        pe.wait_ge(xT_l_ready, 2 * t - 1 + k // 4)
                    o = pe.transpose(xT_ps[k // 4][:, k % 4 * P:(k % 4 + 1) * P], xn[:, par, k * P:(k + 1) * P], ident[:, :])
                    if k % 4 == 3:
                        o.then_inc(xT_done, 1)

            def transpose_q(t, par):
                pe.wait_ge(q_copied, 2 * t + 2)
                if not known(t) or t >= 1:
                    pe.wait_ge(qT_l_ready, t)
                for k in range(KC):
                    o = pe.transpose(qT_ps[k // 4][:, k % 4 * P:(k % 4 + 1) * P], q_sb[:, par, k * P:(k + 1) * P], ident[:, :])
                    if k % 4 == 3:
                        o.then_inc(qT_done, 1)

            pe.wait_ge(ident_ready, 1)
            transpose_x(0, 0)

            def step(t, par):
                pe.wait_ge(xT_l_ready, 2 * t + 2)
                if not known(t) or t >= 2:
                    pe.wait_ge(q_copied, 2 * t - 2)
                for k in range(KC):
                    if known(t) and t == 0:
                        pe.wait_ge(wq_ready, k + 1)
                    if k == 4 and (not known(t) or t + 1 < NT):
                        transpose_x(t + 1, 1 - par)
                    if k == 6 and (not known(t) or t >= 1):
                        transpose_q(t - 1, 1 - par)
                    for h in range(2):
                        for n, (a, b) in enumerate(PASSES):
                            o = pe.matmul(q_ps[par][h][:, :], xT[a][:, par, k * P:(k + 1) * P],
                                          wq_s[b][:, k, h * 512:(h + 1) * 512],
                                          start=(k == 0 and n == 0), stop=(k == KC - 1 and n == 2))
                        if k == KC - 1:
                            o.then_inc(q_done, 1)
            pipelined(pe, NT, step, head=3)
            transpose_q(7, 1)


def slot_head(s):
    return s % 2, s // 2


def slot_cols(s):
    j, g = slot_head(s)
    return slice((4 * j + g) * DH, (4 * j + g + 1) * DH)


def over_batches(eng, step):
    pipelined(eng, B + 2, step, head=3, tail=5)


class Stages:

    def __init__(self, b):
        self.project = not known(b) or b < B
        self.next = not known(b) or b + 1 < B
        self.heads = not known(b) or 1 <= b <= B
        self.rest = not known(b) or b >= 2


TURNED_BY_SCALAR = (1, 4, 6)


def cross_attention(nc, ident, banks, ctx_dram, q_dram, k_dram, vlast_dram, wkv, oT):
    with ExitStack() as ctx:
        sb = lambda *a: ctx.enter_context(nc.sbuf_tensor(*a))
        sem = lambda n: ctx.enter_context(nc.semaphore(n))
        parts = lambda n, s: [sb(n + "_h", s, F32R), sb(n + "_l", s, F32R)]
        cx = sb("cx", [P, 2, 2, D], F32)
        cT = parts("cT", [P, 2, KC, 2 * P])
        kT = parts("kT", [P, 2, 2, SKP])
        kcat = sb("kcat", [P, 2, 4 * 2, SKP], F32R)
        qcat = sb("qcat", [P, 2, NG, REP * SQ], F32R)
        v_sb = sb("v_sb", [P, 2, 2, KV], F32)
        vl = sb("vl", [NG, 2, KV], F32)
        prob = sb("prob", [P, 2, NG, SKP], F32)
        pT = sb("pT", [P, NG, 2 * P], F32)
        plT = sb("plT", [NG, P], F32)
        nmax = sb("nmax", [P, 2, NG], F32)
        sums = sb("sums", [P, 2, NG], F32)
        rsums = sb("rsums", [P, NG], F32)
        o_sb = sb("o_sb", [P, KV], F32)
        cl = sb("cl", [B, D], F32)
        clT = parts("clT", [P, KC, P])
        kl = parts("kl", [P, 2, B])
        vl_sb = sb("vl_sb", [B, KV], F32)
        zeros = sb("zeros", [P, 512], F32)
        cT_ps, k_ps, v_ps, s_ps = banks[0:2], banks[2], banks[3], banks[4:6]
        turn_ps = banks[6][:, 0:256]
        o_ps = banks[7]

        cx_loaded = [sem("cx_loaded0"), sem("cx_loaded1")]
        kcat_loaded = [sem("kcat_loaded0"), sem("kcat_loaded1")]
        qcat_loaded = [sem("qcat_loaded0"), sem("qcat_loaded1")]
        vl_loaded = [sem("vl_loaded0"), sem("vl_loaded1")]
        cl_loaded, zeros_ready, pads_ready, vl_zeroed, vl_placed = (
            sem("cl_loaded"), sem("zeros_ready"), sem("pads_ready"), sem("vl_zeroed"), sem("vl_placed"))
        clT_done, clT_h_ready, clT_l_ready, kvl_done, kl_h_ready, kl_l_ready, vl_copied = (
            sem("clT_done"), sem("clT_h_ready"), sem("clT_l_ready"), sem("kvl_done"), sem("kl_h_ready"),
            sem("kl_l_ready"), sem("vl_copied"))
        cT_done, cT_h_ready, cT_l_ready = sem("cT_done"), sem("cT_h_ready"), sem("cT_l_ready")
        k_done, kT_h_ready, kT_l_ready, klast_ready = sem("k_done"), sem("kT_h_ready"), sem("kT_l_ready"), sem("klast_ready")
        v_done, v_copied = sem("v_done"), sem("v_copied")
        s_done, max_done, exp_done = sem("s_done"), sem("max_done"), sem("exp_done")
        k_stored = [sem("k_h_stored"), sem("k_l_stored")]
        passed = sem("passed1")
        turned, turn_copied = sem("turned"), sem("turn_copied")
        last_turned, last_copied, o_turned, o_turn_copied = (
            sem("last_turned"), sem("last_copied"), sem("o_turned"), sem("o_turn_copied"))
        pv_done, o_done, o_copied, rsums_ready = sem("pv_done"), sem("o_done"), sem("o_copied"), sem("rsums_ready")

        def copy_turned(eng, copy, a, i):
            if not known(a) or a >= 1:
                eng.wait_ge(pv_done, NG * (a - 1) + i + 1)
            eng.wait_ge(turned, NG * a + i + 1)
            copy(pT[:, i, :], turn_ps).then_inc(turn_copied, 1)

        block = ctx.enter_context(nc.Block())

        @block.sync
        def _(sp):
            def load_cx(b, par):
                sp.dma_start(cx[:, par, :, :].rearrange("p a n -> p (a n)"),
                             ctx_dram[bass.ds(b, 1), 0:2 * P, :].rearrange("o (p a) n -> p (o a n)", a=2)).then_inc(cx_loaded[par], 16)

            load_cx(0, 0)
            sp.dma_start(cl[:, :], ctx_dram[:, 2 * P, :]).then_inc(cl_loaded, 16)
            load_cx(1, 1)
            sp.wait_ge(zeros_ready, 1)
            sp.dma_start(vlast_dram.rearrange("b s n -> (b s n)").rearrange("(p n) -> p n", p=P), zeros[:, :]).then_inc(vl_zeroed, 16)
            sp.wait_ge(vl_zeroed, 16)
            sp.wait_ge(vl_copied, 1)
            for s in range(NG):
                sp.dma_start(vlast_dram[:, s, slot_cols(s)], vl_sb[:, slot_cols(s)]).then_inc(vl_placed, 16)

            def step(b, par):
                st = Stages(b)
                if not st.project:
                    return
                if not known(b) or b >= 2:
                    sp.wait_ge(s_done, NG * (b - 1))
                if not known(b) or b + 2 < B:
                    sp.wait_ge(cT_done, 4 * b + 4)
                    load_cx(b + 2, par)
                for part, ready in enumerate((kT_h_ready, kT_l_ready)):
                    if part == 0:
                        wait_apart(sp, klast_ready, 2 * b + 2, passed)
                    sp.wait_ge(ready, b + 1)
                    sp.dma_start(k_dram[part, par], kT[part][:, par, :, :].rearrange("p j n -> p (j n)").bitcast(F32)).then_inc(k_stored[part], 16)
                for part in range(2):
                    sp.wait_ge(k_stored[part], 16 * b + 16)
                    for c in (part, part + 2):
                        sp.dma_start(kcat[c * DH:(c + 1) * DH, par, :, :].rearrange("d (g j) n -> d g (j n)", g=4).bitcast(F32),
                                     k_dram[part, par].rearrange("(g d) n -> d g n", g=4)).then_inc(kcat_loaded[par], 16)

            over_batches(sp, step)

        @block.gpsimd
        def _(pool):
            pool.memset(zeros[:, :], 0.0).then_inc(zeros_ready, 1)
            for part in range(2):
                pool.memset(clT[part][:, :, :].bitcast(F32), 0.0).then_inc(pads_ready, 1)
                pool.memset(kT[part][:, :, :, SK:SKP].bitcast(F32), 0.0).then_inc(pads_ready, 1)
            pool.wait_ge(kl_l_ready, 1)
            pool.wait_ge(vl_placed, 16 * NG)

            def q_of_batch(b, part):
                return q_dram[part, bass.ds(b // BT, 1), :, bass.ds((b % BT) * NG * SQ, NG * SQ)].rearrange("o (g d) n -> d (o g) n", g=4)

            def step(b, par):
                st = Stages(b)
                if st.project:
                    if not known(b) or b >= 2:
                        pool.wait_ge(k_stored[0], 16 * b - 16)
                        pool.wait_ge(k_stored[1], 16 * b - 16)
                    for part in range(2):
                        pool.tensor_copy(kT[part][:, par, :, SK - 1:SK], kl[part][:, :, bass.ds(b, 1)].bitcast(F32)).then_inc(klast_ready, 1)
                if st.heads:
                    if not known(b) or b >= 3:
                        pool.wait_ge(o_done, b - 2)
                    pool.dma_start(vl[:, 1 - par, :], vlast_dram[bass.ds(b - 1, 1)].rearrange("o s n -> s (o n)")).then_inc(vl_loaded[1 - par], 16)
                if not st.project:
                    return
                if not known(b) or b >= 2:
                    pool.wait_ge(s_done, NG * (b - 1))
                for c in range(4):
                    pool.dma_start(qcat[c * DH:(c + 1) * DH, par, :, :].rearrange("d (g j) n -> d g (j n)", g=4).bitcast(F32),
                                   q_of_batch(b, c // 2)).then_inc(qcat_loaded[par], 16)
            over_batches(pool, step)

        @block.scalar
        def _(act):
            def context_high(b, par, m):
                if not known(b) or b >= 2:
                    act.wait_ge(v_done, b - 1)
                act.wait_ge(cT_done, 4 * b + m + 1)
                act.activation(cT[0][:, par, 2 * m:2 * m + 2, :].rearrange("p a n -> p (a n)"), cT_ps[m % 2][:, :], ACT.Copy).then_inc(cT_h_ready, 1)

            def copy_v(b, par):
                if not known(b) or b >= 2:
                    act.wait_ge(pv_done, NG * (b - 1))
                act.wait_ge(v_done, b + 1)
                act.activation(v_sb[:, par, :, :].rearrange("p a n -> p (a n)"), v_ps[:, :], ACT.Copy).then_inc(v_copied, 1)

            act.wait_ge(pads_ready, 4)
            act.wait_ge(clT_done, 1)
            act.activation(clT[0][:, :, 0:B], cT_ps[0][:, 0:KC * B].rearrange("p (k b) -> p k b", b=B), ACT.Copy).then_inc(clT_h_ready, 1)
            act.wait_ge(kvl_done, 2)
            act.activation(kl[0][:, :, :].rearrange("p j b -> p (j b)"), k_ps[:, 0:2 * B], ACT.Copy).then_inc(kl_h_ready, 1)
            act.activation(vl_sb[:, :], v_ps[0:B, 0:KV], ACT.Copy).then_inc(vl_copied, 1)
            for m in range(4):
                context_high(0, 0, m)

            def step(b, par):
                st = Stages(b)
                for s in range(NG):
                    if s == 0 and (not known(b) or 1 <= b <= B):
                        copy_v(b - 1, 1 - par)
                    if st.heads:
                        act.wait_ge(max_done, NG * (b - 1) + s + 1)
                        act.activation(prob[:, 1 - par, s, 0:SK], s_ps[s % 2][:, 0:SK], ACT.Exp, bias=nmax[:, 1 - par, s:s + 1],
                                       accum_out=sums[:, 1 - par, s:s + 1]).then_inc(exp_done, 1)
                    i = (s - 2) % NG
                    if i in TURNED_BY_SCALAR and (st.rest if s < 2 else st.heads):
                        copy_turned(act, act.copy, b - 2 if s < 2 else b - 1, i)
                    if s == 2 and st.rest:
                        act.wait_ge(last_turned, b - 1)
                        act.activation(plT[:, :], v_ps[0:NG, 0:P], ACT.Copy).then_inc(last_copied, 1)
                    if s == 5 and st.rest:
                        act.wait_ge(o_turned, b - 1)
                        act.activation(oT[:, :, bass.ds((b - 2) * SQ, SQ)],
                                       k_ps[:, 0:2 * P].rearrange("p (m q) -> p m q", q=SQ), ACT.Copy).then_inc(o_turn_copied, 1)
                    if s % 2 == 1 and st.next:
                        context_high(b + 1, 1 - par, s // 2)
                    if s == 4 and st.project:
                        if not known(b) or b >= 2:
                            act.wait_ge(k_stored[0], 16 * b - 16)
                        act.wait_ge(k_done, b + 1)
                        act.activation(kT[0][:, par, :, 0:2 * P], k_ps[:, :].rearrange("p (j n) -> p j n", j=2), ACT.Copy).then_inc(kT_h_ready, 1)
            over_batches(act, step)

        @block.vector
        def _(dve):
            def context_low(b, par, m):
                dve.wait_ge(cT_h_ready, 4 * b + m + 1)
                high = cT[0][:, par, 2 * m:2 * m + 2, :].rearrange("p a n -> p (a n)").bitcast(F32)
                dve.tensor_tensor(cT[1][:, par, 2 * m:2 * m + 2, :].rearrange("p a n -> p (a n)"), cT_ps[m % 2][:, :],
                                  high, ALU.subtract).then_inc(cT_l_ready, 1)

            dve.wait_ge(clT_h_ready, 1)
            dve.tensor_tensor(clT[1][:, :, 0:B], cT_ps[0][:, 0:KC * B].rearrange("p (k b) -> p k b", b=B),
                              clT[0][:, :, 0:B].bitcast(F32), ALU.subtract).then_inc(clT_l_ready, 1)
            dve.wait_ge(kl_h_ready, 1)
            dve.tensor_tensor(kl[1][:, :, :].rearrange("p j b -> p (j b)"), k_ps[:, 0:2 * B],
                              kl[0][:, :, :].rearrange("p j b -> p (j b)").bitcast(F32), ALU.subtract).then_inc(kl_l_ready, 1)
            for m in range(4):
                context_low(0, 0, m)

            def step(b, par):
                st = Stages(b)
                for s in range(NG):
                    if st.heads:
                        dve.wait_ge(s_done, NG * (b - 1) + s + 1)
                        dve.reduce_max(nmax[:, 1 - par, s:s + 1], s_ps[s % 2][:, 0:SK], AXX, negate=True).then_inc(max_done, 1)
                    i = (s - 2) % NG
                    if i not in TURNED_BY_SCALAR and (st.rest if s < 2 else st.heads):
                        copy_turned(dve, dve.tensor_copy, b - 2 if s < 2 else b - 1, i)
                    if s % 2 == 1 and st.next:
                        context_low(b + 1, 1 - par, s // 2)
                    if s == 3 and st.rest:
                        dve.wait_ge(o_done, b - 1)
                        dve.reciprocal(rsums[:, :].rearrange("p (j g) -> p j g", j=2),
                                       sums[:, par, :].rearrange("p (g j) -> p j g", j=2)).then_inc(rsums_ready, 1)
                        dve.wait_ge(rsums_ready, b - 1)
                        if not known(b) or b >= 3:
                            dve.wait_ge(o_turned, b - 2)
                        dve.tensor_tensor(o_sb[:, :].rearrange("p (g d) -> p g d", d=DH), o_ps[:, 0:KV].rearrange("p (g d) -> p g d", d=DH),
                                          rsums[:, :].unsqueeze(2).to_broadcast([P, NG, DH]), ALU.mult).then_inc(o_copied, 1)
                    if s == 4 and st.project:
                        if not known(b) or b >= 2:
                            dve.wait_ge(k_stored[1], 16 * b - 16)
                        dve.wait_ge(kT_h_ready, b + 1)
                        dve.tensor_tensor(kT[1][:, par, :, 0:2 * P], k_ps[:, :].rearrange("p (j n) -> p j n", j=2),
                                          kT[0][:, par, :, 0:2 * P].bitcast(F32), ALU.subtract).then_inc(kT_l_ready, 1)
            over_batches(dve, step)

        @block.tensor
        def _(pe):
            def transpose_context(b, par, m):
                if m == 0:
                    pe.wait_ge(cx_loaded[par], 8 * (b - par) + 16)
                if not known(b) or 4 * b + m >= 2:
                    pe.wait_ge(cT_l_ready, 4 * b + m - 1)
                for k in range(2 * m, 2 * m + 2):
                    for a in range(2):
                        n = (k % 2) * 2 + a
                        o = pe.transpose(cT_ps[m % 2][:, n * P:(n + 1) * P], cx[:, par, a, k * P:(k + 1) * P], ident[:, :])
                o.then_inc(cT_done, 1)

            def keys(b, par, s, first):
                j = s // 2
                for k in range(s % 2 * 4 + (0 if first else 2), s % 2 * 4 + (2 if first else 4)):
                    for n, (x, y) in enumerate(PASSES):
                        o = pe.matmul(k_ps[:, j * 256:(j + 1) * 256], wkv[x][:, k, j * P:(j + 1) * P], cT[y][:, par, k, :],
                                      start=(j == 0 and k == 0 and n == 0), stop=(j == 1 and k == KC - 1 and n == 2), skip_group_check=True)
                if s == 3 and not first:
                    o.then_inc(k_done, 1)

            def values(b, par, s, first):
                a = s // 2 - 2
                for k in range(s % 2 * 4 + (0 if first else 2), s % 2 * 4 + (2 if first else 4)):
                    for n, (x, y) in enumerate(PASSES):
                        o = pe.matmul(v_ps[:, a * KV:(a + 1) * KV], cT[x][:, par, k, a * P:(a + 1) * P], wkv[y][:, k, KV:2 * KV],
                                      start=(a == 0 and k == 0 and n == 0), stop=(a == 1 and k == KC - 1 and n == 2), skip_group_check=True)
                if s == 7 and not first:
                    o.then_inc(v_done, 1)

            def turn(dst, pieces):
                for n, (rows, src) in enumerate(pieces):
                    o = pe.transpose(dst[0:rows, n * P:(n + 1) * P], src, ident[:, :])
                return o

            def turn_prob(a, ap, i):
                pe.wait_ge(exp_done, NG * a + i + 1)
                if not known(a) or NG * a + i >= 1:
                    pe.wait_ge(turn_copied, NG * a + i)
                turn(turn_ps, [(P, prob[:, ap, i, c * P:(c + 1) * P]) for c in range(2)]).then_inc(turned, 1)

            def times_values(a, ap, i):
                pe.wait_ge(turn_copied, NG * a + i + 1)
                if i == 0:
                    pe.wait_ge(v_copied, a + 1)
                    if not known(a) or a >= 1:
                        pe.wait_ge(o_copied, a)
                for c in range(2):
                    o = pe.matmul(o_ps[:, slot_cols(i)], pT[:, i, c * P:(c + 1) * P], v_sb[:, ap, c, slot_cols(i)],
                                  start=(i == 0 and c == 0), stop=False, skip_group_check=True)
                o.then_inc(pv_done, 1)

            pe.wait_ge(cl_loaded, 16)
            for k in range(KC):
                o = pe.transpose(cT_ps[0][:, k * B:(k + 1) * B], cl[:, k * P:(k + 1) * P], ident[0:B, 0:B])
            o.then_inc(clT_done, 1)
            pe.wait_ge(clT_l_ready, 1)
            for j in range(2):
                for k in range(KC):
                    for n, (x, y) in enumerate(PASSES):
                        o = pe.matmul(k_ps[:, j * B:(j + 1) * B], wkv[x][:, k, j * P:(j + 1) * P], clT[y][:, k, 0:B],
                                      start=(j == 0 and k == 0 and n == 0), stop=(j == 1 and k == KC - 1 and n == 2), skip_group_check=True)
            o.then_inc(kvl_done, 1)
            for k in range(KC):
                for n, (x, y) in enumerate(PASSES):
                    o = pe.matmul(v_ps[:, 0:KV], clT[x][:, k, :], wkv[y][:, k, KV:2 * KV],
                                  start=(k == 0 and n == 0), stop=(k == KC - 1 and n == 2))
            o.then_inc(kvl_done, 1)
            for m in range(4):
                transpose_context(0, 0, m)
            pe.wait_ge(vl_copied, 1)

            def step(b, par):
                st = Stages(b)
                for s in range(NG):
                    if s < 4 and st.rest:
                        times_values(b - 2, par, s + 4)
                    if s == 3 and st.rest:
                        pe.wait_ge(last_copied, b - 1)
                        pe.wait_ge(vl_loaded[par], 8 * (b - 2 - par) + 16)
                        pe.matmul(o_ps[:, 0:KV], plT[:, :], vl[:, par, :], start=False, stop=True, skip_group_check=True).then_inc(o_done, 1)
                    if st.heads:
                        if s == 0:
                            pe.wait_ge(qcat_loaded[1 - par], 32 * (b - 2 + par) + 64)
                            pe.wait_ge(kcat_loaded[1 - par], 32 * (b - 2 + par) + 64)
                        if not known(b) or NG * (b - 1) + s >= 2:
                            pe.wait_ge(exp_done, NG * (b - 1) + s - 1)
                        pe.matmul(s_ps[s % 2][:, 0:SKP], qcat[:, 1 - par, s, :], kcat[:, 1 - par, s, :], start=True, stop=True).then_inc(s_done, 1)
                    project = keys if s < 4 else values
                    if s < 2 and st.rest:
                        turn_prob(b - 2, par, s + 6)
                    if s == 2 and st.rest:
                        pe.wait_ge(v_copied, b if st.project else B)
                        turn(v_ps, [(NG, prob[:, par, :, SK - 1])]).then_inc(last_turned, 1)
                    if s == 5 and st.rest:
                        pe.wait_ge(o_copied, b - 1)
                        pe.wait_ge(kT_l_ready, b + 1 if st.project else B)
                        turn(k_ps, [(P, o_sb[:, j * P:(j + 1) * P]) for j in range(2)]).then_inc(o_turned, 1)
                    if st.project:
                        if s == 0:
                            pe.wait_ge(cT_l_ready, 4 * b + 4)
                            if not known(b) or b >= 1:
                                pe.wait_ge(kT_l_ready, b)
                            if not known(b) or b >= 3:
                                pe.wait_ge(o_turn_copied, b - 2)
                        if s == 4 and (not known(b) or b >= 1):
                            pe.wait_ge(v_copied, b)
                            if not known(b) or b >= 2:
                                pe.wait_ge(last_copied, b - 1)
                        project(b, par, s, True)
                    if s >= 2 and st.heads:
                        turn_prob(b - 1, 1 - par, s - 2)
                    if s % 2 == 0 and st.next:
                        transpose_context(b + 1, 1 - par, s // 2)
                    if st.project:
                        project(b, par, s, False)
                    if s >= 4 and st.heads:
                        times_values(b - 1, 1 - par, s - 4)
            over_batches(pe, step)


MT = 2 * NT + E - 1
ROWS = (E - 1) * B * SQ + (MT - E + 1) * P
COLS = MT + 1


def mixing(nc, ident, banks, chunk_loaded, x, wo, eta, gate, x3_dram, n_dram, slot_dram, oT, y_pos, wts, tiles):
    with ExitStack() as ctx:
        sb = lambda *a: ctx.enter_context(nc.sbuf_tensor(*a))
        sem = lambda n: ctx.enter_context(nc.semaphore(n))
        raw = sb("wo_raw", [P, KC, D], F32)
        wo_s = [sb("wo_h", [P, KC, D], F32R), sb("wo_l", [P, KC, D], F32R)]
        ot = [sb("ot_h", [P, 2, KC, P], F32R), sb("ot_l", [P, 2, KC, P], F32R)]
        x_in = sb("x_in2", [P, 2, D], F32)
        x2 = sb("x2", [P, 2, D], F32)
        y = sb("y", [P, 2, D], F32)
        yT = sb("yT", [P, D], F32)
        x3 = sb("x3", [P, 2, D], F32)
        n = sb("n", [P, 2, D], F32)
        x3z = n
        nT = sb("nT", [P, D], F32)
        gate_sb = sb("gate_sb", [P, KC, E], F32)
        eta_sb = sb("eta_sb", [P, 1], F32)
        scores = sb("scores", [P, SQ], F32)
        low = sb("low", [P, 1], F32)
        prob = sb("prob2", [P, SQ], F32)
        psum_row = sb("psum_row", [P, 1], F32)
        scale = sb("scale", [P, 2, 1], F32)
        probT = sb("probT", [P, P], F32)
        logits = sb("logits", [P, E], F32)
        top = sb("top", [P, E], F32)
        top_i = sb("top_i", [P, E], U32)
        gap = sb("gap", [P, 1], F32)
        egap = sb("egap", [P, 1], F32)
        chosen_f = sb("chosen_f", [P, 2], F32)
        hot = sb("hot", [P, 2, E], F32)
        both = sb("both", [P, E], F32)
        before = sb("before", [P, E], F32)
        ranked = sb("ranked", [P, E], F32)
        row = sb("row", [P, 2, E], F32)
        slot = sb("slot", [P, 2 * NT], I32)
        earlier = sb("earlier", [P, P], F32)
        ones = sb("ones", [P, P], F32)
        expert_iota = sb("expert_iota", [P, E], F32)
        region = sb("region", [P, E], F32)
        token = sb("token", [P, NT], I32)
        zero_slots = sb("zero_slots", [P, ROWS // P], I32)
        counts = sb("counts", [P, E], F32)
        steps128 = sb("steps128", [P, E, NT], F32)
        over = sb("over", [P, E, NT], F32)
        n_tiles = sb("n_tiles", [P, E], F32)
        n_tiles1 = sb("n_tiles1", [P, E], F32)
        first = sb("first", [P, E], F32)
        zero8 = sb("zero8", [P, E], F32)
        cut = sb("cut", [P, E], F32)
        slot_f = sb("slot_f", [P, 2 * NT], F32)
        behind = sb("behind", [P, 2 * NT, E], F32)
        cuts = sb("cuts", [P, 2 * NT, E], F32)
        cut_of = sb("cut_of", [P, 2 * NT], F32)
        tile_iota = sb("tile_iota", [1, COLS], F32)
        reached = sb("reached", [1, COLS, E], F32)
        start = sb("start", [1, COLS, E], F32)
        e_f = sb("e_f", [1, 2, COLS], F32)
        f_f = sb("f_f", [1, 2, COLS], F32)
        norm2 = Norm(nc, ctx, "norm2")
        norm3 = Norm(nc, ctx, "norm3")
        o_ps, t_ps, r_ps, g_ps, e_ps = banks[0:2], banks[2:4], banks[4:6], banks[6], banks[7]

        x_loaded = [sem("x2_loaded0"), sem("x2_loaded1")]
        small_loaded, slots_zeroed = sem("small_loaded"), sem("slots_zeroed")
        wo_h_ready, wo_ready = sem("wo_h_ready"), sem("wo_ready")
        consts = sem("consts")
        ot_h_ready, ot_l_ready, xo_done, x2_ready, y_ready = sem("ot_h_ready"), sem("ot_l_ready"), sem("xo_done"), sem("x2_ready"), sem("y_ready")
        t_done, t_copied, g_done, blocks, low_ready, prob_ready, probT_ready = (
            sem("t_done"), sem("t_copied"), sem("g_done"), sem("blocks"), sem("low_ready"), sem("prob_ready"), sem("probT_ready"))
        psr_ready, scale_ready, r_done, z_ready, x3_ready, n_ready = (
            sem("psr_ready"), sem("scale_ready"), sem("r_done"), sem("z_ready"), sem("x3_ready"), sem("n_ready"))
        x3_stored = [sem("x3_stored0"), sem("x3_stored1")]
        gate_done, logits_ready, route, gap_ready, egap_ready, both_ready, rank_done, rows_ready = (
            sem("gate_done"), sem("logits_ready"), sem("route"), sem("gap_ready"), sem("egap_ready"), sem("both_ready"),
            sem("rank_done"), sem("rows_ready"))
        scattered, counted, plan, passed = sem("scattered"), sem("counted"), sem("plan"), sem("passed2")
        N_STEPS = NT + 3

        def steps(eng, step):
            pipelined(eng, N_STEPS, step, head=3, tail=4)

        def on(t, lag):
            return not known(t) or 0 <= t - lag < NT

        block = ctx.enter_context(nc.Block())

        def turned_before(t):
            if known(t):
                return sum((0 <= s - 1 < NT) + (0 <= s - 2 < NT) for s in range(t))
            return 2 * t - 3

        @block.sync
        def _(sp):
            def load_x(t, par):
                sp.dma_start(x_in[:, par, :], x[bass.ts(t, P), :]).then_inc(x_loaded[par], 16)
            for c in range(KC):
                sp.dma_start(raw[:, c, :], wo[c * P:(c + 1) * P, :]).then_inc(chunk_loaded[c], 16)
            load_x(0, 0)
            load_x(1, 1)
            sp.dma_start(gate_sb[:, :, :], gate.rearrange("(c p) e -> p c e", p=P)).then_inc(small_loaded, 16)
            sp.dma_start(eta_sb[:, :], eta.rearrange("(a b) -> a b", a=1).to_broadcast([P, 1])).then_inc(small_loaded, 16)
            sp.wait_ge(consts, 10)
            sp.dma_start(slot_dram.rearrange("(p n) o -> p (n o)", p=P), zero_slots[:, :]).then_inc(slots_zeroed, 16)

            def step(t, par):
                if (not known(t) or t >= 1) and (not known(t) or t + 1 < NT) and not (known(t) and t < 1):
                    sp.wait_ge(x2_ready, 2 * t)
                    load_x(t + 1, 1 - par)
                if on(t, 2):
                    sp.wait_ge(n_ready, t - 1)
                    sp.dma_start(n_dram[bass.ds((t - 2) * P, P), :], n[:, par, :]).then_inc(x3_stored[par], 16)
                    sp.dma_start(x3_dram[bass.ds((t - 2) * P, P), :], x3[:, par, :]).then_inc(x3_stored[par], 16)
            steps(sp, step)
            for par in range(2):
                sp.wait_ge(x3_stored[par], 32 * NT // 2)

        @block.gpsimd
        def _(pool):
            pool.memset(probT[:, :], 0.0).then_inc(consts, 1)
            pool.memset(ones[:, :], 1.0).then_inc(consts, 1)
            pool.memset(before[:, :], 0.0).then_inc(consts, 1)
            pool.memset(zero_slots[:, :], 0).then_inc(consts, 1)
            pool.memset(zero8[:, :], 0.0).then_inc(consts, 1)
            pool.iota(expert_iota[:, :], [[1, E]], base=0, channel_multiplier=0, allow_small_or_imprecise_dtypes=True).then_inc(consts, 1)
            pool.iota(region[:, :], [[B * SQ, E]], base=0, channel_multiplier=0, allow_small_or_imprecise_dtypes=True).then_inc(consts, 1)
            pool.iota(token[:, :], [[P, NT]], base=0, channel_multiplier=1).then_inc(consts, 1)
            pool.iota(steps128[:, :, :], [[0, E], [P, NT]], base=0, channel_multiplier=0, allow_small_or_imprecise_dtypes=True).then_inc(consts, 1)
            pool.iota(tile_iota[:, :], [[1, COLS]], base=0, channel_multiplier=0, allow_small_or_imprecise_dtypes=True).then_inc(consts, 1)
            pool.wait_ge(consts, 10)
            pool.affine_select(out=earlier[:, :], in_=ones[:, :], compare_op=ALU.is_gt, fill=0.0, base=0,
                               pattern=[[1, P]], channel_multiplier=-1).then_inc(consts, 1)
            norm2.start_gpsimd(pool)
            norm3.start_gpsimd(pool)
            pool.wait_ge(slots_zeroed, 16)

            def step(t, par):
                if on(t, 1):
                    norm2.on_gpsimd(pool, t - 1)
                if on(t, 2):
                    for h in range(2):
                        pool.wait_ge(z_ready, 2 * (t - 2) + h + 1)
                        if h == 0 and (not known(t) or t >= 4):
                            pool.wait_ge(x3_stored[par], (t - 2 - par) * 16)
                        pool.tensor_tensor(x3[:, par, h * 512:(h + 1) * 512], x2[:, par, h * 512:(h + 1) * 512],
                                           x3z[:, par, h * 512:(h + 1) * 512], ALU.add).then_inc(x3_ready, 1)
                    norm3.on_gpsimd(pool, t - 2)
                if on(t, 3):
                    wait_apart(pool, rows_ready, t - 2, passed)
                    for c in range(2):
                        pool.indirect_dma_start(slot_dram, bass.IndirectOffsetOnAxis(ap=slot_of(t - 3, c), axis=0),
                                                token_of(t - 3), None).then_inc(scattered, 16)
            def slot_of(t, c):
                return slot[:, bass.ds(2 * t + c, 1)]

            def token_of(t):
                return token[:, bass.ds(t, 1)]
            for t in range(N_STEPS):
                step(t, t % 2)
            pool.wait_ge(scattered, 16 * 2 * NT)

        @block.scalar
        def _(act):
            def ot_high(t, par):
                if not known(t) or t >= 2:
                    act.wait_ge(xo_done, 2 * t - 2)
                act.activation(ot[0][:, par, :, :], oT[:, :, bass.ds(t * P, P)], ACT.Copy).then_inc(ot_h_ready, 1)
            ot_high(0, 0)
            for c in range(KC):
                act.wait_ge(chunk_loaded[c], 32)
                act.activation(wo_s[0][:, c, :], raw[:, c, :], ACT.Copy).then_inc(wo_h_ready, 1)

            def copy_turned(dst, number):
                for h in range(2):
                    act.wait_ge(t_done, 2 * number + h + 1)
                    act.activation(dst[:, h * 512:(h + 1) * 512], t_ps[h][:, :], ACT.Copy).then_inc(t_copied, 1)

            def step(t, par):
                if on(t, -1) and on(t, 0):
                    ot_high(t + 1, 1 - par)
                if on(t, 1):
                    if not known(t) or t >= 2:
                        act.wait_ge(g_done, t - 1)
                    copy_turned(yT, turned_before(t))
                if on(t, 2):
                    if not known(t) or t >= 3:
                        act.wait_ge(gate_done, t - 2)
                    copy_turned(nT, turned_before(t) + (1 if on(t, 1) else 0))
                if on(t, 1):
                    act.wait_ge(low_ready, t)
                    act.activation(prob[:, :], scores[:, :], ACT.Exp, bias=low[:, 0:1], scale=-1.0,
                                   accum_out=psum_row[:, :]).then_inc(prob_ready, 1)
                if on(t, 3):
                    act.wait_ge(gap_ready, t - 2)
                    act.activation(egap[:, :], gap[:, :], ACT.Exp).then_inc(egap_ready, 1)
            steps(act, step)

        @block.vector
        def _(dve):
            def ot_low(t, par):
                dve.wait_ge(ot_h_ready, t + 1)
                dve.tensor_tensor(ot[1][:, par, :, :], oT[:, :, bass.ds(t * P, P)], ot[0][:, par, :, :].bitcast(F32), ALU.subtract).then_inc(ot_l_ready, 1)
            ot_low(0, 0)
            for c in range(KC):
                dve.wait_ge(wo_h_ready, c + 1)
                dve.tensor_tensor(wo_s[1][:, c, :], raw[:, c, :], wo_s[0][:, c, :].bitcast(F32), ALU.subtract).then_inc(wo_ready, 1)
            dve.wait_ge(consts, 11)
            dve.wait_ge(small_loaded, 32)

            def step(t, par):
                if on(t, 1):
                    dve.wait_ge(x_loaded[1 - par], (t - 2 + par) * 8 + 16)
                    if not known(t) or t >= 3:
                        dve.wait_ge(x3_ready, 2 * (t - 3) + 2)
                    for h in range(2):
                        dve.wait_ge(xo_done, 2 * (t - 1) + h + 1)
                        dve.tensor_tensor(x2[:, 1 - par, h * 512:(h + 1) * 512], o_ps[h][:, :], x_in[:, 1 - par, h * 512:(h + 1) * 512], ALU.add).then_inc(x2_ready, 1)
                    dve.wait_ge(x2_ready, 2 * t)
                    norm2.on_vector(dve, t - 1, y[:, 1 - par, :], x2[:, 1 - par, :]).then_inc(y_ready, 1)
                if on(t, 3):
                    route_tile(t - 3)
                if on(t, 2):
                    if not known(t) or t >= 4:
                        dve.wait_ge(x3_stored[par], (t - 2 - par) * 16)
                    for h in range(2):
                        dve.wait_ge(r_done, 2 * (t - 2) + h + 1)
                        dve.scalar_tensor_tensor(out=x3z[:, par, h * 512:(h + 1) * 512], in0=r_ps[h][:, :], scalar=scale[:, par, :],
                                                 in1=y[:, par, h * 512:(h + 1) * 512], op0=ALU.mult, op1=ALU.add).then_inc(z_ready, 1)
                    dve.wait_ge(x3_ready, 2 * (t - 2) + 2)
                    norm3.on_vector(dve, t - 2, n[:, par, :], x3[:, par, :]).then_inc(n_ready, 1)
                if on(t, -1) and on(t, 0):
                    ot_low(t + 1, 1 - par)
                if on(t, 1):
                    dve.wait_ge(g_done, t)
                    for b in range(BT):
                        q = slice(b * SQ, (b + 1) * SQ)
                        dve.tensor_copy(scores[q, :], g_ps[q, q]).then_inc(blocks, 1)
                    dve.wait_ge(blocks, 4 * t)
                    dve.tensor_reduce(low[:, :], scores[:, :], AXX, ALU.min).then_inc(low_ready, 1)
                    dve.wait_ge(prob_ready, t)
                    dve.reciprocal(scale[:, 1 - par, :], psum_row[:, :]).then_inc(psr_ready, 1)
                    if not known(t) or t >= 2:
                        dve.wait_ge(r_done, 2 * (t - 1))
                    for b in range(BT):
                        q = slice(b * SQ, (b + 1) * SQ)
                        o = dve.transpose(probT[q, q], prob[q, :])
                    o.then_inc(probT_ready, 1)
                    dve.wait_ge(psr_ready, t)
                    dve.tensor_scalar(scale[:, 1 - par, :], scale[:, 1 - par, :], eta_sb[:, 0:1], None, ALU.mult).then_inc(scale_ready, 1)
                if on(t, 3):
                    rank_tile(t - 3)

            def chain(o, count):
                o.then_inc(route, 1)
                wait_apart(dve, route, count, passed)

            def route_tile(t):
                c = 12 * t
                dve.wait_ge(gate_done, t + 1)
                chain(dve.tensor_copy(logits[:, :], e_ps[:, 0:E]), c + 1)
                chain(dve.max(top[:, :], logits[:, :]), c + 2)
                dve.tensor_tensor(gap[:, :], top[:, 1:2], top[:, 0:1], ALU.subtract).then_inc(gap_ready, 1)
                chain(dve.max_index(top_i[:, :], top[:, :], logits[:, :]), c + 3)
                chain(dve.tensor_copy(chosen_f[:, :], top_i[:, 0:2]), c + 4)
                for k in range(2):
                    chain(dve.tensor_scalar(hot[:, k, :], expert_iota[:, :], chosen_f[:, k:k + 1], None, ALU.is_equal), c + 5 + k)
                dve.tensor_tensor(both[:, :], hot[:, 0, :], hot[:, 1, :], ALU.add).then_inc(both_ready, 1)

            def rank_tile(t):
                c = 12 * t
                dve.wait_ge(egap_ready, t + 1)
                chain(dve.tensor_scalar(chosen_f[:, 0:1], egap[:, :], 1.0, None, ALU.add), c + 7)
                chain(dve.reciprocal(wts[:, bass.ds(2 * t, 1)], chosen_f[:, 0:1]), c + 8)
                dve.tensor_tensor(wts[:, bass.ds(2 * t + 1, 1)], egap[:, :], wts[:, bass.ds(2 * t, 1)], ALU.mult)
                dve.wait_ge(rank_done, t + 1)
                chain(dve.tensor_tensor(ranked[:, :], e_ps[:, 64:64 + E], region[:, :], ALU.add), c + 9)
                dve.tensor_tensor(before[:, :], before[:, :], both[:, :], ALU.add)
                chain(dve.tensor_tensor(row[:, :, :], hot[:, :, :], ranked[:, :].unsqueeze(1).to_broadcast([P, 2, E]), ALU.mult), c + 10)
                chain(dve.tensor_reduce(slot_f[:, bass.ds(2 * t, 2)], row[:, :, :], AXX, ALU.add), c + 11)
                chain(dve.tensor_copy(slot[:, bass.ds(2 * t, 2)], slot_f[:, bass.ds(2 * t, 2)]), c + 12)
                dve.sem_inc(rows_ready, 1)
            steps(dve, step)

            pc = [0]

            def then(o):
                pc[0] += 1
                o.then_inc(plan, 1)
                dve.wait_ge(plan, pc[0])
            dve.wait_ge(counted, 1)
            then(dve.tensor_copy(counts[:, :], e_ps[:, 0:E]))
            then(dve.tensor_tensor(over[:, :, :], counts[:, :].unsqueeze(2).to_broadcast([P, E, NT]), steps128[:, :, :], ALU.is_gt))
            then(dve.tensor_reduce(n_tiles[:, :], over[:, :, :], AXX, ALU.add))
            then(dve.tensor_scalar(n_tiles1[:, :], n_tiles[:, :], 1.0, None, ALU.max))
            then(dve.tensor_tensor_scan(first[:, :], n_tiles1[:, :], zero8[:, :], 0.0, ALU.add, ALU.add))
            then(dve.tensor_tensor(first[:, :], first[:, :], n_tiles1[:, :], ALU.subtract))
            first_b = first[0:1, :].unsqueeze(1).to_broadcast([1, COLS, E])
            then(dve.tensor_tensor(reached[:, :, :], tile_iota[:, :].unsqueeze(2).to_broadcast([1, COLS, E]), first_b, ALU.is_ge))
            then(dve.tensor_tensor(start[:, :, :], reached[:, :, :], first_b, ALU.mult))
            then(dve.tensor_reduce(e_f[:, 0, :], reached[:, :, :], AXX, ALU.add))
            then(dve.tensor_reduce(e_f[:, 1, :], start[:, :, :], AXX, ALU.max))
            then(dve.tensor_scalar(f_f[:, 0, :], e_f[:, 0, :], -1.0, None, ALU.add))
            then(dve.tensor_tensor(f_f[:, 1, :], tile_iota[:, :], e_f[:, 1, :], ALU.subtract))
            then(dve.tensor_copy(tiles[:, 0, :], f_f[:, 0, :]))
            then(dve.tensor_copy(tiles[:, 1, :], f_f[:, 1, :]))
            then(dve.tensor_scalar(e_f[:, 0, :], f_f[:, 1, :], 0.0, None, ALU.is_equal))
            then(dve.tensor_scalar(e_f[:, 1, :], f_f[:, 0, :], float(E - 1), None, ALU.is_lt))
            then(dve.tensor_tensor(f_f[:, 0, :], e_f[:, 0, :], e_f[:, 1, :], ALU.mult))
            then(dve.tensor_copy(tiles[:, 2, :], f_f[:, 0, :]))
            then(dve.scalar_tensor_tensor(out=cut[:, :], in0=first[:, :], scalar=-float(P), in1=region[:, :], op0=ALU.mult, op1=ALU.add))
            then(dve.tensor_tensor(behind[:, :, :], slot_f[:, :].unsqueeze(2).to_broadcast([P, 2 * NT, E]),
                                   region[:, :].unsqueeze(1).to_broadcast([P, 2 * NT, E]), ALU.is_ge))
            then(dve.tensor_tensor(cuts[:, :, :], behind[:, :, :], cut[:, :].unsqueeze(1).to_broadcast([P, 2 * NT, E]), ALU.mult))
            then(dve.tensor_reduce(cut_of[:, :], cuts[:, :, :], AXX, ALU.max))
            then(dve.tensor_tensor(behind[:, :, 0], slot_f[:, :], cut_of[:, :], ALU.subtract))
            then(dve.tensor_copy(y_pos[:, :], behind[:, :, 0]))

        @block.tensor
        def _(pe):
            def product(t, par, unit):
                h = unit // 4
                if unit == 0:
                    pe.wait_ge(ot_l_ready, t + 1)
                if unit % 4 == 0 and (not known(t) or t >= 1):
                    pe.wait_ge(x2_ready, 2 * (t - 1) + h + 1)
                for k in range(unit % 4 * 2, unit % 4 * 2 + 2):
                    if known(t) and t == 0 and h == 0:
                        pe.wait_ge(wo_ready, k + 1)
                    for m, (a, b) in enumerate(PASSES):
                        o = pe.matmul(o_ps[h][:, :], ot[a][:, par, k, :], wo_s[b][:, k, h * 512:(h + 1) * 512],
                                      start=(k == 0 and m == 0), stop=(k == KC - 1 and m == 2))
                if unit % 4 == 3:
                    o.then_inc(xo_done, 1)

            def turn(src, number):
                for k in range(KC):
                    if k % 4 == 0 and (not known(number) or number >= 1):
                        pe.wait_ge(t_copied, 2 * (number - 1) + k // 4 + 1)
                    o = pe.transpose(t_ps[k // 4][:, k % 4 * P:(k % 4 + 1) * P], src[:, k * P:(k + 1) * P], ident[:, :])
                    if k % 4 == 3:
                        o.then_inc(t_done, 1)

            pe.wait_ge(consts, 11)
            pe.wait_ge(small_loaded, 32)

            def step(t, par):
                for unit in range(KC):
                    if unit == 5 and on(t, 3):
                        pe.wait_ge(both_ready, t - 2)
                        pe.matmul(e_ps[:, 64:64 + E], earlier[:, :], both[:, :], start=True, stop=False)
                        pe.matmul(e_ps[:, 64:64 + E], ones[:, :], before[:, :], start=False, stop=True).then_inc(rank_done, 1)
                    if unit == 2 and on(t, 2):
                        pe.wait_ge(probT_ready, t - 1)
                        for h in range(2):
                            if not known(t) or t >= 3:
                                pe.wait_ge(z_ready, 2 * (t - 3) + h + 1)
                            pe.matmul(r_ps[h][:, :], probT[:, :], y[:, par, h * 512:(h + 1) * 512], start=True, stop=True).then_inc(r_done, 1)
                    if unit == 4 and on(t, 1):
                        pe.wait_ge(y_ready, t)
                        turn(y[:, 1 - par, :], turned_before(t))
                    if unit == 6 and on(t, 2):
                        pe.wait_ge(n_ready, t - 1)
                        turn(n[:, par, :], turned_before(t) + (1 if on(t, 1) else 0))
                    if unit == 6 and on(t, 1):
                        pe.wait_ge(t_copied, 2 * turned_before(t) + 2)
                        if not known(t) or t >= 2:
                            pe.wait_ge(blocks, 4 * (t - 1))
                        for k in range(KC):
                            o = pe.matmul(g_ps[:, 0:P], yT[:, k * P:(k + 1) * P], yT[:, k * P:(k + 1) * P], start=(k == 0), stop=(k == KC - 1))
                        o.then_inc(g_done, 1)
                    if on(t, 0):
                        product(t, par, unit)
                if on(t, 2):
                    pe.wait_ge(t_copied, 2 * (turned_before(t) + (1 if on(t, 1) else 0)) + 2)
                    if not known(t) or t >= 3:
                        pe.wait_ge(rows_ready, t - 2)
                    for k in range(KC):
                        o = pe.matmul(e_ps[:, 0:E], nT[:, k * P:(k + 1) * P], gate_sb[:, k, :], start=(k == 0), stop=(k == KC - 1))
                    o.then_inc(gate_done, 1)
            steps(pe, step)
            pe.wait_ge(rows_ready, NT)
            pe.matmul(e_ps[:, 0:E], ones[:, :], before[:, :], start=True, stop=True).then_inc(counted, 1)


def experts(nc, ident, banks, chunk_loaded, expert_w, n_dram, slot_dram, y_dram, tiles):
    with ExitStack() as ctx:
        sb = lambda *a: ctx.enter_context(nc.sbuf_tensor(*a))
        sem = lambda n: ctx.enter_context(nc.semaphore(n))
        w = [sb("w_h", [P, 2 * KC * D], F32R), sb("w_l", [P, 2 * KC * D], F32R)]
        raw = sb("w_raw", [P, KC, D], F32)
        idx = sb("idx", [P, 2], I32)
        xg = sb("xg", [P, 2, D], F32)
        gT = [sb("gT_h", [P, 2, D], F32R), sb("gT_l", [P, 2, D], F32R)]
        y_sb = sb("y_sb", [P, 2, D], F32)
        t_ps, y_ps = banks[0:2], [banks[2:4], banks[4:6]]

        w_h_ready, w_l_ready = sem("w_h_ready"), sem("w_l_ready")
        idx_loaded = [sem("idx_loaded0"), sem("idx_loaded1")]
        xg_loaded = [sem("xg_loaded0"), sem("xg_loaded1")]
        gT_done, gT_h_ready, gT_l_ready = sem("gT_done"), sem("gT_h_ready"), sem("gT_l_ready")
        y_done, y0_copied, y1_copied = sem("y_done"), sem("y0_copied"), sem("y1_copied")
        y_stored = [sem("y_stored0"), sem("y_stored1")]
        passed = sem("passed3")

        def more(i, by=1):
            return not known(i) or i + by < MT

        def entry(eng, i, what, most):
            return eng.value_load(tiles[0:1, what, bass.ds(i, 1)], min_val=0, max_val=most)

        def steps(eng, step):
            pipelined(eng, MT, step, head=3, tail=2)

        block = ctx.enter_context(nc.Block())

        @block.sync
        def _(sp):
            for c in range(KC):
                sp.dma_start(raw[:, c, :], expert_w[0, c * P:(c + 1) * P, :]).then_inc(chunk_loaded[c], 16)
            with sp.Fori(1, E) as e:
                for c in range(KC):
                    sp.wait_ge(w_l_ready, KC * e - KC + c + 1)
                    sp.dma_start(raw[:, c, :], expert_w[bass.ds(e, 1), c * P:(c + 1) * P, :].rearrange("o p n -> p (o n)")).then_inc(chunk_loaded[c], 16)

        @block.gpsimd
        def _(pool):
            def first_row(i):
                e = entry(pool, i, 0, E - 1)
                j = entry(pool, i, 1, MT - E)
                return pool.snap(e * (B * SQ) + j * P, min_val=0, max_val=ROWS - P)

            def load_idx(i, par):
                pool.dma_start(idx[:, par:par + 1], slot_dram[bass.ds(first_row(i), P), :]).then_inc(idx_loaded[par], 16)

            def gather(i, par):
                if not known(i) or i >= 2:
                    pool.wait_ge(gT_done, 2 * i - 2)
                wait_apart(pool, idx_loaded[par], 8 * (i - par) + 16, passed)
                pool.indirect_dma_start(xg[:, par, :], None, n_dram, bass.IndirectOffsetOnAxis(ap=idx[:, par:par + 1], axis=0)).then_inc(xg_loaded[par], 16)

            def store(i, par):
                pool.wait_ge(y0_copied, i + 1)
                pool.wait_ge(y1_copied, i + 1)
                pool.dma_start(y_dram[bass.ds(i * P, P), :], y_sb[:, par, :]).then_inc(y_stored[par], 16)

            load_idx(0, 0)
            load_idx(1, 1)
            gather(0, 0)

            def step(i, par):
                if more(i):
                    gather(i + 1, 1 - par)
                if more(i, 2):
                    pool.wait_ge(xg_loaded[par], 8 * (i - par) + 16)
                    load_idx(i + 2, par)
                if not known(i) or i >= 1:
                    store(i - 1, 1 - par)
            steps(pool, step)
            store(MT - 1, (MT - 1) % 2)
            pool.wait_ge(y_stored[0], 16 * ((MT + 1) // 2))
            pool.wait_ge(y_stored[1], 16 * (MT // 2))

        @block.scalar
        def _(act):
            def rows_high(i, par):
                if not known(i) or i >= 2:
                    act.wait_ge(y_done, 2 * i - 2)
                for h in range(2):
                    act.wait_ge(gT_done, 2 * i + h + 1)
                    act.activation(gT[0][:, par, h * 512:(h + 1) * 512], t_ps[h][:, :], ACT.Copy).then_inc(gT_h_ready, 1)

            def split_high(e, slot):
                for c in range(KC):
                    act.wait_ge(chunk_loaded[c], 16 * e + 48)
                    act.activation(w[0][:, bass.ds(slot + c * D, D)], raw[:, c, :], ACT.Copy).then_inc(w_h_ready, 1)
            split_high(0, 0)
            rows_high(0, 0)

            def step(i, par):
                if more(i):
                    rows_high(i + 1, 1 - par)
                flag = entry(act, i, 2, 1)
                e = entry(act, i, 0, E - 1)
                with act.If(flag > 0):
                    if not known(i) or i >= 1:
                        act.wait_ge(y_done, 2 * i)
                    split_high(e + 1, (e + 1) % 2 * (KC * D))
                if not known(i) or i >= 2:
                    act.wait_ge(y_stored[par], 8 * (i - par))
                act.wait_ge(y_done, 2 * i + 1)
                act.activation(y_sb[:, par, 0:512], y_ps[par][0][:, :], ACT.Copy).then_inc(y0_copied, 1)
            steps(act, step)

        @block.vector
        def _(dve):
            def rows_low(i, par):
                for h in range(2):
                    dve.wait_ge(gT_h_ready, 2 * i + h + 1)
                    dve.tensor_tensor(gT[1][:, par, h * 512:(h + 1) * 512], t_ps[h][:, :],
                                      gT[0][:, par, h * 512:(h + 1) * 512].bitcast(F32), ALU.subtract).then_inc(gT_l_ready, 1)

            def split_low(e, slot):
                for c in range(KC):
                    dve.wait_ge(w_h_ready, KC * e + c + 1)
                    dve.tensor_tensor(w[1][:, bass.ds(slot + c * D, D)], raw[:, c, :],
                                      w[0][:, bass.ds(slot + c * D, D)].bitcast(F32), ALU.subtract).then_inc(w_l_ready, 1)
            split_low(0, 0)
            rows_low(0, 0)

            def step(i, par):
                if more(i):
                    rows_low(i + 1, 1 - par)
                flag = entry(dve, i, 2, 1)
                e = entry(dve, i, 0, E - 1)
                with dve.If(flag > 0):
                    split_low(e + 1, (e + 1) % 2 * (KC * D))
                if not known(i) or i >= 2:
                    dve.wait_ge(y_stored[par], 8 * (i - par))
                dve.wait_ge(y_done, 2 * i + 2)
                dve.tensor_copy(y_sb[:, par, 512:D], y_ps[par][1][:, :]).then_inc(y1_copied, 1)
            steps(dve, step)

        @block.tensor
        def _(pe):
            def turn(i, par):
                pe.wait_ge(xg_loaded[par], 8 * (i - par) + 16)
                for k in range(KC):
                    if k % 4 == 0 and (not known(i) or i >= 1):
                        pe.wait_ge(gT_l_ready, 2 * i - 1 + k // 4)
                    o = pe.transpose(t_ps[k // 4][:, k % 4 * P:(k % 4 + 1) * P], xg[:, par, k * P:(k + 1) * P], ident[:, :])
                    if k % 4 == 3:
                        o.then_inc(gT_done, 1)
            turn(0, 0)

            def step(i, par):
                e = entry(pe, i, 0, E - 1)
                slot = pe.snap(e % 2 * (KC * D), min_val=0, max_val=KC * D)
                pe.wait_ge(w_l_ready, KC * e + KC)
                pe.wait_ge(gT_l_ready, 2 * i + 2)
                if not known(i) or i >= 2:
                    pe.wait_ge(y0_copied, i - 1)
                    pe.wait_ge(y1_copied, i - 1)
                for unit in range(KC):
                    h = unit // 4
                    if unit == 4 and more(i):
                        turn(i + 1, 1 - par)
                    for k in range(unit % 4 * 2, unit % 4 * 2 + 2):
                        for n, (a, b) in enumerate(PASSES):
                            o = pe.matmul(y_ps[par][h][:, :], gT[a][:, par, k * P:(k + 1) * P],
                                          w[b][:, bass.ds(slot + (k * D + h * 512), 512)],
                                          start=(k == 0 and n == 0), stop=(k == KC - 1 and n == 2))
                    if unit % 4 == 3:
                        o.then_inc(y_done, 1)
            steps(pe, step)


def combine(nc, x3_dram, y_dram, out, y_pos, wts):
    with ExitStack() as ctx:
        sb = lambda *a: ctx.enter_context(nc.sbuf_tensor(*a))
        sem = lambda n: ctx.enter_context(nc.semaphore(n))
        x3 = sb("x3_in", [P, NT, D], F32)
        yy = sb("yy", [P, 2 * NT, D], F32)
        x3_loaded = sem("x3_loaded")
        y_loaded = [sem(f"y_loaded{t}") for t in range(NT)]
        half_added, added, stored = sem("half_added"), sem("added"), sem("stored")
        block = ctx.enter_context(nc.Block())

        @block.sync
        def _(sp):
            sp.dma_start(x3[:, :, :], x3_dram.rearrange("(t p) n -> p t n", p=P)).then_inc(x3_loaded, 16)

        @block.gpsimd
        def _(pool):
            for t in range(NT):
                for k in range(2):
                    pool.indirect_dma_start(yy[:, 2 * t + k, :], None, y_dram, bass.IndirectOffsetOnAxis(
                        ap=y_pos[:, 2 * t + k:2 * t + k + 1], axis=0)).then_inc(y_loaded[t], 16)

        @block.vector
        def _(dve):
            dve.wait_ge(x3_loaded, 16)
            for t in range(NT):
                dve.wait_ge(y_loaded[t], 32)
                for k in range(2):
                    if k == 1:
                        dve.wait_ge(half_added, t + 1)
                    dve.scalar_tensor_tensor(out=x3[:, t, :], in0=yy[:, 2 * t + k, :], scalar=wts[:, 2 * t + k:2 * t + k + 1],
                                             in1=x3[:, t, :], op0=ALU.mult, op1=ALU.add).then_inc((half_added, added)[k], 1)

        @block.scalar
        def _(act):
            for t in range(NT):
                act.wait_ge(added, t + 1)
                act.dma_start(out[t * P:(t + 1) * P, :], x3[:, t, :]).then_inc(stored, 16)
            act.wait_ge(stored, 16 * NT)


def program(nc, x, context, wq, wk, wv, wo, eta, gate, expert_w, out):
    scratch = lambda name, shape, dt: nc.dram_tensor(name, shape, dt, kind="Internal").ap()
    q_dram = scratch("q_scratch", [2, NT, P, D], F32)
    k_dram = scratch("k_scratch", [2, 2, P, 2 * SKP], F32)
    vlast_dram = scratch("vlast_scratch", [B, NG, KV], F32)
    x3_dram = scratch("x3_scratch", [B * SQ, D], F32)
    n_dram = scratch("n_scratch", [B * SQ, D], F32)
    slot_dram = scratch("slot_scratch", [ROWS, 1], I32)
    y_dram = scratch("y_scratch", [MT * P, D], F32)
    with ExitStack() as ctx:
        sb = lambda *a: ctx.enter_context(nc.sbuf_tensor(*a))
        ident = sb("ident", [P, P], F32)
        y_pos = sb("y_pos", [P, 2 * NT], I32)
        wts = sb("wts", [P, 2 * NT], F32)
        tiles = sb("tiles", [1, 3, COLS], I32)
        chunk_loaded = [ctx.enter_context(nc.semaphore(f"chunk_loaded{c}")) for c in range(KC)]
        banks = [ctx.enter_context(nc.psum_tensor(f"bank{i}", [P, 512], F32)) for i in range(8)]
        with ExitStack() as attention:
            oT = attention.enter_context(nc.sbuf_tensor("oT", [P, KC, B * SQ], F32))
            with nc.sbuf_tensor("wkv_h", [P, KC, 2 * KV], F32R) as wkv_h, nc.sbuf_tensor("wkv_l", [P, KC, 2 * KV], F32R) as wkv_l:
                queries(nc, ident, banks, chunk_loaded, x, wq, wk, wv, q_dram, oT, [wkv_h, wkv_l])
                cross_attention(nc, ident, banks, context, q_dram, k_dram, vlast_dram, [wkv_h, wkv_l], oT)
            mixing(nc, ident, banks, chunk_loaded, x, wo, eta, gate, x3_dram, n_dram, slot_dram, oT, y_pos, wts, tiles)
        experts(nc, ident, banks, chunk_loaded, expert_w, n_dram, slot_dram, y_dram, tiles)
        combine(nc, x3_dram, y_dram, out, y_pos, wts)


def kernel(**inputs):
    import numpy as np
    import concourse.bacc as bacc
    from concourse.bass_utils import run_bass_kernel_spmd as run

    wq = inputs["L0_xattn_Wq"]
    wo = inputs["L0_xattn_Wo"]
    arrays = {
        "x": np.asarray(inputs["x"]).reshape(B * SQ, D),
        "context": np.asarray(inputs["ctx_4096"]),
        "wq": np.ascontiguousarray(np.asarray(wq).reshape(D, 2, 4, REP, DH).transpose(0, 1, 3, 2, 4).reshape(D, D)),
        "wk": np.asarray(inputs["L0_xattn_Wk"]),
        "wv": np.asarray(inputs["L0_xattn_Wv"]),
        "wo": np.ascontiguousarray(np.asarray(wo).reshape(2, 4, REP, DH, D).transpose(0, 2, 1, 3, 4).reshape(D, D)),
        "eta": np.asarray(inputs["L0_attn_eta"]),
        "gate": np.asarray(inputs["L0_ffn_gate_w"]),
        "expert_w": np.asarray(inputs["L0_ffn_expert_w"]),
    }
    nc = bacc.Bacc("TRN2", target_bir_lowering=False, num_devices=1)
    args = [nc.dram_tensor(f"in_{k}", a.shape, mybir.dt.from_np(a.dtype), kind="ExternalInput").ap() for k, a in arrays.items()]
    out = nc.dram_tensor("out_x", (B * SQ, D), F32, kind="ExternalOutput").ap()
    program(nc, *args, out)
    r = run(nc, [{f"in_{k}": a for k, a in arrays.items()}], core_ids=[0])
    return r.results[0]["out_x"].reshape(B, SQ, D)
```

```python
from contextlib import ExitStack

import concourse.bass as bass
from concourse import mybir

ALU = mybir.AluOpType
ACT = mybir.ActivationFunctionType
AXX = mybir.AxisListType.X
F32 = mybir.dt.float32
F32R = mybir.dt.float32r
U32 = mybir.dt.uint32
I32 = mybir.dt.int32

P = 128
B = 32
SQ = 32
SK = 257
D = 1024
KC = D // P
NH, NG, DH = 32, 8, 32
REP = NH // NG
KV = NG * DH
NT = B * SQ // P
BT = P // SQ
SCALE = DH ** -0.5
EPS = 1e-5
E = 8
SKP = SK + 1
PASSES = ((0, 0), (0, 1), (1, 0))


SLOT = KC * D
SLOT_BYTES = 4 * SLOT
HIGH0, HIGH1, LOW0, LOW1, STAGE = (i * SLOT_BYTES for i in range(5))


class Shared:

    def __init__(self, nc, ctx):
        sb = lambda *a: ctx.enter_context(nc.sbuf_tensor(*a))
        sem = lambda n: ctx.enter_context(nc.semaphore(n))
        self.ident = sb("ident", [P, P], F32)
        base = nc.sbuf_base
        sb("shared_map", [P, 4 * SLOT + 4 * D], F32)
        self.at = lambda name, offset, shape, dtype=F32: nc.alloc_sbuf_tensor_at(name, shape, dtype, offset=base + offset)
        self.wkv = [self.at("wkv_" + part, HIGH1 + i * SLOT_BYTES // 2, [P, KC, 2 * KV], F32R) for i, part in enumerate("hl")]
        self.cx = self.at("cx", STAGE, [P, 2, 2, D])
        self.oT = self.at("oT", HIGH0, [P, KC, B * SQ])
        self.wo = [self.at("wo_h", HIGH1, [P, KC, D], F32R), self.at("wo_l", LOW1, [P, KC, D], F32R)]
        self.w = [self.at("w_h", HIGH0, [P, 2 * SLOT], F32R), self.at("w_l", LOW0, [P, 2 * SLOT], F32R)]
        self.y_pos = sb("y_pos", [P, 2 * NT], I32)
        self.wts = sb("wts", [P, 2 * NT], F32)
        self.tiles = sb("tiles", [1, 5, COLS], I32)
        self.banks = [ctx.enter_context(nc.psum_tensor(f"bank{i}", [P, 512], F32)) for i in range(8)]
        self.chunk_loaded = [sem(f"chunk_loaded{c}") for c in range(KC)]
        self.cl_loaded, self.cx_loaded = sem("cl_loaded"), [sem("cx_loaded0"), sem("cx_loaded1")]
        self.w_h_ready, self.w_l_ready = sem("w_h_ready"), sem("w_l_ready")
        self.x3_loaded = sem("x3_loaded")
        self.idx = sb("idx", [P, 2], I32)
        self.xg = self.at("xg", STAGE, [P, 2, D])
        self.idx_loaded, self.xg_loaded = sem("idx_loaded"), sem("xg_loaded")


def pipelined(eng, n, step, head=1, tail=1):
    assert head % 2 == 1
    pairs = (n - head - tail) // 2
    for t in range(head):
        step(t, t % 2)
    with eng.Fori(0, pairs) as i:
        step(2 * i + head, head % 2)
        step(2 * i + head + 1, (head + 1) % 2)
    for t in range(head + 2 * pairs, n):
        step(t, t % 2)


def wait_apart(eng, sem, value, passed):
    eng.wait_ge(sem, value)
    if not known(value):
        eng.sem_inc(passed, 1)


def known(t):
    return isinstance(t, int)


class Norm:

    def __init__(self, nc, ctx, name):
        self.stats = ctx.enter_context(nc.sbuf_tensor(name + "_stats", [P, 2, 6], F32))
        self.mean_var = ctx.enter_context(nc.sbuf_tensor(name + "_mean_var", [P, 2], F32))
        self.rstd = ctx.enter_context(nc.sbuf_tensor(name + "_rstd", [P, 1], F32))
        self.var_eps = ctx.enter_context(nc.sbuf_tensor(name + "_var_eps", [P, 1], F32))
        self.minus_half = ctx.enter_context(nc.sbuf_tensor(name + "_minus_half", [P, 1], F32))
        self.eps_added = ctx.enter_context(nc.semaphore(name + "_eps_added"))
        self.passed = ctx.enter_context(nc.semaphore(name + "_passed"))
        self.stats_ready = ctx.enter_context(nc.semaphore(name + "_stats_ready"))
        self.var_ready = ctx.enter_context(nc.semaphore(name + "_var_ready"))
        self.rstd_ready = ctx.enter_context(nc.semaphore(name + "_rstd_ready"))

    def on_vector(self, dve, t, out, src):
        for h in range(2):
            dve.bn_stats(self.stats[:, h, :], src[:, h * 512:(h + 1) * 512]).then_inc(self.stats_ready, 1)
        wait_apart(dve, self.stats_ready, 2 * t + 2, self.passed)
        dve.bn_aggr(self.mean_var[:, :], self.stats[:, :, :].rearrange("p a b -> p (a b)")).then_inc(self.var_ready, 1)
        dve.wait_ge(self.rstd_ready, t + 1)
        return dve.tensor_scalar(out, src, self.mean_var[:, 0:1], self.rstd[:, 0:1], ALU.subtract, ALU.mult)

    def start_gpsimd(self, pool):
        pool.memset(self.minus_half[:, :], -0.5).then_inc(self.eps_added, 1)
        pool.wait_ge(self.eps_added, 1)

    def on_gpsimd(self, pool, t):
        wait_apart(pool, self.var_ready, t + 1, self.passed)
        pool.tensor_scalar(self.var_eps[:, :], self.mean_var[:, 1:2], EPS, None, ALU.add).then_inc(self.eps_added, 1)
        pool.wait_ge(self.eps_added, t + 2)
        pool.tensor_tensor(self.rstd[:, :], self.var_eps[:, :], self.minus_half[:, :], ALU.pow).then_inc(self.rstd_ready, 1)


def queries(nc, sh, x, wq, wk, wv, context, q_dram, cl):
    with ExitStack() as ctx:
        sb = lambda *a: ctx.enter_context(nc.sbuf_tensor(*a))
        sem = lambda n: ctx.enter_context(nc.semaphore(n))
        ident, banks, wkv, cx, chunk_loaded, cx_loaded = sh.ident, sh.banks, sh.wkv, sh.cx, sh.chunk_loaded, sh.cx_loaded
        wkv_raw = sh.at("wkv_raw", STAGE, [P, KC, 2 * KV])
        wq_raw = sh.at("wq_raw", HIGH0, [P, KC, D])
        wq_s = [sh.at("wq_h", LOW0, [P, KC, D], F32R), sh.at("wq_l", LOW1, [P, KC, D], F32R)]
        x_in = sb("x_in", [P, 2, D], F32)
        xn = sb("xn", [P, 2, D], F32)
        xT = [sb("xT_h", [P, 2, D], F32R), sb("xT_l", [P, 2, D], F32R)]
        q_sb = sb("q_sb", [P, 2, D], F32)
        qT = [sb("qT_h", [P, 2, D], F32R), sb("qT_l", [P, 2, D], F32R)]
        norm = Norm(nc, ctx, "norm1")
        xT_ps = banks[0:2]
        q_ps = [banks[2:4], banks[4:6]]
        qT_ps = banks[6:8]

        x_loaded = [sem("x_loaded0"), sem("x_loaded1")]
        wkv_loaded = [sem("wk_loaded"), sem("wv_loaded")]
        ident_zero, ident_ready = sem("ident_zero"), sem("ident_ready")
        wq_h_ready, wq_ready = sem("wq_h_ready"), sem("wq_ready")
        wkv_h_ready, wkv_l_ready = sem("wkv_h_ready"), sem("wkv_l_ready")
        xn_ready, xT_done, xT_h_ready, xT_l_ready = sem("xn_ready"), sem("xT_done"), sem("xT_h_ready"), sem("xT_l_ready")
        q_done, q_copied, qT_done, qT_h_ready, qT_l_ready = (
            sem("q_done"), sem("q_copied"), sem("qT_done"), sem("qT_h_ready"), sem("qT_l_ready"))
        q_stored = [sem("q_stored0"), sem("q_stored1")]

        by_batch = lambda ap: ap.rearrange("p (b m q) -> p m b q", b=BT, q=SQ)

        block = ctx.enter_context(nc.Block())

        @block.sync
        def _(sp):
            def load_x(t, par):
                sp.dma_start(x_in[:, par, :], x[bass.ts(t, P), :]).then_inc(x_loaded[par], 16)
            load_x(0, 0)
            for c in range(KC):
                sp.dma_start(wq_raw[:, c, :], wq[c * P:(c + 1) * P, :]).then_inc(chunk_loaded[c], 16)
                if c == 0:
                    load_x(1, 1)
            for n, w in enumerate((wk, wv)):
                sp.dma_start(wkv_raw[:, :, n * KV:(n + 1) * KV], w.rearrange("(c p) n -> p c n", p=P)).then_inc(wkv_loaded[n], 16)

            def step(t, par):
                if not known(t) or t + 2 < NT:
                    sp.wait_ge(xn_ready, t + 1)
                    load_x(t + 2, par)
            pipelined(sp, NT, step, tail=3)
            sp.dma_start(cl[:, :], context[:, 2 * P, :]).then_inc(sh.cl_loaded, 16)
            sp.wait_ge(wkv_l_ready, KC)
            for b in range(2):
                sp.dma_start(context_tile(cx, b), context_rows(context, b)).then_inc(cx_loaded[b], 16)
            for par in range(2):
                sp.wait_ge(q_stored[par], 32 * NT // 2)

        @block.gpsimd
        def _(pool):
            pool.memset(ident[:, :], 0.0).then_inc(ident_zero, 1)
            pool.wait_ge(ident_zero, 1)
            pool.affine_select(out=ident[:, :], in_=ident[:, :], compare_op=ALU.not_equal, fill=1.0, base=0,
                               pattern=[[-1, P]], channel_multiplier=1).then_inc(ident_ready, 1)
            norm.start_gpsimd(pool)
            pipelined(pool, NT, lambda t, par: norm.on_gpsimd(pool, t))

        @block.scalar
        def _(act):
            def xT_high(t, par):
                if not known(t) or t >= 2:
                    act.wait_ge(q_done, 2 * t - 2)
                for h in range(2):
                    act.wait_ge(xT_done, 2 * t + h + 1)
                    act.activation(xT[0][:, par, h * 512:(h + 1) * 512], xT_ps[h][:, :], ACT.Copy).then_inc(xT_h_ready, 1)
            xT_high(0, 0)
            for c in range(KC):
                act.wait_ge(chunk_loaded[c], 16)
                act.activation(wq_s[0][:, c, :], wq_raw[:, c, :], ACT.Copy).then_inc(wq_h_ready, 1)

            def step(t, par):
                if not known(t) or t + 1 < NT:
                    xT_high(t + 1, 1 - par)
                if known(t) and t == 0:
                    for n in range(2):
                        act.wait_ge(wkv_loaded[n], 16)
                    for c in range(KC):
                        act.activation(wkv[0][:, c, :], wkv_raw[:, c, :], ACT.Copy).then_inc(wkv_h_ready, 1)
                for h in range(2):
                    act.wait_ge(q_done, 2 * t + h + 1)
                    if h == 0 and (not known(t) or t >= 2):
                        act.wait_ge(qT_done, 2 * t - 2)
                    act.activation(q_sb[:, par, h * 512:(h + 1) * 512], q_ps[par][h][:, :], ACT.Copy).then_inc(q_copied, 1)
                if not known(t) or t >= 1:
                    qT_high(t - 1, 1 - par)
                if not known(t) or t >= 2:
                    store_q(t - 2, par)

            def store_q(t, par):
                act.wait_ge(qT_l_ready, t + 1)
                for part in range(2):
                    act.dma_start(q_dram[part, bass.ds(t, 1)].rearrange("a p n -> p (a n)"),
                                  qT[part][:, par, :].bitcast(F32)).then_inc(q_stored[par], 16)

            def qT_high(t, par):
                if not known(t) or t >= 2:
                    act.wait_ge(q_stored[par], (t - par) * 16)
                for h in range(2):
                    act.wait_ge(qT_done, 2 * t + h + 1)
                    o = act.activation(by_batch(qT[0][:, par, :])[:, 4 * h:4 * h + 4],
                                       qT_ps[h][:, :].rearrange("p (m b q) -> p m b q", m=4, q=SQ), ACT.Copy, scale=SCALE)
                    if h == 1:
                        o.then_inc(qT_h_ready, 1)
            pipelined(act, NT, step, head=3)
            store_q(6, 0)
            qT_high(7, 1)
            store_q(7, 1)

        @block.vector
        def _(dve):
            def normalize(t, par):
                dve.wait_ge(x_loaded[par], (t - par) * 8 + 16)
                if not known(t) or t >= 2:
                    dve.wait_ge(xT_done, 2 * t - 2)
                norm.on_vector(dve, t, xn[:, par, :], x_in[:, par, :]).then_inc(xn_ready, 1)

            def xT_low(t, par):
                for h in range(2):
                    dve.wait_ge(xT_h_ready, 2 * t + h + 1)
                    dve.tensor_tensor(xT[1][:, par, h * 512:(h + 1) * 512], xT_ps[h][:, :],
                                      xT[0][:, par, h * 512:(h + 1) * 512].bitcast(F32), ALU.subtract).then_inc(xT_l_ready, 1)

            def qT_low(t, par):
                if not known(t) or t >= 2:
                    dve.wait_ge(q_stored[par], (t - par) * 16)
                dve.wait_ge(qT_h_ready, t + 1)
                for h in range(2):
                    for m in range(4):
                        o = dve.scalar_tensor_tensor(out=by_batch(qT[1][:, par, :])[:, 4 * h + m],
                                                     in0=qT_ps[h][:, m * P:(m + 1) * P].rearrange("p (b q) -> p b q", q=SQ),
                                                     scalar=SCALE, in1=by_batch(qT[0][:, par, :])[:, 4 * h + m].bitcast(F32),
                                                     op0=ALU.mult, op1=ALU.subtract)
                o.then_inc(qT_l_ready, 1)

            normalize(0, 0)
            normalize(1, 1)
            xT_low(0, 0)
            for c in range(KC):
                dve.wait_ge(wq_h_ready, c + 1)
                dve.tensor_tensor(wq_s[1][:, c, :], wq_raw[:, c, :], wq_s[0][:, c, :].bitcast(F32), ALU.subtract).then_inc(wq_ready, 1)

            def step(t, par):
                if not known(t) or t + 1 < NT:
                    if not known(t) or t >= 1:
                        normalize(t + 1, 1 - par)
                    xT_low(t + 1, 1 - par)
                if known(t) and t == 0:
                    dve.wait_ge(wkv_h_ready, KC)
                    for c in range(KC):
                        dve.tensor_tensor(wkv[1][:, c, :], wkv_raw[:, c, :], wkv[0][:, c, :].bitcast(F32),
                                          ALU.subtract).then_inc(wkv_l_ready, 1)
                if not known(t) or t >= 1:
                    qT_low(t - 1, 1 - par)
            pipelined(dve, NT, step, head=3)
            qT_low(7, 1)

        @block.tensor
        def _(pe):
            def transpose_x(t, par):
                pe.wait_ge(xn_ready, t + 1)
                for k in range(KC):
                    if k % 4 == 0 and (not known(t) or t >= 1):
                        pe.wait_ge(xT_l_ready, 2 * t - 1 + k // 4)
                    o = pe.transpose(xT_ps[k // 4][:, k % 4 * P:(k % 4 + 1) * P], xn[:, par, k * P:(k + 1) * P], ident[:, :])
                    if k % 4 == 3:
                        o.then_inc(xT_done, 1)

            def transpose_q(t, par):
                pe.wait_ge(q_copied, 2 * t + 2)
                if not known(t) or t >= 1:
                    pe.wait_ge(qT_l_ready, t)
                for k in range(KC):
                    o = pe.transpose(qT_ps[k // 4][:, k % 4 * P:(k % 4 + 1) * P], q_sb[:, par, k * P:(k + 1) * P], ident[:, :])
                    if k % 4 == 3:
                        o.then_inc(qT_done, 1)

            pe.wait_ge(ident_ready, 1)
            transpose_x(0, 0)

            def step(t, par):
                pe.wait_ge(xT_l_ready, 2 * t + 2)
                if not known(t) or t >= 2:
                    pe.wait_ge(q_copied, 2 * t - 2)
                for k in range(KC):
                    if known(t) and t == 0:
                        pe.wait_ge(wq_ready, k + 1)
                    if k == 4 and (not known(t) or t + 1 < NT):
                        transpose_x(t + 1, 1 - par)
                    if k == 6 and (not known(t) or t >= 1):
                        transpose_q(t - 1, 1 - par)
                    for h in range(2):
                        for n, (a, b) in enumerate(PASSES):
                            o = pe.matmul(q_ps[par][h][:, :], xT[a][:, par, k * P:(k + 1) * P],
                                          wq_s[b][:, k, h * 512:(h + 1) * 512],
                                          start=(k == 0 and n == 0), stop=(k == KC - 1 and n == 2))
                        if k == KC - 1:
                            o.then_inc(q_done, 1)
            pipelined(pe, NT, step, head=3)
            transpose_q(7, 1)


def context_tile(cx, par):
    return cx[:, par, :, :].rearrange("p a n -> p (a n)")


def context_rows(context, b):
    return context[bass.ds(b, 1), 0:2 * P, :].rearrange("o (p a) n -> p (o a n)", a=2)


def slot_head(s):
    return s % 2, s // 2


def slot_cols(s):
    j, g = slot_head(s)
    return slice((4 * j + g) * DH, (4 * j + g + 1) * DH)


def over_batches(eng, step):
    pipelined(eng, B + 2, step, head=3, tail=5)


class Stages:

    def __init__(self, b):
        self.project = not known(b) or b < B
        self.next = not known(b) or b + 1 < B
        self.heads = not known(b) or 1 <= b <= B
        self.rest = not known(b) or b >= 2


def wo_chunks(b, s):
    if known(b) and b == B and s >= 2:
        return [s - 2]
    if known(b) and b == B + 1 and s == 4:
        return [6, 7]
    return []


TURNED_BY_SCALAR = (1, 4, 6)


def cross_attention(nc, sh, context, wo, q_dram, k_dram, vlast_dram, cl):
    with ExitStack() as ctx:
        sb = lambda *a: ctx.enter_context(nc.sbuf_tensor(*a))
        sem = lambda n: ctx.enter_context(nc.semaphore(n))
        ident, banks, wkv, cx, oT, wo_s, chunk_loaded, cx_loaded = (
            sh.ident, sh.banks, sh.wkv, sh.cx, sh.oT, sh.wo, sh.chunk_loaded, sh.cx_loaded)
        half = SLOT_BYTES // 2
        cT = [sh.at("cT_" + part, LOW0 + i * half, [P, 2, KC, 2 * P], F32R) for i, part in enumerate("hl")]
        kT = [sh.at("kT_" + part, LOW1 + i * half, [P, 2, 2, SKP], F32R) for i, part in enumerate("hl")]
        clT = [sh.at("clT_" + part, LOW1 + i * half + 16 * SKP, [P, KC, P], F32R) for i, part in enumerate("hl")]
        zeros = sh.at("zeros", LOW1 + 16 * SKP + 4 * KC * P, [P, 512])
        vl_sb = sh.at("vl_sb", LOW1 + half + 16 * SKP + 4 * KC * P, [B, KV])
        assert 16 * SKP + 4 * KC * P + 4 * 512 <= half
        wo_raw = [sh.at("wo_raw0", STAGE, [P, KC // 2, D]), sh.at("wo_raw1", LOW0, [P, KC // 2, D])]
        wo_loaded = lambda c: wo_raw[c // (KC // 2)][:, c % (KC // 2), :]
        kcat = sb("kcat", [P, 2, 4 * 2, SKP], F32R)
        qcat = sb("qcat", [P, 2, NG, REP * SQ], F32R)
        v_sb = sb("v_sb", [P, 2, 2, KV], F32)
        vl = sb("vl", [NG, 2, KV], F32)
        prob = sb("prob", [P, 2, NG, SKP], F32)
        pT = sb("pT", [P, NG, 2 * P], F32)
        plT = sb("plT", [NG, P], F32)
        nmax = sb("nmax", [P, 2, NG], F32)
        sums = sb("sums", [P, 2, NG], F32)
        rsums = sb("rsums", [P, NG], F32)
        o_sb = sb("o_sb", [P, KV], F32)
        kl = [sb("kl_h", [P, 2, B], F32R), sb("kl_l", [P, 2, B], F32R)]
        cT_ps, k_ps, v_ps, s_ps = banks[0:2], banks[2], banks[3], banks[4:6]
        turn_ps = banks[6][:, 0:256]
        o_ps = banks[7]

        kcat_loaded = [sem("kcat_loaded0"), sem("kcat_loaded1")]
        qcat_loaded = [sem("qcat_loaded0"), sem("qcat_loaded1")]
        vl_loaded = [sem("vl_loaded0"), sem("vl_loaded1")]
        wo_h_ready, wo_l_ready = sem("wo_h_ready"), sem("wo_l_ready")
        zeros_ready, pads_ready, vl_zeroed, vl_placed = (
            sem("zeros_ready"), sem("pads_ready"), sem("vl_zeroed"), sem("vl_placed"))
        clT_done, clT_h_ready, clT_l_ready, kvl_done, kl_h_ready, kl_l_ready, vl_copied = (
            sem("clT_done"), sem("clT_h_ready"), sem("clT_l_ready"), sem("kvl_done"), sem("kl_h_ready"),
            sem("kl_l_ready"), sem("vl_copied"))
        cT_done, cT_h_ready, cT_l_ready = sem("cT_done"), sem("cT_h_ready"), sem("cT_l_ready")
        k_done, kT_h_ready, kT_l_ready, klast_ready = sem("k_done"), sem("kT_h_ready"), sem("kT_l_ready"), sem("klast_ready")
        v_done, v_copied = sem("v_done"), sem("v_copied")
        s_done, max_done, exp_done = sem("s_done"), sem("max_done"), sem("exp_done")
        k_stored = [sem("k_h_stored"), sem("k_l_stored")]
        passed = sem("passed1")
        turned, turn_copied = sem("turned"), sem("turn_copied")
        last_turned, last_copied, o_turned, o_turn_copied = (
            sem("last_turned"), sem("last_copied"), sem("o_turned"), sem("o_turn_copied"))
        pv_done, o_done, o_copied, rsums_ready = sem("pv_done"), sem("o_done"), sem("o_copied"), sem("rsums_ready")

        def copy_turned(eng, copy, a, i):
            if not known(a) or a >= 1:
                eng.wait_ge(pv_done, NG * (a - 1) + i + 1)
            eng.wait_ge(turned, NG * a + i + 1)
            copy(pT[:, i, :], turn_ps).then_inc(turn_copied, 1)

        block = ctx.enter_context(nc.Block())

        @block.sync
        def _(sp):
            sp.wait_ge(zeros_ready, 1)
            sp.dma_start(vlast_dram.rearrange("b s n -> (b s n)").rearrange("(p n) -> p n", p=P), zeros[:, :]).then_inc(vl_zeroed, 16)
            sp.wait_ge(vl_zeroed, 16)
            sp.wait_ge(vl_copied, 1)
            for s in range(NG):
                sp.dma_start(vlast_dram[:, s, slot_cols(s)], vl_sb[:, slot_cols(s)]).then_inc(vl_placed, 16)

            def step(b, par):
                st = Stages(b)
                if not st.project:
                    if b == B:
                        sp.wait_ge(v_done, B)
                        for c in range(KC // 2, KC):
                            load_wo(c)
                    return
                if not known(b) or b >= 2:
                    sp.wait_ge(s_done, NG * (b - 1))
                if not known(b) or b + 2 < B:
                    sp.wait_ge(cT_done, 4 * b + 4)
                    sp.dma_start(context_tile(cx, par), context_rows(context, b + 2)).then_inc(cx_loaded[par], 16)
                for part, ready in enumerate((kT_h_ready, kT_l_ready)):
                    if part == 0:
                        wait_apart(sp, klast_ready, 2 * b + 2, passed)
                    sp.wait_ge(ready, b + 1)
                    sp.dma_start(k_dram[part, par], kT[part][:, par, :, :].rearrange("p j n -> p (j n)").bitcast(F32)).then_inc(k_stored[part], 16)
                for part in range(2):
                    sp.wait_ge(k_stored[part], 16 * b + 16)
                    for c in (part, part + 2):
                        sp.dma_start(kcat[c * DH:(c + 1) * DH, par, :, :].rearrange("d (g j) n -> d g (j n)", g=4).bitcast(F32),
                                     k_dram[part, par].rearrange("(g d) n -> d g n", g=4)).then_inc(kcat_loaded[par], 16)

                if known(b) and b == B - 1:
                    sp.wait_ge(cT_done, 4 * B)
                    for c in range(KC // 2):
                        load_wo(c)

            def load_wo(c):
                sp.dma_start(wo_loaded(c), wo[c * P:(c + 1) * P, :]).then_inc(chunk_loaded[c], 16)

            over_batches(sp, step)

        @block.gpsimd
        def _(pool):
            pool.memset(zeros[:, :], 0.0).then_inc(zeros_ready, 1)
            for part in range(2):
                pool.memset(clT[part][:, :, :].bitcast(F32), 0.0).then_inc(pads_ready, 1)
                pool.memset(kT[part][:, :, :, SK:SKP].bitcast(F32), 0.0).then_inc(pads_ready, 1)
            pool.wait_ge(kl_l_ready, 1)
            pool.wait_ge(vl_placed, 16 * NG)

            def q_of_batch(b, part):
                return q_dram[part, bass.ds(b // BT, 1), :, bass.ds((b % BT) * NG * SQ, NG * SQ)].rearrange("o (g d) n -> d (o g) n", g=4)

            def step(b, par):
                st = Stages(b)
                if st.project:
                    if not known(b) or b >= 2:
                        pool.wait_ge(k_stored[0], 16 * b - 16)
                        pool.wait_ge(k_stored[1], 16 * b - 16)
                    for part in range(2):
                        pool.tensor_copy(kT[part][:, par, :, SK - 1:SK], kl[part][:, :, bass.ds(b, 1)].bitcast(F32)).then_inc(klast_ready, 1)
                if st.heads:
                    if not known(b) or b >= 3:
                        pool.wait_ge(o_done, b - 2)
                    pool.dma_start(vl[:, 1 - par, :], vlast_dram[bass.ds(b - 1, 1)].rearrange("o s n -> s (o n)")).then_inc(vl_loaded[1 - par], 16)
                if not st.project:
                    return
                if not known(b) or b >= 2:
                    pool.wait_ge(s_done, NG * (b - 1))
                for c in range(4):
                    pool.dma_start(qcat[c * DH:(c + 1) * DH, par, :, :].rearrange("d (g j) n -> d g (j n)", g=4).bitcast(F32),
                                   q_of_batch(b, c // 2)).then_inc(qcat_loaded[par], 16)
            over_batches(pool, step)

        @block.scalar
        def _(act):
            def context_high(b, par, m):
                if not known(b) or b >= 2:
                    act.wait_ge(v_done, b - 1)
                act.wait_ge(cT_done, 4 * b + m + 1)
                act.activation(cT[0][:, par, 2 * m:2 * m + 2, :].rearrange("p a n -> p (a n)"), cT_ps[m % 2][:, :], ACT.Copy).then_inc(cT_h_ready, 1)

            def copy_v(b, par):
                if not known(b) or b >= 2:
                    act.wait_ge(pv_done, NG * (b - 1))
                act.wait_ge(v_done, b + 1)
                act.activation(v_sb[:, par, :, :].rearrange("p a n -> p (a n)"), v_ps[:, :], ACT.Copy).then_inc(v_copied, 1)

            def split_wo(c):
                act.wait_ge(v_done, B)
                act.wait_ge(chunk_loaded[c], 32)
                act.activation(wo_s[0][:, c, :], wo_loaded(c), ACT.Copy).then_inc(wo_h_ready, 1)

            act.wait_ge(pads_ready, 4)
            act.wait_ge(clT_done, 1)
            act.activation(clT[0][:, :, 0:B], cT_ps[0][:, 0:KC * B].rearrange("p (k b) -> p k b", b=B), ACT.Copy).then_inc(clT_h_ready, 1)
            act.wait_ge(kvl_done, 2)
            act.activation(kl[0][:, :, :].rearrange("p j b -> p (j b)"), k_ps[:, 0:2 * B], ACT.Copy).then_inc(kl_h_ready, 1)
            act.activation(vl_sb[:, :], v_ps[0:B, 0:KV], ACT.Copy).then_inc(vl_copied, 1)
            for m in range(4):
                context_high(0, 0, m)

            def step(b, par):
                st = Stages(b)
                for s in range(NG):
                    if st.heads:
                        act.wait_ge(max_done, NG * (b - 1) + s + 1)
                        act.activation(prob[:, 1 - par, s, 0:SK], s_ps[s % 2][:, 0:SK], ACT.Exp, bias=nmax[:, 1 - par, s:s + 1],
                                       accum_out=sums[:, 1 - par, s:s + 1]).then_inc(exp_done, 1)
                    if s == 3 and st.project:
                        if not known(b) or b >= 2:
                            act.wait_ge(k_stored[0], 16 * b - 16)
                        act.wait_ge(k_done, b + 1)
                        act.activation(kT[0][:, par, :, 0:2 * P], k_ps[:, :].rearrange("p (j n) -> p j n", j=2), ACT.Copy).then_inc(kT_h_ready, 1)
                    i = (s - 2) % NG
                    if i in TURNED_BY_SCALAR and (st.rest if s < 2 else st.heads):
                        copy_turned(act, act.copy, b - 2 if s < 2 else b - 1, i)
                    if s == 1 and st.rest:
                        act.wait_ge(last_turned, b - 1)
                        act.activation(plT[:, :], v_ps[0:NG, 0:P], ACT.Copy).then_inc(last_copied, 1)
                    if s == 5 and st.rest:
                        act.wait_ge(o_turned, b - 1)
                        act.activation(oT[:, :, bass.ds((b - 2) * SQ, SQ)],
                                       k_ps[:, 0:2 * P].rearrange("p (m q) -> p m q", q=SQ), ACT.Copy).then_inc(o_turn_copied, 1)
                    if s % 2 == 1 and st.next:
                        context_high(b + 1, 1 - par, s // 2)
                    if s == 7 and st.project:
                        copy_v(b, par)
                    for c in wo_chunks(b, s):
                        split_wo(c)
            over_batches(act, step)

        @block.vector
        def _(dve):
            def context_low(b, par, m):
                dve.wait_ge(cT_h_ready, 4 * b + m + 1)
                high = cT[0][:, par, 2 * m:2 * m + 2, :].rearrange("p a n -> p (a n)").bitcast(F32)
                dve.tensor_tensor(cT[1][:, par, 2 * m:2 * m + 2, :].rearrange("p a n -> p (a n)"), cT_ps[m % 2][:, :],
                                  high, ALU.subtract).then_inc(cT_l_ready, 1)

            dve.wait_ge(clT_h_ready, 1)
            dve.tensor_tensor(clT[1][:, :, 0:B], cT_ps[0][:, 0:KC * B].rearrange("p (k b) -> p k b", b=B),
                              clT[0][:, :, 0:B].bitcast(F32), ALU.subtract).then_inc(clT_l_ready, 1)
            dve.wait_ge(kl_h_ready, 1)
            dve.tensor_tensor(kl[1][:, :, :].rearrange("p j b -> p (j b)"), k_ps[:, 0:2 * B],
                              kl[0][:, :, :].rearrange("p j b -> p (j b)").bitcast(F32), ALU.subtract).then_inc(kl_l_ready, 1)
            for m in range(4):
                context_low(0, 0, m)

            def step(b, par):
                st = Stages(b)
                for s in range(NG):
                    if st.heads:
                        dve.wait_ge(s_done, NG * (b - 1) + s + 1)
                        dve.reduce_max(nmax[:, 1 - par, s:s + 1], s_ps[s % 2][:, 0:SK], AXX, negate=True).then_inc(max_done, 1)
                    i = (s - 2) % NG
                    if i not in TURNED_BY_SCALAR and (st.rest if s < 2 else st.heads):
                        copy_turned(dve, dve.tensor_copy, b - 2 if s < 2 else b - 1, i)
                    if s == 3 and st.project:
                        if not known(b) or b >= 2:
                            dve.wait_ge(k_stored[1], 16 * b - 16)
                        dve.wait_ge(kT_h_ready, b + 1)
                        dve.tensor_tensor(kT[1][:, par, :, 0:2 * P], k_ps[:, :].rearrange("p (j n) -> p j n", j=2),
                                          kT[0][:, par, :, 0:2 * P].bitcast(F32), ALU.subtract).then_inc(kT_l_ready, 1)
                    if s % 2 == 1 and st.next:
                        context_low(b + 1, 1 - par, s // 2)
                    if s == 3 and st.rest:
                        dve.wait_ge(o_done, b - 1)
                        dve.reciprocal(rsums[:, :].rearrange("p (j g) -> p j g", j=2),
                                       sums[:, par, :].rearrange("p (g j) -> p j g", j=2)).then_inc(rsums_ready, 1)
                        dve.wait_ge(rsums_ready, b - 1)
                        if not known(b) or b >= 3:
                            dve.wait_ge(o_turned, b - 2)
                        dve.tensor_tensor(o_sb[:, :].rearrange("p (g d) -> p g d", d=DH), o_ps[:, 0:KV].rearrange("p (g d) -> p g d", d=DH),
                                          rsums[:, :].unsqueeze(2).to_broadcast([P, NG, DH]), ALU.mult).then_inc(o_copied, 1)
                    for c in wo_chunks(b, s):
                        if c == 0:
                            for part in range(2):
                                dve.wait_ge(k_stored[part], 16 * B)
                        dve.wait_ge(wo_h_ready, c + 1)
                        dve.tensor_tensor(wo_s[1][:, c, :], wo_loaded(c), wo_s[0][:, c, :].bitcast(F32), ALU.subtract).then_inc(wo_l_ready, 1)
            over_batches(dve, step)

        @block.tensor
        def _(pe):
            def transpose_context(b, par, m):
                if m == 0:
                    pe.wait_ge(cx_loaded[par], 8 * (b - par) + 16)
                if not known(b) or 4 * b + m >= 2:
                    pe.wait_ge(cT_l_ready, 4 * b + m - 1)
                for k in range(2 * m, 2 * m + 2):
                    for a in range(2):
                        n = (k % 2) * 2 + a
                        o = pe.transpose(cT_ps[m % 2][:, n * P:(n + 1) * P], cx[:, par, a, k * P:(k + 1) * P], ident[:, :])
                o.then_inc(cT_done, 1)

            def keys(b, par, s, first):
                j = s // 2
                for k in range(s % 2 * 4 + (0 if first else 2), s % 2 * 4 + (2 if first else 4)):
                    for n, (x, y) in enumerate(PASSES):
                        o = pe.matmul(k_ps[:, j * 256:(j + 1) * 256], wkv[x][:, k, j * P:(j + 1) * P], cT[y][:, par, k, :],
                                      start=(j == 0 and k == 0 and n == 0), stop=(j == 1 and k == KC - 1 and n == 2), skip_group_check=True)
                if s == 3 and not first:
                    o.then_inc(k_done, 1)

            def values(b, par, s, first):
                a = s // 2 - 2
                for k in range(s % 2 * 4 + (0 if first else 2), s % 2 * 4 + (2 if first else 4)):
                    for n, (x, y) in enumerate(PASSES):
                        o = pe.matmul(v_ps[:, a * KV:(a + 1) * KV], cT[x][:, par, k, a * P:(a + 1) * P], wkv[y][:, k, KV:2 * KV],
                                      start=(a == 0 and k == 0 and n == 0), stop=(a == 1 and k == KC - 1 and n == 2), skip_group_check=True)
                if s == 7 and not first:
                    o.then_inc(v_done, 1)

            def project(b, par, s, first):
                st = Stages(b)
                if s < 3 and st.project:
                    keys(b, par, s + 1, first)
                elif s < 7 and st.project:
                    values(b, par, s + 1, first)
                elif s == 7 and st.next:
                    keys(b + 1, 1 - par, 0, first)

            def turn(dst, pieces):
                for n, (rows, src) in enumerate(pieces):
                    o = pe.transpose(dst[0:rows, n * P:(n + 1) * P], src, ident[:, :])
                return o

            def turn_prob(a, ap, i):
                pe.wait_ge(exp_done, NG * a + i + 1)
                if not known(a) or NG * a + i >= 1:
                    pe.wait_ge(turn_copied, NG * a + i)
                turn(turn_ps, [(P, prob[:, ap, i, c * P:(c + 1) * P]) for c in range(2)]).then_inc(turned, 1)

            def times_values(a, ap, i):
                pe.wait_ge(turn_copied, NG * a + i + 1)
                if i == 0:
                    pe.wait_ge(v_copied, a + 1)
                    if not known(a) or a >= 1:
                        pe.wait_ge(o_copied, a)
                for c in range(2):
                    o = pe.matmul(o_ps[:, slot_cols(i)], pT[:, i, c * P:(c + 1) * P], v_sb[:, ap, c, slot_cols(i)],
                                  start=(i == 0 and c == 0), stop=False, skip_group_check=True)
                o.then_inc(pv_done, 1)

            pe.wait_ge(sh.cl_loaded, 16)
            for k in range(KC):
                o = pe.transpose(cT_ps[0][:, k * B:(k + 1) * B], cl[:, k * P:(k + 1) * P], ident[0:B, 0:B])
            o.then_inc(clT_done, 1)
            pe.wait_ge(clT_l_ready, 1)
            for j in range(2):
                for k in range(KC):
                    for n, (x, y) in enumerate(PASSES):
                        o = pe.matmul(k_ps[:, j * B:(j + 1) * B], wkv[x][:, k, j * P:(j + 1) * P], clT[y][:, k, 0:B],
                                      start=(j == 0 and k == 0 and n == 0), stop=(j == 1 and k == KC - 1 and n == 2), skip_group_check=True)
            o.then_inc(kvl_done, 1)
            for k in range(KC):
                for n, (x, y) in enumerate(PASSES):
                    o = pe.matmul(v_ps[:, 0:KV], clT[x][:, k, :], wkv[y][:, k, KV:2 * KV],
                                  start=(k == 0 and n == 0), stop=(k == KC - 1 and n == 2))
            o.then_inc(kvl_done, 1)
            for m in range(4):
                transpose_context(0, 0, m)
            pe.wait_ge(vl_copied, 1)
            pe.wait_ge(kl_l_ready, 1)
            pe.wait_ge(cT_l_ready, 2)
            for first in (True, False):
                keys(0, 0, 0, first)

            def step(b, par):
                st = Stages(b)
                for s in range(NG):
                    if s < 4 and st.rest:
                        times_values(b - 2, par, s + 4)
                    if s == 3 and st.rest:
                        pe.wait_ge(last_copied, b - 1)
                        pe.wait_ge(vl_loaded[par], 8 * (b - 2 - par) + 16)
                        pe.matmul(o_ps[:, 0:KV], plT[:, :], vl[:, par, :], start=False, stop=True, skip_group_check=True).then_inc(o_done, 1)
                    if st.heads:
                        if s == 0:
                            pe.wait_ge(qcat_loaded[1 - par], 32 * (b - 2 + par) + 64)
                            pe.wait_ge(kcat_loaded[1 - par], 32 * (b - 2 + par) + 64)
                        if not known(b) or NG * (b - 1) + s >= 2:
                            pe.wait_ge(exp_done, NG * (b - 1) + s - 1)
                        pe.matmul(s_ps[s % 2][:, 0:SKP], qcat[:, 1 - par, s, :], kcat[:, 1 - par, s, :], start=True, stop=True).then_inc(s_done, 1)
                    if s < 2 and st.rest:
                        turn_prob(b - 2, par, s + 6)
                    if s == 1 and st.rest:
                        pe.wait_ge(v_copied, b if st.project else B)
                        turn(v_ps, [(NG, prob[:, par, :, SK - 1])]).then_inc(last_turned, 1)
                    if s == 5 and st.rest:
                        pe.wait_ge(o_copied, b - 1)
                        pe.wait_ge(kT_l_ready, b + 1 if st.project else B)
                        turn(k_ps, [(P, o_sb[:, j * P:(j + 1) * P]) for j in range(2)]).then_inc(o_turned, 1)
                    if s == 0 and st.project:
                        pe.wait_ge(cT_l_ready, 4 * b + 4)
                    if s == 3 and st.project and (not known(b) or b >= 1):
                        pe.wait_ge(v_copied, b)
                        if not known(b) or b >= 2:
                            pe.wait_ge(last_copied, b - 1)
                    if s == 7 and st.next:
                        pe.wait_ge(cT_l_ready, 4 * b + 6)
                        pe.wait_ge(kT_l_ready, b + 1)
                        if not known(b) or b >= 2:
                            pe.wait_ge(o_turn_copied, b - 1)
                    project(b, par, s, True)
                    if s >= 2 and st.heads:
                        turn_prob(b - 1, 1 - par, s - 2)
                    if s % 2 == 0 and st.next:
                        transpose_context(b + 1, 1 - par, s // 2)
                    project(b, par, s, False)
                    if s >= 4 and st.heads:
                        times_values(b - 1, 1 - par, s - 4)
            over_batches(pe, step)


MT = 2 * NT + E - 1
AHEAD = 3
COLS = MT + AHEAD
ROWS = (E - 1) * B * SQ + (COLS - E + 1) * P


def mixing(nc, sh, x, eta, gate, expert_w, x3_dram, n_dram, slot_dram):
    with ExitStack() as ctx:
        sb = lambda *a: ctx.enter_context(nc.sbuf_tensor(*a))
        sem = lambda n: ctx.enter_context(nc.semaphore(n))
        ident, banks, oT, wo_s, chunk_loaded = sh.ident, sh.banks, sh.oT, sh.wo, sh.chunk_loaded
        w_h_ready, w_l_ready, y_pos, wts, tiles = sh.w_h_ready, sh.w_l_ready, sh.y_pos, sh.wts, sh.tiles
        raw = sh.at("expert0_raw", HIGH1, [P, KC, D])
        expert0 = [sh.w[part][:, 0:SLOT].rearrange("p (c n) -> p c n", n=D) for part in range(2)]
        ot = [sb("ot_h", [P, 2, KC, P], F32R), sb("ot_l", [P, 2, KC, P], F32R)]
        x_in, x2 = sh.at("x_in2", STAGE, [P, 2, D]), sh.at("x2", STAGE + 8 * D, [P, 2, D])
        y = sb("y", [P, 2, D], F32)
        yT = sb("yT", [P, D], F32)
        x3 = sb("x3", [P, 2, D], F32)
        n = sb("n", [P, 2, D], F32)
        x3z = n
        nT = sb("nT", [P, D], F32)
        gate_sb = sb("gate_sb", [P, KC, E], F32)
        eta_sb = sb("eta_sb", [P, 1], F32)
        scores = sb("scores", [P, SQ], F32)
        low = sb("low", [P, 1], F32)
        prob = sb("prob2", [P, SQ], F32)
        psum_row = sb("psum_row", [P, 1], F32)
        scale = sb("scale", [P, 2, 1], F32)
        probT = sb("probT", [P, P], F32)
        logits = sb("logits", [P, E], F32)
        top = sb("top", [P, E], F32)
        top_i = sb("top_i", [P, E], U32)
        gap = sb("gap", [P, 1], F32)
        egap = sb("egap", [P, 1], F32)
        chosen_f = sb("chosen_f", [P, 2], F32)
        hot = sb("hot", [P, 2, E], F32)
        both = sb("both", [P, E], F32)
        before = sb("before", [P, E], F32)
        ranked = sb("ranked", [P, E], F32)
        row = sb("row", [P, 2, E], F32)
        slot = sb("slot", [P, 2 * NT], I32)
        earlier = sb("earlier", [P, P], F32)
        ones = sb("ones", [P, P], F32)
        expert_iota = sb("expert_iota", [P, E], F32)
        region = sb("region", [P, E], F32)
        token = sb("token", [P, NT], I32)
        zero_slots = sb("zero_slots", [P, ROWS // P], I32)
        counts = sb("counts", [P, E], F32)
        steps128 = sb("steps128", [P, E, NT], F32)
        over = sb("over", [P, E, NT], F32)
        n_tiles = sb("n_tiles", [P, E], F32)
        n_tiles1 = sb("n_tiles1", [P, E], F32)
        first = sb("first", [P, E], F32)
        zero8 = sb("zero8", [P, E], F32)
        cut = sb("cut", [P, E], F32)
        slot_f = sb("slot_f", [P, 2 * NT], F32)
        behind = sb("behind", [P, 2 * NT, E], F32)
        cuts = sb("cuts", [P, 2 * NT, E], F32)
        cut_of = sb("cut_of", [P, 2 * NT], F32)
        tile_iota = sb("tile_iota", [1, COLS], F32)
        reached = sb("reached", [1, COLS, E], F32)
        start = sb("start", [1, COLS, E], F32)
        e_f = sb("e_f", [1, 2, COLS], F32)
        f_f = sb("f_f", [1, 2, COLS], F32)
        norm2 = Norm(nc, ctx, "norm2")
        norm3 = Norm(nc, ctx, "norm3")
        o_ps, t_ps, r_ps, g_ps, e_ps = banks[0:2], banks[2:4], banks[4:6], banks[6], banks[7]

        x_loaded = [sem("x2_loaded0"), sem("x2_loaded1")]
        small_loaded, slots_zeroed = sem("small_loaded"), sem("slots_zeroed")
        consts = sem("consts")
        ot_h_ready, ot_l_ready, xo_done, x2_ready, y_ready = sem("ot_h_ready"), sem("ot_l_ready"), sem("xo_done"), sem("x2_ready"), sem("y_ready")
        t_done, t_copied, g_done, blocks, low_ready, prob_ready, probT_ready = (
            sem("t_done"), sem("t_copied"), sem("g_done"), sem("blocks"), sem("low_ready"), sem("prob_ready"), sem("probT_ready"))
        psr_ready, scale_ready, r_done, z_ready, x3_ready, n_ready = (
            sem("psr_ready"), sem("scale_ready"), sem("r_done"), sem("z_ready"), sem("x3_ready"), sem("n_ready"))
        x3_stored = [sem("x3_stored0"), sem("x3_stored1")]
        gate_done, logits_ready, route, gap_ready, egap_ready, both_ready, rank_done, rows_ready = (
            sem("gate_done"), sem("logits_ready"), sem("route"), sem("gap_ready"), sem("egap_ready"), sem("both_ready"),
            sem("rank_done"), sem("rows_ready"))
        scattered, counted, plan, passed = sem("scattered"), sem("counted"), sem("plan"), sem("passed2")
        N_STEPS = NT + 3

        def steps(eng, step):
            pipelined(eng, N_STEPS, step, head=3, tail=4)

        def on(t, lag):
            return not known(t) or 0 <= t - lag < NT

        block = ctx.enter_context(nc.Block())

        def expert0_chunks(t):
            return {NT + 1: range(0, 5), NT + 2: range(5, KC)}.get(t, ()) if known(t) else ()

        def turned_before(t):
            if known(t):
                return sum((0 <= s - 1 < NT) + (0 <= s - 2 < NT) for s in range(t))
            return 2 * t - 3

        @block.sync
        def _(sp):
            def load_x(t, par):
                sp.dma_start(x_in[:, par, :], x[bass.ts(t, P), :]).then_inc(x_loaded[par], 16)
            load_x(0, 0)
            load_x(1, 1)
            sp.dma_start(gate_sb[:, :, :], gate.rearrange("(c p) e -> p c e", p=P)).then_inc(small_loaded, 16)
            sp.dma_start(eta_sb[:, :], eta.rearrange("(a b) -> a b", a=1).to_broadcast([P, 1])).then_inc(small_loaded, 16)
            sp.wait_ge(consts, 10)
            sp.dma_start(slot_dram.rearrange("(p n) o -> p (n o)", p=P), zero_slots[:, :]).then_inc(slots_zeroed, 16)

            def step(t, par):
                if (not known(t) or t >= 1) and (not known(t) or t + 1 < NT) and not (known(t) and t < 1):
                    sp.wait_ge(x2_ready, 2 * t)
                    load_x(t + 1, 1 - par)
                if known(t) and t == NT:
                    sp.wait_ge(xo_done, 2 * NT)
                    for c in range(KC):
                        sp.dma_start(raw[:, c, :], expert_w[0, c * P:(c + 1) * P, :]).then_inc(chunk_loaded[c], 16)
                if on(t, 2):
                    sp.wait_ge(n_ready, t - 1)
                    sp.dma_start(n_dram[bass.ds((t - 2) * P, P), :], n[:, par, :]).then_inc(x3_stored[par], 16)
                    sp.dma_start(x3_dram[bass.ds((t - 2) * P, P), :], x3[:, par, :]).then_inc(x3_stored[par], 16)
            steps(sp, step)
            for par in range(2):
                sp.wait_ge(x3_stored[par], 32 * NT // 2)

        @block.gpsimd
        def _(pool):
            pool.memset(probT[:, :], 0.0).then_inc(consts, 1)
            pool.memset(ones[:, :], 1.0).then_inc(consts, 1)
            pool.memset(before[:, :], 0.0).then_inc(consts, 1)
            pool.memset(zero_slots[:, :], 0).then_inc(consts, 1)
            pool.memset(zero8[:, :], 0.0).then_inc(consts, 1)
            pool.iota(expert_iota[:, :], [[1, E]], base=0, channel_multiplier=0, allow_small_or_imprecise_dtypes=True).then_inc(consts, 1)
            pool.iota(region[:, :], [[B * SQ, E]], base=0, channel_multiplier=0, allow_small_or_imprecise_dtypes=True).then_inc(consts, 1)
            pool.iota(token[:, :], [[P, NT]], base=0, channel_multiplier=1).then_inc(consts, 1)
            pool.iota(steps128[:, :, :], [[0, E], [P, NT]], base=0, channel_multiplier=0, allow_small_or_imprecise_dtypes=True).then_inc(consts, 1)
            pool.iota(tile_iota[:, :], [[1, COLS]], base=0, channel_multiplier=0, allow_small_or_imprecise_dtypes=True).then_inc(consts, 1)
            pool.wait_ge(consts, 10)
            pool.affine_select(out=earlier[:, :], in_=ones[:, :], compare_op=ALU.is_gt, fill=0.0, base=0,
                               pattern=[[1, P]], channel_multiplier=-1).then_inc(consts, 1)
            norm2.start_gpsimd(pool)
            norm3.start_gpsimd(pool)
            pool.wait_ge(slots_zeroed, 16)

            def step(t, par):
                if on(t, 1):
                    norm2.on_gpsimd(pool, t - 1)
                if on(t, 2):
                    for h in range(2):
                        pool.wait_ge(z_ready, 2 * (t - 2) + h + 1)
                        if h == 0 and (not known(t) or t >= 4):
                            pool.wait_ge(x3_stored[par], (t - 2 - par) * 16)
                        pool.tensor_tensor(x3[:, par, h * 512:(h + 1) * 512], x2[:, par, h * 512:(h + 1) * 512],
                                           x3z[:, par, h * 512:(h + 1) * 512], ALU.add).then_inc(x3_ready, 1)
                    norm3.on_gpsimd(pool, t - 2)
                if on(t, 3):
                    wait_apart(pool, rows_ready, t - 2, passed)
                    for c in range(2):
                        pool.indirect_dma_start(slot_dram, bass.IndirectOffsetOnAxis(ap=slot_of(t - 3, c), axis=0),
                                                token_of(t - 3), None).then_inc(scattered, 16)
            def slot_of(t, c):
                return slot[:, bass.ds(2 * t + c, 1)]

            def token_of(t):
                return token[:, bass.ds(t, 1)]
            for t in range(N_STEPS):
                step(t, t % 2)
            pool.wait_ge(scattered, 16 * 2 * NT)
            pool.dma_start(sh.idx[:, 0:1], slot_dram[0:P, :]).then_inc(sh.idx_loaded, 16)
            pool.wait_ge(x2_ready, 2 * NT)
            for par in range(2):
                pool.wait_ge(x3_stored[par], 32 * NT // 2)
            pool.wait_ge(sh.idx_loaded, 16)
            pool.indirect_dma_start(sh.xg[:, 0, :], None, n_dram, bass.IndirectOffsetOnAxis(ap=sh.idx[:, 0:1], axis=0)).then_inc(sh.xg_loaded, 16)

        @block.scalar
        def _(act):
            def ot_high(t, par):
                if not known(t) or t >= 2:
                    act.wait_ge(xo_done, 2 * t - 2)
                act.activation(ot[0][:, par, :, :], oT[:, :, bass.ds(t * P, P)], ACT.Copy).then_inc(ot_h_ready, 1)
            ot_high(0, 0)

            def copy_turned(dst, number):
                for h in range(2):
                    act.wait_ge(t_done, 2 * number + h + 1)
                    act.activation(dst[:, h * 512:(h + 1) * 512], t_ps[h][:, :], ACT.Copy).then_inc(t_copied, 1)

            def step(t, par):
                if on(t, -1) and on(t, 0):
                    ot_high(t + 1, 1 - par)
                if on(t, 1):
                    if not known(t) or t >= 2:
                        act.wait_ge(g_done, t - 1)
                    copy_turned(yT, turned_before(t))
                if on(t, 2):
                    if not known(t) or t >= 3:
                        act.wait_ge(gate_done, t - 2)
                    copy_turned(nT, turned_before(t) + (1 if on(t, 1) else 0))
                if on(t, 3):
                    act.wait_ge(gap_ready, t - 2)
                    act.activation(egap[:, :], gap[:, :], ACT.Exp).then_inc(egap_ready, 1)
                if on(t, 1):
                    act.wait_ge(low_ready, t)
                    act.activation(prob[:, :], scores[:, :], ACT.Exp, bias=low[:, 0:1], scale=-1.0,
                                   accum_out=psum_row[:, :]).then_inc(prob_ready, 1)
                for c in expert0_chunks(t):
                    act.wait_ge(chunk_loaded[c], 48)
                    act.activation(expert0[0][:, c, :], raw[:, c, :], ACT.Copy).then_inc(w_h_ready, 1)
            steps(act, step)

        @block.vector
        def _(dve):
            def ot_low(t, par):
                dve.wait_ge(ot_h_ready, t + 1)
                dve.tensor_tensor(ot[1][:, par, :, :], oT[:, :, bass.ds(t * P, P)], ot[0][:, par, :, :].bitcast(F32), ALU.subtract).then_inc(ot_l_ready, 1)
            ot_low(0, 0)
            dve.wait_ge(consts, 11)
            dve.wait_ge(small_loaded, 32)

            def step(t, par):
                if on(t, 1):
                    dve.wait_ge(x_loaded[1 - par], (t - 2 + par) * 8 + 16)
                    if not known(t) or t >= 3:
                        dve.wait_ge(x3_ready, 2 * (t - 3) + 2)
                    for h in range(2):
                        dve.wait_ge(xo_done, 2 * (t - 1) + h + 1)
                        dve.tensor_tensor(x2[:, 1 - par, h * 512:(h + 1) * 512], o_ps[h][:, :], x_in[:, 1 - par, h * 512:(h + 1) * 512], ALU.add).then_inc(x2_ready, 1)
                    dve.wait_ge(x2_ready, 2 * t)
                    norm2.on_vector(dve, t - 1, y[:, 1 - par, :], x2[:, 1 - par, :]).then_inc(y_ready, 1)
                if on(t, 2):
                    if not known(t) or t >= 4:
                        dve.wait_ge(x3_stored[par], (t - 2 - par) * 16)
                    wait_apart(dve, scale_ready, t - 1, passed)
                    for h in range(2):
                        dve.wait_ge(r_done, 2 * (t - 2) + h + 1)
                        dve.scalar_tensor_tensor(out=x3z[:, par, h * 512:(h + 1) * 512], in0=r_ps[h][:, :], scalar=scale[:, par, :],
                                                 in1=y[:, par, h * 512:(h + 1) * 512], op0=ALU.mult, op1=ALU.add).then_inc(z_ready, 1)
                if on(t, 3):
                    route_tile(t - 3)
                if on(t, 2):
                    dve.wait_ge(x3_ready, 2 * (t - 2) + 2)
                    norm3.on_vector(dve, t - 2, n[:, par, :], x3[:, par, :]).then_inc(n_ready, 1)
                if on(t, -1) and on(t, 0):
                    ot_low(t + 1, 1 - par)
                for c in expert0_chunks(t):
                    dve.wait_ge(w_h_ready, c + 1)
                    dve.tensor_tensor(expert0[1][:, c, :], raw[:, c, :], expert0[0][:, c, :].bitcast(F32), ALU.subtract).then_inc(w_l_ready, 1)
                if on(t, 3):
                    rank_tile(t - 3)
                if on(t, 1):
                    dve.wait_ge(g_done, t)
                    for b in range(BT):
                        q = slice(b * SQ, (b + 1) * SQ)
                        dve.tensor_copy(scores[q, :], g_ps[q, q]).then_inc(blocks, 1)
                    dve.wait_ge(blocks, 4 * t)
                    dve.tensor_reduce(low[:, :], scores[:, :], AXX, ALU.min).then_inc(low_ready, 1)
                    dve.wait_ge(prob_ready, t)
                    dve.reciprocal(scale[:, 1 - par, :], psum_row[:, :]).then_inc(psr_ready, 1)
                    if not known(t) or t >= 2:
                        dve.wait_ge(r_done, 2 * (t - 1))
                    for b in range(BT):
                        q = slice(b * SQ, (b + 1) * SQ)
                        o = dve.transpose(probT[q, q], prob[q, :])
                    o.then_inc(probT_ready, 1)
                    dve.wait_ge(psr_ready, t)
                    dve.tensor_scalar(scale[:, 1 - par, :], scale[:, 1 - par, :], eta_sb[:, 0:1], None, ALU.mult).then_inc(scale_ready, 1)
            def chain(o, count):
                o.then_inc(route, 1)
                wait_apart(dve, route, count, passed)

            def route_tile(t):
                c = 12 * t
                dve.wait_ge(gate_done, t + 1)
                chain(dve.tensor_copy(logits[:, :], e_ps[:, 0:E]), c + 1)
                chain(dve.max(top[:, :], logits[:, :]), c + 2)
                dve.tensor_tensor(gap[:, :], top[:, 1:2], top[:, 0:1], ALU.subtract).then_inc(gap_ready, 1)
                chain(dve.max_index(top_i[:, :], top[:, :], logits[:, :]), c + 3)
                chain(dve.tensor_copy(chosen_f[:, :], top_i[:, 0:2]), c + 4)
                for k in range(2):
                    chain(dve.tensor_scalar(hot[:, k, :], expert_iota[:, :], chosen_f[:, k:k + 1], None, ALU.is_equal), c + 5 + k)
                dve.tensor_tensor(both[:, :], hot[:, 0, :], hot[:, 1, :], ALU.add).then_inc(both_ready, 1)

            def rank_tile(t):
                c = 12 * t
                dve.wait_ge(egap_ready, t + 1)
                chain(dve.tensor_scalar(chosen_f[:, 0:1], egap[:, :], 1.0, None, ALU.add), c + 7)
                chain(dve.reciprocal(wts[:, bass.ds(2 * t, 1)], chosen_f[:, 0:1]), c + 8)
                dve.tensor_tensor(wts[:, bass.ds(2 * t + 1, 1)], egap[:, :], wts[:, bass.ds(2 * t, 1)], ALU.mult)
                dve.wait_ge(rank_done, t + 1)
                chain(dve.tensor_tensor(ranked[:, :], e_ps[:, 64:64 + E], region[:, :], ALU.add), c + 9)
                dve.tensor_tensor(before[:, :], before[:, :], both[:, :], ALU.add)
                chain(dve.tensor_tensor(row[:, :, :], hot[:, :, :], ranked[:, :].unsqueeze(1).to_broadcast([P, 2, E]), ALU.mult), c + 10)
                chain(dve.tensor_reduce(slot_f[:, bass.ds(2 * t, 2)], row[:, :, :], AXX, ALU.add), c + 11)
                chain(dve.tensor_copy(slot[:, bass.ds(2 * t, 2)], slot_f[:, bass.ds(2 * t, 2)]), c + 12)
                dve.sem_inc(rows_ready, 1)
            steps(dve, step)

            pc = [0]

            def then(o):
                pc[0] += 1
                o.then_inc(plan, 1)
                dve.wait_ge(plan, pc[0])
            dve.wait_ge(counted, 1)
            then(dve.tensor_copy(counts[:, :], e_ps[:, 0:E]))
            then(dve.tensor_tensor(over[:, :, :], counts[:, :].unsqueeze(2).to_broadcast([P, E, NT]), steps128[:, :, :], ALU.is_gt))
            then(dve.tensor_reduce(n_tiles[:, :], over[:, :, :], AXX, ALU.add))
            then(dve.tensor_scalar(n_tiles1[:, :], n_tiles[:, :], 1.0, None, ALU.max))
            then(dve.tensor_tensor_scan(first[:, :], n_tiles1[:, :], zero8[:, :], 0.0, ALU.add, ALU.add))
            then(dve.tensor_tensor(f_f[:, 0, :], tile_iota[:, :], first[0:1, E - 1:E].to_broadcast([1, COLS]), ALU.is_lt))
            then(dve.tensor_copy(tiles[:, 3, :], f_f[:, 0, :]))
            then(dve.tensor_copy(tiles[:, 4, :], first[0:1, E - 1:E].to_broadcast([1, COLS])))
            then(dve.tensor_tensor(first[:, :], first[:, :], n_tiles1[:, :], ALU.subtract))
            first_b = first[0:1, :].unsqueeze(1).to_broadcast([1, COLS, E])
            then(dve.tensor_tensor(reached[:, :, :], tile_iota[:, :].unsqueeze(2).to_broadcast([1, COLS, E]), first_b, ALU.is_ge))
            then(dve.tensor_tensor(start[:, :, :], reached[:, :, :], first_b, ALU.mult))
            then(dve.tensor_reduce(e_f[:, 0, :], reached[:, :, :], AXX, ALU.add))
            then(dve.tensor_reduce(e_f[:, 1, :], start[:, :, :], AXX, ALU.max))
            then(dve.tensor_scalar(f_f[:, 0, :], e_f[:, 0, :], -1.0, None, ALU.add))
            then(dve.tensor_tensor(f_f[:, 1, :], tile_iota[:, :], e_f[:, 1, :], ALU.subtract))
            then(dve.tensor_copy(tiles[:, 0, :], f_f[:, 0, :]))
            then(dve.tensor_copy(tiles[:, 1, :], f_f[:, 1, :]))
            then(dve.tensor_scalar(e_f[:, 0, :], f_f[:, 1, :], 0.0, None, ALU.is_equal))
            then(dve.tensor_scalar(e_f[:, 1, :], f_f[:, 0, :], float(E - 1), None, ALU.is_lt))
            then(dve.tensor_tensor(f_f[:, 0, :], e_f[:, 0, :], e_f[:, 1, :], ALU.mult))
            then(dve.tensor_copy(tiles[:, 2, :], f_f[:, 0, :]))
            then(dve.scalar_tensor_tensor(out=cut[:, :], in0=first[:, :], scalar=-float(P), in1=region[:, :], op0=ALU.mult, op1=ALU.add))
            then(dve.tensor_tensor(behind[:, :, :], slot_f[:, :].unsqueeze(2).to_broadcast([P, 2 * NT, E]),
                                   region[:, :].unsqueeze(1).to_broadcast([P, 2 * NT, E]), ALU.is_ge))
            then(dve.tensor_tensor(cuts[:, :, :], behind[:, :, :], cut[:, :].unsqueeze(1).to_broadcast([P, 2 * NT, E]), ALU.mult))
            then(dve.tensor_reduce(cut_of[:, :], cuts[:, :, :], AXX, ALU.max))
            then(dve.tensor_tensor(behind[:, :, 0], slot_f[:, :], cut_of[:, :], ALU.subtract))
            then(dve.tensor_copy(y_pos[:, :], behind[:, :, 0]))

        @block.tensor
        def _(pe):
            def product(t, par, unit):
                h = unit // 4
                if unit == 0:
                    pe.wait_ge(ot_l_ready, t + 1)
                if unit % 4 == 0 and (not known(t) or t >= 1):
                    pe.wait_ge(x2_ready, 2 * (t - 1) + h + 1)
                for k in range(unit % 4 * 2, unit % 4 * 2 + 2):
                    for m, (a, b) in enumerate(PASSES):
                        o = pe.matmul(o_ps[h][:, :], ot[a][:, par, k, :], wo_s[b][:, k, h * 512:(h + 1) * 512],
                                      start=(k == 0 and m == 0), stop=(k == KC - 1 and m == 2))
                if unit % 4 == 3:
                    o.then_inc(xo_done, 1)

            def turn(src, number):
                for k in range(KC):
                    if k % 4 == 0 and (not known(number) or number >= 1):
                        pe.wait_ge(t_copied, 2 * (number - 1) + k // 4 + 1)
                    o = pe.transpose(t_ps[k // 4][:, k % 4 * P:(k % 4 + 1) * P], src[:, k * P:(k + 1) * P], ident[:, :])
                    if k % 4 == 3:
                        o.then_inc(t_done, 1)

            def step(t, par):
                if known(t) and t == 1:
                    pe.wait_ge(consts, 11)
                    pe.wait_ge(small_loaded, 32)
                for unit in range(KC):
                    if unit == 7 and on(t, 3):
                        pe.wait_ge(both_ready, t - 2)
                        pe.matmul(e_ps[:, 64:64 + E], earlier[:, :], both[:, :], start=True, stop=False)
                        pe.matmul(e_ps[:, 64:64 + E], ones[:, :], before[:, :], start=False, stop=True).then_inc(rank_done, 1)
                    if unit == 2 and on(t, 2):
                        pe.wait_ge(probT_ready, t - 1)
                        for h in range(2):
                            if not known(t) or t >= 3:
                                pe.wait_ge(z_ready, 2 * (t - 3) + h + 1)
                            pe.matmul(r_ps[h][:, :], probT[:, :], y[:, par, h * 512:(h + 1) * 512], start=True, stop=True).then_inc(r_done, 1)
                    if unit == 4 and on(t, 1):
                        pe.wait_ge(y_ready, t)
                        turn(y[:, 1 - par, :], turned_before(t))
                    if unit == 6 and on(t, 2):
                        pe.wait_ge(n_ready, t - 1)
                        turn(n[:, par, :], turned_before(t) + (1 if on(t, 1) else 0))
                    if unit == 6 and on(t, 1):
                        pe.wait_ge(t_copied, 2 * turned_before(t) + 2)
                        if not known(t) or t >= 2:
                            pe.wait_ge(blocks, 4 * (t - 1))
                        for k in range(KC):
                            o = pe.matmul(g_ps[:, 0:P], yT[:, k * P:(k + 1) * P], yT[:, k * P:(k + 1) * P], start=(k == 0), stop=(k == KC - 1))
                        o.then_inc(g_done, 1)
                    if on(t, 0):
                        product(t, par, unit)
                if on(t, 2):
                    pe.wait_ge(t_copied, 2 * (turned_before(t) + (1 if on(t, 1) else 0)) + 2)
                    if not known(t) or t >= 3:
                        pe.wait_ge(rows_ready, t - 2)
                    for k in range(KC):
                        o = pe.matmul(e_ps[:, 0:E], nT[:, k * P:(k + 1) * P], gate_sb[:, k, :], start=(k == 0), stop=(k == KC - 1))
                    o.then_inc(gate_done, 1)
            steps(pe, step)
            pe.wait_ge(rows_ready, NT)
            pe.matmul(e_ps[:, 0:E], ones[:, :], before[:, :], start=True, stop=True).then_inc(counted, 1)


def experts(nc, sh, expert_w, n_dram, slot_dram, x3_dram, y_dram, raw):
    with ExitStack() as ctx:
        sb = lambda *a: ctx.enter_context(nc.sbuf_tensor(*a))
        sem = lambda n: ctx.enter_context(nc.semaphore(n))
        ident, banks, w, tiles, chunk_loaded, w_h_ready, w_l_ready = (
            sh.ident, sh.banks, sh.w, sh.tiles, sh.chunk_loaded, sh.w_h_ready, sh.w_l_ready)
        gT = [sb("gT_h", [P, 2, D], F32R), sb("gT_l", [P, 2, D], F32R)]
        idx, xg, idx_loaded, xg_loaded = sh.idx, sh.xg, sh.idx_loaded, sh.xg_loaded
        y_sb = sh.at("y_sb", STAGE + 8 * D, [P, 2, D])
        t_ps, y_ps = banks[0:2], [banks[2:4], banks[4:6]]

        y_stored = sem("y_stored")
        gT_done, gT_h_ready, gT_l_ready = sem("gT_done"), sem("gT_h_ready"), sem("gT_l_ready")
        y_done, y0_copied, y1_copied = sem("y_done"), sem("y0_copied"), sem("y1_copied")
        passed = sem("passed3")

        def entry(eng, i, what, most):
            return eng.value_load(tiles[0:1, what, bass.ds(i, 1)], min_val=0, max_val=most)

        def steps(eng, step, unused=None):
            def step_if_used(i, par):
                if known(i) and i < E:
                    step(i, par)
                    return
                used = entry(eng, i, 3, 1)
                with eng.If(used > 0):
                    step(i, par)
                if unused:
                    with eng.If(used < 1):
                        unused(i, par)
            pipelined(eng, MT, step_if_used, head=3, tail=2)

        block = ctx.enter_context(nc.Block())

        @block.sync
        def _(sp):
            def load_chunk(e, c):
                sp.dma_start(raw[:, c, :], expert_w[bass.ds(e, 1), c * P:(c + 1) * P, :].rearrange("o p n -> p (o n)")).then_inc(chunk_loaded[c], 16)
            sp.wait_ge(xg_loaded, 32)
            for c in range(KC):
                load_chunk(1, c)
            with sp.Fori(2, E) as e:
                for c in range(KC):
                    sp.wait_ge(w_l_ready, KC * e - KC + c + 1)
                    load_chunk(e, c)
            for c in range(KC):
                sp.wait_ge(w_l_ready, KC * (E - 1) + c + 1)
                sp.dma_start(raw[:, c, :], x3_dram[c * P:(c + 1) * P, :]).then_inc(sh.x3_loaded, 16)

        @block.gpsimd
        def _(pool):
            def first_row(i):
                e = entry(pool, i, 0, E - 1)
                j = entry(pool, i, 1, COLS - E)
                return pool.snap(e * (B * SQ) + j * P, min_val=0, max_val=ROWS - P)

            def load_idx(i, par):
                pool.dma_start(idx[:, par:par + 1], slot_dram[bass.ds(first_row(i), P), :]).then_inc(idx_loaded, 16)

            def gather(i, par):
                wait_apart(pool, idx_loaded, 16 * i + 16, passed)
                pool.indirect_dma_start(xg[:, par, :], None, n_dram, bass.IndirectOffsetOnAxis(ap=idx[:, par:par + 1], axis=0)).then_inc(xg_loaded, 16)

            load_idx(1, 1)
            pool.wait_ge(xg_loaded, 16)
            gather(1, 1)
            load_idx(2, 0)

            def step(i, par):
                if known(i) and i == 0:
                    pool.wait_ge(xg_loaded, 32)
                pool.wait_ge(gT_done, 2 * i + 2)
                gather(i + 2, par)
                pool.wait_ge(xg_loaded, 16 * i + 48)
                load_idx(i + 3, 1 - par)
                pool.wait_ge(y0_copied, i + 1)
                pool.wait_ge(y1_copied, i + 1)
                if not known(i) or i >= 1:
                    pool.wait_ge(y_stored, 16 * i)
                store(i, par)

            def store(i, par):
                pool.dma_start(y_dram[bass.ds(i * P, P), :], y_sb[:, par, :]).then_inc(y_stored, 16)

            steps(pool, step, unused=store)
            used = pool.value_load(tiles[0:1, 4, 0:1], min_val=E, max_val=MT)
            pool.wait_ge(idx_loaded, used * 16 + 48)
            pool.wait_ge(y_stored, 16 * MT)

        @block.scalar
        def _(act):
            def rows_high(i, par):
                if not known(i) or i >= 2:
                    act.wait_ge(y_done, 2 * i - 2)
                for h in range(2):
                    act.wait_ge(gT_done, 2 * i + h + 1)
                    act.activation(gT[0][:, par, h * 512:(h + 1) * 512], t_ps[h][:, :], ACT.Copy).then_inc(gT_h_ready, 1)

            def split_high(e, slot):
                for c in range(KC):
                    act.wait_ge(chunk_loaded[c], 16 * e + 48)
                    act.activation(w[0][:, bass.ds(slot + c * D, D)], raw[:, c, :], ACT.Copy).then_inc(w_h_ready, 1)
            rows_high(0, 0)

            def step(i, par):
                rows_high(i + 1, 1 - par)
                flag = entry(act, i, 2, 1)
                e = entry(act, i, 0, E - 1)
                with act.If(flag > 0):
                    if not known(i) or i >= 1:
                        act.wait_ge(y_done, 2 * i)
                    split_high(e + 1, (e + 1) % 2 * SLOT)
                if not known(i) or i >= 2:
                    act.wait_ge(y_stored, 16 * i - 16)
                act.wait_ge(y_done, 2 * i + 1)
                act.activation(y_sb[:, par, 0:512], y_ps[par][0][:, :], ACT.Copy).then_inc(y0_copied, 1)
            steps(act, step)

        @block.vector
        def _(dve):
            def rows_low(i, par):
                for h in range(2):
                    dve.wait_ge(gT_h_ready, 2 * i + h + 1)
                    dve.tensor_tensor(gT[1][:, par, h * 512:(h + 1) * 512], t_ps[h][:, :],
                                      gT[0][:, par, h * 512:(h + 1) * 512].bitcast(F32), ALU.subtract).then_inc(gT_l_ready, 1)

            def split_low(e, slot):
                for c in range(KC):
                    dve.wait_ge(w_h_ready, KC * e + c + 1)
                    dve.tensor_tensor(w[1][:, bass.ds(slot + c * D, D)], raw[:, c, :],
                                      w[0][:, bass.ds(slot + c * D, D)].bitcast(F32), ALU.subtract).then_inc(w_l_ready, 1)
            rows_low(0, 0)

            def step(i, par):
                rows_low(i + 1, 1 - par)
                flag = entry(dve, i, 2, 1)
                e = entry(dve, i, 0, E - 1)
                with dve.If(flag > 0):
                    split_low(e + 1, (e + 1) % 2 * SLOT)
                if not known(i) or i >= 2:
                    dve.wait_ge(y_stored, 16 * i - 16)
                dve.wait_ge(y_done, 2 * i + 2)
                dve.tensor_copy(y_sb[:, par, 512:D], y_ps[par][1][:, :]).then_inc(y1_copied, 1)
            steps(dve, step)

        @block.tensor
        def _(pe):
            def turn(i, par):
                pe.wait_ge(xg_loaded, 16 * i + 16)
                for k in range(KC):
                    if k % 4 == 0 and (not known(i) or i >= 1):
                        pe.wait_ge(gT_l_ready, 2 * i - 1 + k // 4)
                    o = pe.transpose(t_ps[k // 4][:, k % 4 * P:(k % 4 + 1) * P], xg[:, par, k * P:(k + 1) * P], ident[:, :])
                    if k % 4 == 3:
                        o.then_inc(gT_done, 1)
            turn(0, 0)

            def step(i, par):
                e = entry(pe, i, 0, E - 1)
                slot = pe.snap(e % 2 * SLOT, min_val=0, max_val=SLOT)
                pe.wait_ge(w_l_ready, KC * e + KC)
                pe.wait_ge(gT_l_ready, 2 * i + 2)
                if not known(i) or i >= 2:
                    pe.wait_ge(y0_copied, i - 1)
                    pe.wait_ge(y1_copied, i - 1)
                for unit in range(KC):
                    h = unit // 4
                    if unit == 4:
                        turn(i + 1, 1 - par)
                    for k in range(unit % 4 * 2, unit % 4 * 2 + 2):
                        for n, (a, b) in enumerate(PASSES):
                            o = pe.matmul(y_ps[par][h][:, :], gT[a][:, par, k * P:(k + 1) * P],
                                          w[b][:, bass.ds(slot + (k * D + h * 512), 512)],
                                          start=(k == 0 and n == 0), stop=(k == KC - 1 and n == 2))
                    if unit % 4 == 3:
                        o.then_inc(y_done, 1)
            steps(pe, step)


def combine(nc, sh, y_dram, out, raw):
    assert KC == NT
    with ExitStack() as ctx:
        sem = lambda n: ctx.enter_context(nc.semaphore(n))
        x3, y_pos, wts = raw, sh.y_pos, sh.wts
        yy = sh.at("yy", HIGH0, [P, 2 * NT, D])
        y_loaded = [sem(f"y_loaded{t}") for t in range(NT)]
        half_added, added, stored = sem("half_added"), sem("added"), sem("stored")
        block = ctx.enter_context(nc.Block())

        @block.gpsimd
        def _(pool):
            for t in range(NT):
                for k in range(2):
                    pool.indirect_dma_start(yy[:, 2 * t + k, :], None, y_dram, bass.IndirectOffsetOnAxis(
                        ap=y_pos[:, 2 * t + k:2 * t + k + 1], axis=0)).then_inc(y_loaded[t], 16)

        @block.vector
        def _(dve):
            dve.wait_ge(sh.x3_loaded, 16 * NT)
            for t in range(NT):
                dve.wait_ge(y_loaded[t], 32)
                for k in range(2):
                    if k == 1:
                        dve.wait_ge(half_added, t + 1)
                    dve.scalar_tensor_tensor(out=x3[:, t, :], in0=yy[:, 2 * t + k, :], scalar=wts[:, 2 * t + k:2 * t + k + 1],
                                             in1=x3[:, t, :], op0=ALU.mult, op1=ALU.add).then_inc((half_added, added)[k], 1)

        @block.scalar
        def _(act):
            for t in range(NT):
                act.wait_ge(added, t + 1)
                act.dma_start(out[t * P:(t + 1) * P, :], x3[:, t, :]).then_inc(stored, 16)
            act.wait_ge(stored, 16 * NT)


def program(nc, x, context, wq, wk, wv, wo, eta, gate, expert_w, out):
    scratch = lambda name, shape, dt: nc.dram_tensor(name, shape, dt, kind="Internal").ap()
    q_dram = scratch("q_scratch", [2, NT, P, D], F32)
    k_dram = scratch("k_scratch", [2, 2, P, 2 * SKP], F32)
    vlast_dram = scratch("vlast_scratch", [B, NG, KV], F32)
    x3_dram = scratch("x3_scratch", [B * SQ, D], F32)
    n_dram = scratch("n_scratch", [B * SQ, D], F32)
    slot_dram = scratch("slot_scratch", [ROWS, 1], I32)
    y_dram = scratch("y_scratch", [MT * P, D], F32)
    with ExitStack() as ctx:
        sh = Shared(nc, ctx)
        with nc.sbuf_tensor("cl", [B, D], F32) as cl:
            queries(nc, sh, x, wq, wk, wv, context, q_dram, cl)
            cross_attention(nc, sh, context, wo, q_dram, k_dram, vlast_dram, cl)
        mixing(nc, sh, x, eta, gate, expert_w, x3_dram, n_dram, slot_dram)
        with nc.sbuf_tensor("raw", [P, KC, D], F32) as raw:
            experts(nc, sh, expert_w, n_dram, slot_dram, x3_dram, y_dram, raw)
            combine(nc, sh, y_dram, out, raw)


def kernel(**inputs):
    import numpy as np
    import concourse.bacc as bacc
    from concourse.bass_utils import run_bass_kernel_spmd as run

    wq = inputs["L0_xattn_Wq"]
    wo = inputs["L0_xattn_Wo"]
    arrays = {
        "x": np.asarray(inputs["x"]).reshape(B * SQ, D),
        "context": np.asarray(inputs["ctx_4096"]),
        "wq": np.ascontiguousarray(np.asarray(wq).reshape(D, 2, 4, REP, DH).transpose(0, 1, 3, 2, 4).reshape(D, D)),
        "wk": np.asarray(inputs["L0_xattn_Wk"]),
        "wv": np.asarray(inputs["L0_xattn_Wv"]),
        "wo": np.ascontiguousarray(np.asarray(wo).reshape(2, 4, REP, DH, D).transpose(0, 2, 1, 3, 4).reshape(D, D)),
        "eta": np.asarray(inputs["L0_attn_eta"]),
        "gate": np.asarray(inputs["L0_ffn_gate_w"]),
        "expert_w": np.asarray(inputs["L0_ffn_expert_w"]),
    }
    nc = bacc.Bacc("TRN2", target_bir_lowering=False, num_devices=1)
    args = [nc.dram_tensor(f"in_{k}", a.shape, mybir.dt.from_np(a.dtype), kind="ExternalInput").ap() for k, a in arrays.items()]
    out = nc.dram_tensor("out_x", (B * SQ, D), F32, kind="ExternalOutput").ap()
    program(nc, *args, out)
    r = run(nc, [{f"in_{k}": a for k, a in arrays.items()}], core_ids=[0])
    return r.results[0]["out_x"].reshape(B, SQ, D)
```

```python
from contextlib import ExitStack

import concourse.bass as bass
from concourse import mybir

ALU = mybir.AluOpType
ACT = mybir.ActivationFunctionType
AXX = mybir.AxisListType.X
F32 = mybir.dt.float32
F32R = mybir.dt.float32r
U32 = mybir.dt.uint32
I32 = mybir.dt.int32

P = 128
B = 32
SQ = 32
SK = 257
D = 1024
KC = D // P
NH, NG, DH = 32, 8, 32
REP = NH // NG
KV = NG * DH
NT = B * SQ // P
BT = P // SQ
SCALE = DH ** -0.5
EPS = 1e-5
E = 8
SKP = SK + 1
PASSES = ((0, 0), (0, 1), (1, 0))


SLOT = KC * D
SLOT_BYTES = 4 * SLOT
HIGH0, HIGH1, LOW0, LOW1, STAGE = (i * SLOT_BYTES for i in range(5))


class Shared:

    def __init__(self, nc, ctx):
        sb = lambda *a: ctx.enter_context(nc.sbuf_tensor(*a))
        sem = lambda n: ctx.enter_context(nc.semaphore(n))
        self.ident = sb("ident", [P, P], F32)
        base = nc.sbuf_base
        sb("shared_map", [P, 4 * SLOT + 4 * D], F32)
        self.at = lambda name, offset, shape, dtype=F32: nc.alloc_sbuf_tensor_at(name, shape, dtype, offset=base + offset)
        self.wkv = [self.at("wkv_" + part, HIGH1 + i * SLOT_BYTES // 2, [P, KC, 2 * KV], F32R) for i, part in enumerate("hl")]
        self.cx = self.at("cx", STAGE, [P, 2, 2, D])
        self.oT = self.at("oT", HIGH0, [P, KC, B * SQ])
        self.wo = [self.at("wo_h", HIGH1, [P, KC, D], F32R), self.at("wo_l", LOW1, [P, KC, D], F32R)]
        self.w = [self.at("w_h", HIGH0, [P, 2 * SLOT], F32R), self.at("w_l", LOW0, [P, 2 * SLOT], F32R)]
        self.tiles = sb("tiles", [1, 7, COLS], I32)
        self.first_raw = [self.at("expert0_raw", LOW0, [P, KC, D]), self.at("expert1_raw", LOW1, [P, KC, D])]
        self.banks = [ctx.enter_context(nc.psum_tensor(f"bank{i}", [P, 512], F32)) for i in range(8)]
        self.chunk_loaded = [sem(f"chunk_loaded{c}") for c in range(KC)]
        self.q_stored = [sem("q_stored0"), sem("q_stored1")]
        self.cl_loaded, self.cx_loaded = sem("cl_loaded"), [sem("cx_loaded0"), sem("cx_loaded1")]
        self.w_h_ready, self.w_l_ready = sem("w_h_ready"), sem("w_l_ready")
        self.idx = sb("idx", [P, 2, 2], I32)
        self.xg = self.at("xg", STAGE, [P, 2, D])
        self.idx_loaded, self.xg_loaded = sem("idx_loaded"), sem("xg_loaded")


def pipelined(eng, n, step, head=1, tail=1):
    assert head % 2 == 1
    pairs = (n - head - tail) // 2
    for t in range(head):
        step(t, t % 2)
    with eng.Fori(0, pairs) as i:
        step(2 * i + head, head % 2)
        step(2 * i + head + 1, (head + 1) % 2)
    for t in range(head + 2 * pairs, n):
        step(t, t % 2)


def wait_apart(eng, sem, value, passed):
    eng.wait_ge(sem, value)
    if not known(value):
        eng.sem_inc(passed, 1)


def known(t):
    return isinstance(t, int)


class Norm:

    def __init__(self, nc, ctx, name):
        self.stats = ctx.enter_context(nc.sbuf_tensor(name + "_stats", [P, 2, 6], F32))
        self.mean_var = ctx.enter_context(nc.sbuf_tensor(name + "_mean_var", [P, 2], F32))
        self.rstd = ctx.enter_context(nc.sbuf_tensor(name + "_rstd", [P, 1], F32))
        self.var_eps = ctx.enter_context(nc.sbuf_tensor(name + "_var_eps", [P, 1], F32))
        self.minus_half = ctx.enter_context(nc.sbuf_tensor(name + "_minus_half", [P, 1], F32))
        self.eps_added = ctx.enter_context(nc.semaphore(name + "_eps_added"))
        self.passed = ctx.enter_context(nc.semaphore(name + "_passed"))
        self.stats_ready = ctx.enter_context(nc.semaphore(name + "_stats_ready"))
        self.var_ready = ctx.enter_context(nc.semaphore(name + "_var_ready"))
        self.rstd_ready = ctx.enter_context(nc.semaphore(name + "_rstd_ready"))

    def on_vector(self, dve, t, out, src):
        for h in range(2):
            dve.bn_stats(self.stats[:, h, :], src[:, h * 512:(h + 1) * 512]).then_inc(self.stats_ready, 1)
        wait_apart(dve, self.stats_ready, 2 * t + 2, self.passed)
        dve.bn_aggr(self.mean_var[:, :], self.stats[:, :, :].rearrange("p a b -> p (a b)")).then_inc(self.var_ready, 1)
        dve.wait_ge(self.rstd_ready, t + 1)
        return dve.tensor_scalar(out, src, self.mean_var[:, 0:1], self.rstd[:, 0:1], ALU.subtract, ALU.mult)

    def start_gpsimd(self, pool):
        pool.memset(self.minus_half[:, :], -0.5).then_inc(self.eps_added, 1)
        pool.wait_ge(self.eps_added, 1)

    def on_gpsimd(self, pool, t):
        wait_apart(pool, self.var_ready, t + 1, self.passed)
        pool.tensor_scalar(self.var_eps[:, :], self.mean_var[:, 1:2], EPS, None, ALU.add).then_inc(self.eps_added, 1)
        pool.wait_ge(self.eps_added, t + 2)
        pool.tensor_tensor(self.rstd[:, :], self.var_eps[:, :], self.minus_half[:, :], ALU.pow).then_inc(self.rstd_ready, 1)


WKV_SPLIT = {NT - 3: range(KC // 2), NT - 2: range(KC // 2, KC)}


def queries(nc, sh, x, wq, wk, wv, context, q_dram, cl):
    with ExitStack() as ctx:
        sb = lambda *a: ctx.enter_context(nc.sbuf_tensor(*a))
        sem = lambda n: ctx.enter_context(nc.semaphore(n))
        ident, banks, wkv, cx, chunk_loaded, cx_loaded = sh.ident, sh.banks, sh.wkv, sh.cx, sh.chunk_loaded, sh.cx_loaded
        q_stored = sh.q_stored
        wkv_raw = sh.at("wkv_raw", STAGE, [P, KC, 2 * KV])
        wq_raw = sh.at("wq_raw", HIGH0, [P, KC, D])
        wq_s = [sh.at("wq_h", LOW0, [P, KC, D], F32R), sh.at("wq_l", LOW1, [P, KC, D], F32R)]
        x_in = sb("x_in", [P, 2, D], F32)
        xn = sb("xn", [P, 2, D], F32)
        xT = [sb("xT_h", [P, 2, D], F32R), sb("xT_l", [P, 2, D], F32R)]
        q_sb = sb("q_sb", [P, 2, D], F32)
        qT = [sb("qT_h", [P, 2, D], F32R), sb("qT_l", [P, 2, D], F32R)]
        norm = Norm(nc, ctx, "norm1")
        xT_ps = banks[0:2]
        q_ps = [banks[2:4], banks[4:6]]
        qT_ps = banks[6:8]

        x_loaded = [sem("x_loaded0"), sem("x_loaded1")]
        wkv_loaded = [sem("wk_loaded"), sem("wv_loaded")]
        ident_zero, ident_ready = sem("ident_zero"), sem("ident_ready")
        wq_h_ready, wq_ready = sem("wq_h_ready"), sem("wq_ready")
        wkv_h_ready, wkv_l_ready = sem("wkv_h_ready"), sem("wkv_l_ready")
        xn_ready, xT_done, xT_h_ready, xT_l_ready = sem("xn_ready"), sem("xT_done"), sem("xT_h_ready"), sem("xT_l_ready")
        q_done, q_copied, qT_done, qT_h_ready, qT_l_ready = (
            sem("q_done"), sem("q_copied"), sem("qT_done"), sem("qT_h_ready"), sem("qT_l_ready"))

        by_batch = lambda ap: ap.rearrange("p (b m q) -> p m b q", b=BT, q=SQ)

        block = ctx.enter_context(nc.Block())

        @block.sync
        def _(sp):
            def load_x(t, par):
                sp.dma_start(x_in[:, par, :], x[bass.ts(t, P), :]).then_inc(x_loaded[par], 16)
            load_x(0, 0)
            for c in range(KC):
                sp.dma_start(wq_raw[:, c, :], wq[c * P:(c + 1) * P, :]).then_inc(chunk_loaded[c], 16)
                if c == 0:
                    load_x(1, 1)
            for n, w in enumerate((wk, wv)):
                sp.dma_start(wkv_raw[:, :, n * KV:(n + 1) * KV], w.rearrange("(c p) n -> p c n", p=P)).then_inc(wkv_loaded[n], 16)

            def step(t, par):
                if not known(t) or t + 2 < NT:
                    sp.wait_ge(xn_ready, t + 1)
                    load_x(t + 2, par)
            pipelined(sp, NT, step, tail=3)
            sp.dma_start(cl[:, :], context[:, 2 * P, :]).then_inc(sh.cl_loaded, 16)
            sp.wait_ge(wkv_l_ready, KC)
            for b in range(2):
                sp.dma_start(context_tile(cx, b), context_rows(context, b)).then_inc(cx_loaded[b], 16)

        @block.gpsimd
        def _(pool):
            pool.memset(ident[:, :], 0.0).then_inc(ident_zero, 1)
            pool.wait_ge(ident_zero, 1)
            pool.affine_select(out=ident[:, :], in_=ident[:, :], compare_op=ALU.not_equal, fill=1.0, base=0,
                               pattern=[[-1, P]], channel_multiplier=1).then_inc(ident_ready, 1)
            norm.start_gpsimd(pool)
            pipelined(pool, NT, lambda t, par: norm.on_gpsimd(pool, t))

        @block.scalar
        def _(act):
            def xT_high(t, par):
                if not known(t) or t >= 2:
                    act.wait_ge(q_done, 2 * t - 2)
                for h in range(2):
                    act.wait_ge(xT_done, 2 * t + h + 1)
                    act.activation(xT[0][:, par, h * 512:(h + 1) * 512], xT_ps[h][:, :], ACT.Copy).then_inc(xT_h_ready, 1)
            xT_high(0, 0)
            for c in range(KC):
                act.wait_ge(chunk_loaded[c], 16)
                act.activation(wq_s[0][:, c, :], wq_raw[:, c, :], ACT.Copy).then_inc(wq_h_ready, 1)

            def step(t, par):
                if not known(t) or t + 1 < NT:
                    xT_high(t + 1, 1 - par)
                if known(t) and t in WKV_SPLIT:
                    for n in range(2):
                        act.wait_ge(wkv_loaded[n], 16)
                    for c in WKV_SPLIT[t]:
                        act.activation(wkv[0][:, c, :], wkv_raw[:, c, :], ACT.Copy).then_inc(wkv_h_ready, 1)
                for h in range(2):
                    act.wait_ge(q_done, 2 * t + h + 1)
                    if h == 0 and (not known(t) or t >= 2):
                        act.wait_ge(qT_done, 2 * t - 2)
                    act.activation(q_sb[:, par, h * 512:(h + 1) * 512], q_ps[par][h][:, :], ACT.Copy).then_inc(q_copied, 1)
                if not known(t) or t >= 1:
                    qT_high(t - 1, 1 - par)
                if not known(t) or t >= 2:
                    store_q(t - 2, par)

            def store_q(t, par):
                act.wait_ge(qT_l_ready, t + 1)
                for part in range(2):
                    act.dma_start(q_dram[part, bass.ds(t, 1)].rearrange("a p n -> p (a n)"),
                                  qT[part][:, par, :].bitcast(F32)).then_inc(q_stored[par], 16)

            def qT_high(t, par):
                if not known(t) or t >= 2:
                    act.wait_ge(q_stored[par], (t - par) * 16)
                for h in range(2):
                    act.wait_ge(qT_done, 2 * t + h + 1)
                    o = act.activation(by_batch(qT[0][:, par, :])[:, 4 * h:4 * h + 4],
                                       qT_ps[h][:, :].rearrange("p (m b q) -> p m b q", m=4, q=SQ), ACT.Copy, scale=SCALE)
                    if h == 1:
                        o.then_inc(qT_h_ready, 1)
            pipelined(act, NT, step, head=3, tail=3)
            store_q(6, 0)
            qT_high(7, 1)
            store_q(7, 1)

        @block.vector
        def _(dve):
            def normalize(t, par):
                dve.wait_ge(x_loaded[par], (t - par) * 8 + 16)
                if not known(t) or t >= 2:
                    dve.wait_ge(xT_done, 2 * t - 2)
                norm.on_vector(dve, t, xn[:, par, :], x_in[:, par, :]).then_inc(xn_ready, 1)

            def xT_low(t, par):
                for h in range(2):
                    dve.wait_ge(xT_h_ready, 2 * t + h + 1)
                    dve.tensor_tensor(xT[1][:, par, h * 512:(h + 1) * 512], xT_ps[h][:, :],
                                      xT[0][:, par, h * 512:(h + 1) * 512].bitcast(F32), ALU.subtract).then_inc(xT_l_ready, 1)

            def qT_low(t, par):
                if not known(t) or t >= 2:
                    dve.wait_ge(q_stored[par], (t - par) * 16)
                dve.wait_ge(qT_h_ready, t + 1)
                for h in range(2):
                    for m in range(4):
                        o = dve.scalar_tensor_tensor(out=by_batch(qT[1][:, par, :])[:, 4 * h + m],
                                                     in0=qT_ps[h][:, m * P:(m + 1) * P].rearrange("p (b q) -> p b q", q=SQ),
                                                     scalar=SCALE, in1=by_batch(qT[0][:, par, :])[:, 4 * h + m].bitcast(F32),
                                                     op0=ALU.mult, op1=ALU.subtract)
                o.then_inc(qT_l_ready, 1)

            normalize(0, 0)
            normalize(1, 1)
            xT_low(0, 0)
            for c in range(KC):
                dve.wait_ge(wq_h_ready, c + 1)
                dve.tensor_tensor(wq_s[1][:, c, :], wq_raw[:, c, :], wq_s[0][:, c, :].bitcast(F32), ALU.subtract).then_inc(wq_ready, 1)

            def step(t, par):
                if not known(t) or t + 1 < NT:
                    xT_low(t + 1, 1 - par)
                if not known(t) or t + 2 < NT:
                    normalize(t + 2, par)
                if known(t) and t in WKV_SPLIT:
                    for c in WKV_SPLIT[t]:
                        dve.wait_ge(wkv_h_ready, c + 1)
                        dve.tensor_tensor(wkv[1][:, c, :], wkv_raw[:, c, :], wkv[0][:, c, :].bitcast(F32),
                                          ALU.subtract).then_inc(wkv_l_ready, 1)
                if not known(t) or t >= 1:
                    qT_low(t - 1, 1 - par)
            pipelined(dve, NT, step, head=3, tail=3)
            qT_low(7, 1)

        @block.tensor
        def _(pe):
            def transpose_x(t, par):
                pe.wait_ge(xn_ready, t + 1)
                for k in range(KC):
                    if k % 4 == 0 and (not known(t) or t >= 1):
                        pe.wait_ge(xT_l_ready, 2 * t - 1 + k // 4)
                    o = pe.transpose(xT_ps[k // 4][:, k % 4 * P:(k % 4 + 1) * P], xn[:, par, k * P:(k + 1) * P], ident[:, :])
                    if k % 4 == 3:
                        o.then_inc(xT_done, 1)

            def transpose_q(t, par):
                pe.wait_ge(q_copied, 2 * t + 2)
                if not known(t) or t >= 1:
                    pe.wait_ge(qT_l_ready, t)
                for k in range(KC):
                    o = pe.transpose(qT_ps[k // 4][:, k % 4 * P:(k % 4 + 1) * P], q_sb[:, par, k * P:(k + 1) * P], ident[:, :])
                    if k % 4 == 3:
                        o.then_inc(qT_done, 1)

            pe.wait_ge(ident_ready, 1)
            transpose_x(0, 0)

            def step(t, par):
                pe.wait_ge(xT_l_ready, 2 * t + 2)
                if not known(t) or t >= 2:
                    pe.wait_ge(q_copied, 2 * t - 2)
                for k in range(KC):
                    if known(t) and t == 0:
                        pe.wait_ge(wq_ready, k + 1)
                    if k == 4 and (not known(t) or t + 1 < NT):
                        transpose_x(t + 1, 1 - par)
                    if k == 6 and (not known(t) or t >= 1):
                        transpose_q(t - 1, 1 - par)
                    for h in range(2):
                        for n, (a, b) in enumerate(PASSES):
                            o = pe.matmul(q_ps[par][h][:, :], xT[a][:, par, k * P:(k + 1) * P],
                                          wq_s[b][:, k, h * 512:(h + 1) * 512],
                                          start=(k == 0 and n == 0), stop=(k == KC - 1 and n == 2))
                        if k == KC - 1:
                            o.then_inc(q_done, 1)
            pipelined(pe, NT, step, head=3)
            transpose_q(7, 1)


def context_tile(cx, par):
    return cx[:, par, :, :].rearrange("p a n -> p (a n)")


def context_rows(context, b):
    return context[bass.ds(b, 1), 0:2 * P, :].rearrange("o (p a) n -> p (o a n)", a=2)


def slot_head(s):
    return s // 4, s % 4


def cat_index(s):
    j, g = slot_head(s)
    return 2 * g + j


def slot_cols(s):
    j, g = slot_head(s)
    return slice((4 * j + g) * DH, (4 * j + g + 1) * DH)


def over_batches(eng, step):
    pipelined(eng, B + 2, step, head=3, tail=5)


class Stages:

    def __init__(self, b):
        self.project = not known(b) or b < B
        self.next = not known(b) or b + 1 < B
        self.heads = not known(b) or 1 <= b <= B
        self.rest = not known(b) or b >= 2


def wo_chunk(b, s, late):
    c = (b - B) * NG + s - 2 - late if known(b) else -1
    return [c] if 0 <= c < KC else []


TURNED_BY_SCALAR = (1, 4, 6)


def cross_attention(nc, sh, context, wo, q_dram, k_dram, vlast_dram, cl):
    with ExitStack() as ctx:
        sb = lambda *a: ctx.enter_context(nc.sbuf_tensor(*a))
        sem = lambda n: ctx.enter_context(nc.semaphore(n))
        ident, banks, wkv, cx, oT, wo_s, chunk_loaded, cx_loaded = (
            sh.ident, sh.banks, sh.wkv, sh.cx, sh.oT, sh.wo, sh.chunk_loaded, sh.cx_loaded)
        half = SLOT_BYTES // 2
        cT = [sh.at("cT_" + part, LOW0 + i * half, [P, 2, KC, 2 * P], F32R) for i, part in enumerate("hl")]
        kT = [sh.at("kT_" + part, LOW1 + i * half, [P, 2, 2, SKP], F32R) for i, part in enumerate("hl")]
        clT = [sh.at("clT_" + part, LOW1 + i * half + 16 * SKP, [P, KC, P], F32R) for i, part in enumerate("hl")]
        zeros = sh.at("zeros", LOW1 + 16 * SKP + 4 * KC * P, [P, 512])
        vl_sb = sh.at("vl_sb", LOW1 + half + 16 * SKP + 4 * KC * P, [B, KV])
        kl = [sh.at("kl_" + part, LOW1 + i * half + 16 * SKP + 4 * KC * P + 4 * 512, [P, 2, B], F32R) for i, part in enumerate("hl")]
        assert 16 * SKP + 4 * KC * P + 4 * 512 + 8 * B <= half
        wo_raw = [sh.at("wo_raw0", STAGE, [P, KC // 2, D]), sh.at("wo_raw1", LOW0, [P, KC // 2, D])]
        wo_loaded = lambda c: wo_raw[c // (KC // 2)][:, c % (KC // 2), :]
        kcat = sb("kcat", [P, 2, 4 * 2, SKP], F32R)
        qcat = sb("qcat", [P, 2, NG, REP * SQ], F32R)
        v_sb = sb("v_sb", [P, 2, 2, KV], F32)
        vl = sb("vl", [NG, 2, KV], F32)
        prob = sb("prob", [P, 2, NG, SKP], F32)
        pT = sb("pT", [P, NG, 2 * P], F32)
        rsums = sb("rsums", [P, NG], F32)
        plT = sb("plT", [NG, P], F32)
        nmax = sb("nmax", [P, 2, NG], F32)
        sums = sb("sums", [P, 2, NG], F32)
        cT_ps, k_ps, v_ps, s_ps = banks[0:2], banks[2], banks[3], banks[4:6]
        turn_ps = banks[6][:, 0:256]
        o_ps = banks[7]

        kcat_loaded = [sem("kcat_loaded0"), sem("kcat_loaded1")]
        qcat_loaded = [sem("qcat_loaded0"), sem("qcat_loaded1")]
        vl_loaded = [sem("vl_loaded0"), sem("vl_loaded1")]
        wo_h_ready, wo_l_ready = sem("wo_h_ready"), sem("wo_l_ready")
        zeros_ready, pads_ready, vl_zeroed, vl_placed = (
            sem("zeros_ready"), sem("pads_ready"), sem("vl_zeroed"), sem("vl_placed"))
        clT_done, clT_h_ready, clT_l_ready, kvl_done, kl_h_ready, kl_l_ready, vl_copied = (
            sem("clT_done"), sem("clT_h_ready"), sem("clT_l_ready"), sem("kvl_done"), sem("kl_h_ready"),
            sem("kl_l_ready"), sem("vl_copied"))
        cT_done, cT_h_ready, cT_l_ready = sem("cT_done"), sem("cT_h_ready"), sem("cT_l_ready")
        k_done, kT_h_ready, kT_l_ready, klast_ready = sem("k_done"), sem("kT_h_ready"), sem("kT_l_ready"), sem("klast_ready")
        v_done, v_copied = sem("v_done"), sem("v_copied")
        s_done, max_done, exp_done = sem("s_done"), sem("max_done"), sem("exp_done")
        k_stored = [sem("k_h_stored"), sem("k_l_stored")]
        passed = sem("passed1")
        turned, turn_copied = sem("turned"), sem("turn_copied")
        last_turned, last_copied = sem("last_turned"), sem("last_copied")
        rsum_ready, prob_ready, pv_done, o_done, o_copied = sem("rsum_ready"), sem("prob_ready"), sem("pv_done"), sem("o_done"), sem("o_copied")

        def copy_turned(eng, copy, a, i):
            if not known(a) or a >= 1:
                eng.wait_ge(pv_done, 2 * (a - 1) + i // 4 + 1)
            eng.wait_ge(turned, NG * a + i + 1)
            copy(pT[:, i, :], turn_ps).then_inc(turn_copied, 1)

        def queries_stored(eng):
            for par in range(2):
                eng.wait_ge(sh.q_stored[par], 32 * NT // 2)

        block = ctx.enter_context(nc.Block())

        @block.sync
        def _(sp):
            sp.wait_ge(zeros_ready, 1)
            sp.dma_start(vlast_dram.rearrange("b s n -> (b s n)").rearrange("(p n) -> p n", p=P), zeros[:, :]).then_inc(vl_zeroed, 16)
            sp.wait_ge(vl_zeroed, 16)
            sp.wait_ge(vl_copied, 1)
            for s in range(NG):
                sp.dma_start(vlast_dram[:, s, slot_cols(s)], vl_sb[:, slot_cols(s)]).then_inc(vl_placed, 16)

            def step(b, par):
                st = Stages(b)
                if not st.project:
                    if b == B:
                        sp.wait_ge(v_done, B)
                        for c in range(KC // 2, KC):
                            load_wo(c)
                    return
                if not known(b) or b >= 2:
                    sp.wait_ge(s_done, NG * (b - 1))
                if not known(b) or b + 2 < B:
                    sp.wait_ge(cT_done, 4 * b + 4)
                    sp.dma_start(context_tile(cx, par), context_rows(context, b + 2)).then_inc(cx_loaded[par], 16)
                for part, ready in enumerate((kT_h_ready, kT_l_ready)):
                    if part == 0:
                        wait_apart(sp, klast_ready, 2 * b + 2, passed)
                    sp.wait_ge(ready, b + 1)
                    sp.dma_start(k_dram[part, par], kT[part][:, par, :, :].rearrange("p j n -> p (j n)").bitcast(F32)).then_inc(k_stored[part], 16)
                for part in range(2):
                    sp.wait_ge(k_stored[part], 16 * b + 16)
                    for c in (part, part + 2):
                        sp.dma_start(kcat[c * DH:(c + 1) * DH, par, :, :].rearrange("d (g j) n -> d g (j n)", g=4).bitcast(F32),
                                     k_dram[part, par].rearrange("(g d) n -> d g n", g=4)).then_inc(kcat_loaded[par], 16)

                if known(b) and b == B - 1:
                    sp.wait_ge(cT_done, 4 * B)
                    for c in range(KC // 2):
                        load_wo(c)

            def load_wo(c):
                sp.dma_start(wo_loaded(c), wo[c * P:(c + 1) * P, :]).then_inc(chunk_loaded[c], 16)

            over_batches(sp, step)

        @block.gpsimd
        def _(pool):
            pool.memset(zeros[:, :], 0.0).then_inc(zeros_ready, 1)
            for part in range(2):
                pool.memset(clT[part][:, :, :].bitcast(F32), 0.0).then_inc(pads_ready, 1)
                pool.memset(kT[part][:, :, :, SK:SKP].bitcast(F32), 0.0).then_inc(pads_ready, 1)
            pool.wait_ge(kl_l_ready, 1)
            pool.wait_ge(vl_placed, 16 * NG)
            queries_stored(pool)

            def q_of_batch(b, part):
                return q_dram[part, bass.ds(b // BT, 1), :, bass.ds((b % BT) * NG * SQ, NG * SQ)].rearrange("o (g d) n -> d (o g) n", g=4)

            def step(b, par):
                st = Stages(b)
                if st.project:
                    if not known(b) or b >= 2:
                        pool.wait_ge(k_stored[0], 16 * b - 16)
                        pool.wait_ge(k_stored[1], 16 * b - 16)
                    for part in range(2):
                        pool.tensor_copy(kT[part][:, par, :, SK - 1:SK], kl[part][:, :, bass.ds(b, 1)].bitcast(F32)).then_inc(klast_ready, 1)
                if st.heads:
                    if not known(b) or b >= 3:
                        pool.wait_ge(o_done, b - 2)
                    pool.dma_start(vl[:, 1 - par, :], vlast_dram[bass.ds(b - 1, 1)].rearrange("o s n -> s (o n)")).then_inc(vl_loaded[1 - par], 16)
                if not st.project:
                    return
                if not known(b) or b >= 2:
                    pool.wait_ge(s_done, NG * (b - 1))
                for c in range(4):
                    pool.dma_start(qcat[c * DH:(c + 1) * DH, par, :, :].rearrange("d (g j) n -> d g (j n)", g=4).bitcast(F32),
                                   q_of_batch(b, c // 2)).then_inc(qcat_loaded[par], 16)
            over_batches(pool, step)

        @block.scalar
        def _(act):
            def context_high(b, par, m):
                if not known(b) or b >= 2:
                    act.wait_ge(v_done, b - 1)
                act.wait_ge(cT_done, 4 * b + m + 1)
                act.activation(cT[0][:, par, 2 * m:2 * m + 2, :].rearrange("p a n -> p (a n)"), cT_ps[m % 2][:, :], ACT.Copy).then_inc(cT_h_ready, 1)

            def copy_v(b, par):
                if not known(b) or b >= 2:
                    act.wait_ge(pv_done, 2 * (b - 1))
                act.wait_ge(v_done, b + 1)
                act.activation(v_sb[:, par, :, :].rearrange("p a n -> p (a n)"), v_ps[:, :], ACT.Copy).then_inc(v_copied, 1)

            def split_wo(c):
                act.wait_ge(v_done, B)
                act.wait_ge(chunk_loaded[c], 32)
                act.activation(wo_s[0][:, c, :], wo_loaded(c), ACT.Copy).then_inc(wo_h_ready, 1)

            act.wait_ge(pads_ready, 4)
            act.wait_ge(clT_done, 1)
            act.activation(clT[0][:, :, 0:B], cT_ps[0][:, 0:KC * B].rearrange("p (k b) -> p k b", b=B), ACT.Copy).then_inc(clT_h_ready, 1)
            act.wait_ge(kvl_done, 2)
            act.activation(kl[0][:, :, :].rearrange("p j b -> p (j b)"), k_ps[:, 0:2 * B], ACT.Copy).then_inc(kl_h_ready, 1)
            act.activation(vl_sb[:, :], v_ps[0:B, 0:KV], ACT.Copy).then_inc(vl_copied, 1)
            for m in range(4):
                context_high(0, 0, m)
            queries_stored(act)

            def step(b, par):
                st = Stages(b)
                for s in range(NG):
                    if st.heads:
                        act.wait_ge(max_done, NG * (b - 1) + s + 1)
                        act.activation(prob[:, 1 - par, s, 0:SK], s_ps[s % 2][:, 0:SK], ACT.Exp, bias=nmax[:, 1 - par, s:s + 1],
                                       accum_out=sums[:, 1 - par, s:s + 1]).then_inc(exp_done, 1)
                    if s == 3 and st.project:
                        if not known(b) or b >= 2:
                            act.wait_ge(k_stored[0], 16 * b - 16)
                        act.wait_ge(k_done, b + 1)
                        act.activation(kT[0][:, par, :, 0:2 * P], k_ps[:, :].rearrange("p (j n) -> p j n", j=2), ACT.Copy).then_inc(kT_h_ready, 1)
                    i = (s - 2) % NG
                    if i in TURNED_BY_SCALAR and (st.rest if s < 2 else st.heads):
                        copy_turned(act, act.copy, b - 2 if s < 2 else b - 1, i)
                    if s == 1 and st.rest:
                        act.wait_ge(last_turned, b - 1)
                        act.activation(plT[:, :], v_ps[0:NG, 0:P], ACT.Copy).then_inc(last_copied, 1)
                    if s == 4 and st.rest:
                        act.wait_ge(o_done, b - 1)
                        act.activation(oT[:, :, bass.ds((b - 2) * SQ, SQ)],
                                       o_ps[:, 0:2 * P].rearrange("p (m q) -> p m q", q=SQ), ACT.Copy).then_inc(o_copied, 1)
                    if s % 2 == 1 and st.next:
                        context_high(b + 1, 1 - par, s // 2)
                    if s == 7 and st.project:
                        copy_v(b, par)
                    for c in wo_chunk(b, s, 0):
                        split_wo(c)
            over_batches(act, step)

        @block.vector
        def _(dve):
            def context_low(b, par, m):
                dve.wait_ge(cT_h_ready, 4 * b + m + 1)
                high = cT[0][:, par, 2 * m:2 * m + 2, :].rearrange("p a n -> p (a n)").bitcast(F32)
                dve.tensor_tensor(cT[1][:, par, 2 * m:2 * m + 2, :].rearrange("p a n -> p (a n)"), cT_ps[m % 2][:, :],
                                  high, ALU.subtract).then_inc(cT_l_ready, 1)

            dve.wait_ge(clT_h_ready, 1)
            dve.tensor_tensor(clT[1][:, :, 0:B], cT_ps[0][:, 0:KC * B].rearrange("p (k b) -> p k b", b=B),
                              clT[0][:, :, 0:B].bitcast(F32), ALU.subtract).then_inc(clT_l_ready, 1)
            dve.wait_ge(kl_h_ready, 1)
            dve.tensor_tensor(kl[1][:, :, :].rearrange("p j b -> p (j b)"), k_ps[:, 0:2 * B],
                              kl[0][:, :, :].rearrange("p j b -> p (j b)").bitcast(F32), ALU.subtract).then_inc(kl_l_ready, 1)
            for m in range(4):
                context_low(0, 0, m)
            queries_stored(dve)

            def normalize(a, ap, i):
                dve.wait_ge(exp_done, NG * a + i + 1)
                dve.reciprocal(rsums[:, i:i + 1], sums[:, ap, i:i + 1]).then_inc(rsum_ready, 1)
                dve.wait_ge(rsum_ready, NG * a + i + 1)
                dve.tensor_scalar(prob[:, ap, i, 0:SK], prob[:, ap, i, 0:SK], rsums[:, i:i + 1], None, ALU.mult).then_inc(prob_ready, 1)

            def step(b, par):
                st = Stages(b)
                for s in range(NG):
                    if st.heads:
                        dve.wait_ge(s_done, NG * (b - 1) + s + 1)
                        dve.reduce_max(nmax[:, 1 - par, s:s + 1], s_ps[s % 2][:, 0:SK], AXX, negate=True).then_inc(max_done, 1)
                    if s == 0 and st.rest:
                        normalize(b - 2, par, NG - 1)
                    if s >= 1 and st.heads:
                        normalize(b - 1, 1 - par, s - 1)
                    i = (s - 2) % NG
                    if i not in TURNED_BY_SCALAR and (st.rest if s < 2 else st.heads):
                        copy_turned(dve, dve.tensor_copy, b - 2 if s < 2 else b - 1, i)
                    if s == 3 and st.project:
                        if not known(b) or b >= 2:
                            dve.wait_ge(k_stored[1], 16 * b - 16)
                        dve.wait_ge(kT_h_ready, b + 1)
                        dve.tensor_tensor(kT[1][:, par, :, 0:2 * P], k_ps[:, :].rearrange("p (j n) -> p j n", j=2),
                                          kT[0][:, par, :, 0:2 * P].bitcast(F32), ALU.subtract).then_inc(kT_l_ready, 1)
                    if s % 2 == 1 and st.next:
                        context_low(b + 1, 1 - par, s // 2)
                    for c in wo_chunk(b, s, 1):
                        if c == 0:
                            for part in range(2):
                                dve.wait_ge(k_stored[part], 16 * B)
                        dve.wait_ge(wo_h_ready, c + 1)
                        dve.tensor_tensor(wo_s[1][:, c, :], wo_loaded(c), wo_s[0][:, c, :].bitcast(F32), ALU.subtract).then_inc(wo_l_ready, 1)
            over_batches(dve, step)

        @block.tensor
        def _(pe):
            def transpose_context(b, par, m):
                if m == 0:
                    pe.wait_ge(cx_loaded[par], 8 * (b - par) + 16)
                if not known(b) or 4 * b + m >= 2:
                    pe.wait_ge(cT_l_ready, 4 * b + m - 1)
                for k in range(2 * m, 2 * m + 2):
                    for a in range(2):
                        n = (k % 2) * 2 + a
                        o = pe.transpose(cT_ps[m % 2][:, n * P:(n + 1) * P], cx[:, par, a, k * P:(k + 1) * P], ident[:, :])
                o.then_inc(cT_done, 1)

            def keys(b, par, s, first):
                j = s // 2
                for k in range(s % 2 * 4 + (0 if first else 2), s % 2 * 4 + (2 if first else 4)):
                    for n, (x, y) in enumerate(PASSES):
                        o = pe.matmul(k_ps[:, j * 256:(j + 1) * 256], wkv[x][:, k, j * P:(j + 1) * P], cT[y][:, par, k, :],
                                      start=(j == 0 and k == 0 and n == 0), stop=(j == 1 and k == KC - 1 and n == 2), skip_group_check=True)
                if s == 3 and not first:
                    o.then_inc(k_done, 1)

            def values(b, par, s, first):
                a = s // 2 - 2
                for k in range(s % 2 * 4 + (0 if first else 2), s % 2 * 4 + (2 if first else 4)):
                    for n, (x, y) in enumerate(PASSES):
                        o = pe.matmul(v_ps[:, a * KV:(a + 1) * KV], cT[x][:, par, k, a * P:(a + 1) * P], wkv[y][:, k, KV:2 * KV],
                                      start=(a == 0 and k == 0 and n == 0), stop=(a == 1 and k == KC - 1 and n == 2), skip_group_check=True)
                if s == 7 and not first:
                    o.then_inc(v_done, 1)

            def project(b, par, s, first):
                st = Stages(b)
                if s < 3 and st.project:
                    keys(b, par, s + 1, first)
                elif s < 7 and st.project:
                    values(b, par, s + 1, first)
                elif s == 7 and st.next:
                    keys(b + 1, 1 - par, 0, first)

            def turn(dst, pieces):
                for n, (rows, src) in enumerate(pieces):
                    o = pe.transpose(dst[0:rows, n * P:(n + 1) * P], src, ident[:, :])
                return o

            def turn_prob(a, ap, i):
                pe.wait_ge(prob_ready, NG * a + i + 1)
                if not known(a) or NG * a + i >= 1:
                    pe.wait_ge(turn_copied, NG * a + i)
                turn(turn_ps, [(P, prob[:, ap, i, c * P:(c + 1) * P]) for c in range(2)]).then_inc(turned, 1)

            def times_values(a, ap, j):
                pe.wait_ge(turn_copied, NG * a + 4 * j + 4)
                if j == 0:
                    pe.wait_ge(v_copied, a + 1)
                    if not known(a) or a >= 1:
                        pe.wait_ge(o_copied, a)
                for c in range(2):
                    for g in range(4):
                        i = 4 * j + g
                        o = pe.matmul(o_ps[g * DH:(g + 1) * DH, j * P:(j + 1) * P], v_sb[:, ap, c, slot_cols(i)], pT[:, i, c * P:(c + 1) * P],
                                      start=(j == 0 and c == 0), stop=False, skip_group_check=True)
                o.then_inc(pv_done, 1)

            pe.wait_ge(sh.cl_loaded, 16)
            for k in range(KC):
                o = pe.transpose(cT_ps[0][:, k * B:(k + 1) * B], cl[:, k * P:(k + 1) * P], ident[0:B, 0:B])
            o.then_inc(clT_done, 1)
            pe.wait_ge(clT_l_ready, 1)
            for j in range(2):
                for k in range(KC):
                    for n, (x, y) in enumerate(PASSES):
                        o = pe.matmul(k_ps[:, j * B:(j + 1) * B], wkv[x][:, k, j * P:(j + 1) * P], clT[y][:, k, 0:B],
                                      start=(j == 0 and k == 0 and n == 0), stop=(j == 1 and k == KC - 1 and n == 2), skip_group_check=True)
            o.then_inc(kvl_done, 1)
            for k in range(KC):
                for n, (x, y) in enumerate(PASSES):
                    o = pe.matmul(v_ps[:, 0:KV], clT[x][:, k, :], wkv[y][:, k, KV:2 * KV],
                                  start=(k == 0 and n == 0), stop=(k == KC - 1 and n == 2))
            o.then_inc(kvl_done, 1)
            for m in range(4):
                transpose_context(0, 0, m)
            pe.wait_ge(vl_copied, 1)
            pe.wait_ge(kl_l_ready, 1)
            pe.wait_ge(cT_l_ready, 2)
            for first in (True, False):
                keys(0, 0, 0, first)

            def step(b, par):
                st = Stages(b)
                for s in range(NG):
                    if s == 3 and st.rest:
                        pe.wait_ge(last_copied, b - 1)
                        pe.wait_ge(vl_loaded[par], 8 * (b - 2 - par) + 16)
                        for j in range(2):
                            o = pe.matmul(o_ps[:, j * P:(j + 1) * P], vl[:, par, j * P:(j + 1) * P], plT[:, :],
                                          start=False, stop=(j == 1), skip_group_check=True)
                        o.then_inc(o_done, 1)
                    if st.heads:
                        if s == 0:
                            pe.wait_ge(qcat_loaded[1 - par], 32 * (b - 2 + par) + 64)
                            pe.wait_ge(kcat_loaded[1 - par], 32 * (b - 2 + par) + 64)
                        if not known(b) or NG * (b - 1) + s >= 2:
                            pe.wait_ge(exp_done, NG * (b - 1) + s - 1)
                        pe.matmul(s_ps[s % 2][:, 0:SKP], qcat[:, 1 - par, cat_index(s), :], kcat[:, 1 - par, cat_index(s), :], start=True, stop=True).then_inc(s_done, 1)
                    if s < 2 and st.rest:
                        turn_prob(b - 2, par, s + 6)
                    if s == 1 and st.rest:
                        pe.wait_ge(v_copied, b if st.project else B)
                        turn(v_ps, [(NG, prob[:, par, :, SK - 1])]).then_inc(last_turned, 1)
                    if s == 0 and st.project:
                        pe.wait_ge(cT_l_ready, 4 * b + 3)
                    if s == 3 and st.project and (not known(b) or b >= 1):
                        pe.wait_ge(v_copied, b)
                        if not known(b) or b >= 2:
                            pe.wait_ge(last_copied, b - 1)
                    if s == 7 and st.next:
                        pe.wait_ge(cT_l_ready, 4 * b + 6)
                        pe.wait_ge(kT_l_ready, b + 1)
                    project(b, par, s, True)
                    if s >= 2 and st.heads:
                        turn_prob(b - 1, 1 - par, s - 2)
                    if s % 2 == 0 and st.next:
                        transpose_context(b + 1, 1 - par, s // 2)
                    if s == 0 and st.project:
                        pe.wait_ge(cT_l_ready, 4 * b + 4)
                    project(b, par, s, False)
                    if s == 6 and st.heads:
                        times_values(b - 1, 1 - par, 0)
                    if s == 2 and st.rest:
                        times_values(b - 2, par, 1)
            over_batches(pe, step)


MT = 2 * NT + E - 1
AHEAD = 3
COLS = MT + AHEAD
ROWS = (E - 1) * B * SQ + (COLS - E + 1) * P


def split_low(dve, sh, e, c):
    high, low = (part[:, e * SLOT + c * D:e * SLOT + (c + 1) * D] for part in sh.w)
    dve.wait_ge(sh.w_h_ready, KC * e + c + 1)
    dve.tensor_tensor(low, sh.first_raw[e][:, c, :], high.bitcast(F32), ALU.subtract).then_inc(sh.w_l_ready, 1)


def mixing(nc, sh, x, eta, gate, expert_w, out, n_dram, slot_dram):
    with ExitStack() as ctx:
        sb = lambda *a: ctx.enter_context(nc.sbuf_tensor(*a))
        sem = lambda n: ctx.enter_context(nc.semaphore(n))
        ident, banks, oT, wo_s, chunk_loaded = sh.ident, sh.banks, sh.oT, sh.wo, sh.chunk_loaded
        w_h_ready, w_l_ready, tiles = sh.w_h_ready, sh.w_l_ready, sh.tiles
        raw = sh.first_raw
        first_experts = [[sh.w[part][:, e * SLOT:(e + 1) * SLOT].rearrange("p (c n) -> p c n", n=D) for part in range(2)]
                         for e in range(2)]
        ot = [sb("ot_h", [P, 2, KC, P], F32R), sb("ot_l", [P, 2, KC, P], F32R)]
        x_in, x2 = sh.at("x_in2", STAGE, [P, 2, D]), sh.at("x2", STAGE + 8 * D, [P, 2, D])
        y = sb("y", [P, 2, D], F32)
        yT = sb("yT", [P, D], F32)
        x3 = sb("x3", [P, 2, D], F32)
        n = sb("n", [P, 2, D], F32)
        x3z = n
        nT = sb("nT", [P, D], F32)
        gate_sb = sb("gate_sb", [P, KC, E], F32)
        eta_sb = sb("eta_sb", [P, 1], F32)
        low = sb("low", [P, 1], F32)
        prob = sb("prob2", [P, SQ], F32)
        psum_row = sb("psum_row", [P, 1], F32)
        scale = sb("scale", [P, 2, 1], F32)
        probT = sb("probT", [P, P], F32)
        logits = sb("logits", [P, E], F32)
        top = sb("top", [P, E], F32)
        top_i = sb("top_i", [P, E], U32)
        gap = sb("gap", [P, 1], F32)
        egap = sb("egap", [P, 1], F32)
        chosen_f = sb("chosen_f", [P, 2], F32)
        hot = sb("hot", [P, 2, E], F32)
        both = sb("both", [P, E], F32)
        before = sb("before", [P, E], F32)
        ranked = sb("ranked", [P, E], F32)
        row = sb("row", [P, 2, E], F32)
        slot = sb("slot", [P, 2 * NT], I32)
        earlier = sb("earlier", [P, P], F32)
        ones = sb("ones", [P, P], F32)
        expert_iota = sb("expert_iota", [P, E], F32)
        region = sb("region", [P, E], F32)
        entries = sb("entries", [P, 4 * NT], I32)
        no_tokens = sb("no_tokens", [P, 2 * ROWS // P], I32)
        counts = sb("counts", [P, E], F32)
        steps128 = sb("steps128", [P, E, NT], F32)
        over = sb("over", [P, E, NT], F32)
        n_tiles = sb("n_tiles", [P, E], F32)
        n_tiles1 = sb("n_tiles1", [P, E], F32)
        first = sb("first", [P, E], F32)
        zero8 = sb("zero8", [P, E], F32)
        slot_f = sb("slot_f", [P, 2], F32)
        tile_iota = sb("tile_iota", [1, COLS], F32)
        reached = sb("reached", [1, COLS, E], F32)
        start = sb("start", [1, COLS, E], F32)
        e_f = sb("e_f", [1, 2, COLS], F32)
        f_f = sb("f_f", [1, 2, COLS], F32)
        only = sb("only", [1, COLS], F32)
        norm2 = Norm(nc, ctx, "norm2")
        norm3 = Norm(nc, ctx, "norm3")
        o_ps, t_ps, r_ps, g_ps, e_ps = banks[0:2], banks[2:4], banks[4:6], banks[6], banks[7]

        x_loaded = [sem("x2_loaded0"), sem("x2_loaded1")]
        small_loaded, slots_cleared = sem("small_loaded"), sem("slots_cleared")
        consts = sem("consts")
        ot_h_ready, ot_l_ready, xo_done, x2_ready, y_ready = sem("ot_h_ready"), sem("ot_l_ready"), sem("xo_done"), sem("x2_ready"), sem("y_ready")
        t_done, t_copied, g_done, low_ready, prob_ready, probT_ready = (
            sem("t_done"), sem("t_copied"), sem("g_done"), sem("low_ready"), sem("prob_ready"), sem("probT_ready"))
        psr_ready, scale_ready, r_done, z_ready, x3_ready, n_ready = (
            sem("psr_ready"), sem("scale_ready"), sem("r_done"), sem("z_ready"), sem("x3_ready"), sem("n_ready"))
        x3_stored = [sem("x3_stored0"), sem("x3_stored1")]
        gate_done, route, gap_ready, egap_ready, both_ready, rank_done, rows_ready = (
            sem("gate_done"), sem("route"), sem("gap_ready"), sem("egap_ready"), sem("both_ready"),
            sem("rank_done"), sem("rows_ready"))
        scattered, counted, plan, passed = sem("scattered"), sem("counted"), sem("plan"), sem("passed2")
        N_STEPS = NT + 3

        def steps(eng, step):
            pipelined(eng, N_STEPS, step, head=3, tail=4)

        def on(t, lag):
            return not known(t) or 0 <= t - lag < NT

        block = ctx.enter_context(nc.Block())

        def halves(n):
            return [(n // 2, n % 2 * KC // 2 + c) for c in range(KC // 2)] if 0 <= n < 4 else []

        def turned_before(t):
            if known(t):
                return sum((0 <= s - 1 < NT) + (0 <= s - 2 < NT) for s in range(t))
            return 2 * t - 3

        @block.sync
        def _(sp):
            def load_x(t, par):
                sp.dma_start(x_in[:, par, :], x[bass.ts(t, P), :]).then_inc(x_loaded[par], 16)
            load_x(0, 0)
            load_x(1, 1)
            sp.dma_start(gate_sb[:, :, :], gate.rearrange("(c p) e -> p c e", p=P)).then_inc(small_loaded, 16)
            sp.dma_start(eta_sb[:, :], eta.rearrange("(a b) -> a b", a=1).to_broadcast([P, 1])).then_inc(small_loaded, 16)
            sp.wait_ge(consts, 10)
            sp.dma_start(slot_dram.rearrange("(p n) o -> p (n o)", p=P), no_tokens[:, :]).then_inc(slots_cleared, 16)

            def step(t, par):
                if not known(t) or 1 <= t < NT - 1:
                    sp.wait_ge(x2_ready, 2 * t)
                    load_x(t + 1, 1 - par)
                if known(t) and t in (2, NT):
                    e = int(t == NT)
                    if e == 1:
                        sp.wait_ge(xo_done, 2 * NT)
                    for c in range(KC):
                        sp.dma_start(raw[e][:, c, :], expert_w[e, c * P:(c + 1) * P, :]).then_inc(chunk_loaded[c], 16)
                if on(t, 2):
                    sp.wait_ge(n_ready, t - 1)
                    sp.dma_start(n_dram[bass.ds((t - 2) * P, P), :], n[:, par, :]).then_inc(x3_stored[par], 16)
                    sp.dma_start(out[bass.ds((t - 2) * P, P), :], x3[:, par, :]).then_inc(x3_stored[par], 16)
            steps(sp, step)
            for par in range(2):
                sp.wait_ge(x3_stored[par], 32 * NT // 2)

        @block.gpsimd
        def _(pool):
            pool.memset(probT[:, :], 0.0).then_inc(consts, 1)
            pool.memset(ones[:, :], 1.0).then_inc(consts, 1)
            pool.memset(before[:, :], 0.0).then_inc(consts, 1)
            pool.iota(no_tokens[:, :], [[1, 2 * ROWS // P]], base=B * SQ, channel_multiplier=2 * ROWS // P).then_inc(consts, 1)
            pool.memset(zero8[:, :], 0.0).then_inc(consts, 1)
            pool.iota(expert_iota[:, :], [[1, E]], base=0, channel_multiplier=0, allow_small_or_imprecise_dtypes=True).then_inc(consts, 1)
            pool.iota(region[:, :], [[B * SQ, E]], base=0, channel_multiplier=0, allow_small_or_imprecise_dtypes=True).then_inc(consts, 1)
            pool.iota(entries[:, :].rearrange("p (t k c) -> p t k c", k=2, c=2)[:, :, :, 0], [[P, NT], [0, 2]], base=0,
                      channel_multiplier=1).then_inc(consts, 1)
            pool.iota(steps128[:, :, :], [[0, E], [P, NT]], base=0, channel_multiplier=0, allow_small_or_imprecise_dtypes=True).then_inc(consts, 1)
            pool.iota(tile_iota[:, :], [[1, COLS]], base=0, channel_multiplier=0, allow_small_or_imprecise_dtypes=True).then_inc(consts, 1)
            pool.wait_ge(consts, 10)
            pool.affine_select(out=earlier[:, :], in_=ones[:, :], compare_op=ALU.is_gt, fill=0.0, base=0,
                               pattern=[[1, P]], channel_multiplier=-1).then_inc(consts, 1)
            norm2.start_gpsimd(pool)
            norm3.start_gpsimd(pool)
            pool.wait_ge(slots_cleared, 16)

            def step(t, par):
                if on(t, 1):
                    norm2.on_gpsimd(pool, t - 1)
                if on(t, 2):
                    for h in range(2):
                        pool.wait_ge(z_ready, 2 * (t - 2) + h + 1)
                        if h == 0 and (not known(t) or t >= 4):
                            pool.wait_ge(x3_stored[par], (t - 2 - par) * 16)
                        pool.tensor_tensor(x3[:, par, h * 512:(h + 1) * 512], x2[:, par, h * 512:(h + 1) * 512],
                                           x3z[:, par, h * 512:(h + 1) * 512], ALU.add).then_inc(x3_ready, 1)
                    norm3.on_gpsimd(pool, t - 2)
                if on(t, 3):
                    wait_apart(pool, rows_ready, t - 2, passed)
                    for c in range(2):
                        pool.indirect_dma_start(slot_dram, bass.IndirectOffsetOnAxis(ap=slot_of(t - 3, c), axis=0),
                                                entry_of(t - 3, c), None).then_inc(scattered, 16)
            def slot_of(t, c):
                return slot[:, bass.ds(2 * t + c, 1)]

            def entry_of(t, c):
                return entries[:, bass.ds(4 * t + 2 * c, 2)]
            for t in range(N_STEPS):
                step(t, t % 2)
            pool.wait_ge(scattered, 16 * 2 * NT)
            pool.dma_start(sh.idx[:, 0, :], slot_dram[0:P, :]).then_inc(sh.idx_loaded, 16)
            pool.wait_ge(x2_ready, 2 * NT)
            for par in range(2):
                pool.wait_ge(x3_stored[par], 32 * NT // 2)
            pool.wait_ge(sh.idx_loaded, 16)
            pool.indirect_dma_start(sh.xg[:, 0, :], None, n_dram, bass.IndirectOffsetOnAxis(ap=sh.idx[:, 0, 0:1], axis=0),
                                    bounds_check=B * SQ - 1, oob_is_err=False).then_inc(sh.xg_loaded, 16)

        @block.scalar
        def _(act):
            def ot_high(t, par):
                if not known(t) or t >= 2:
                    act.wait_ge(xo_done, 2 * t - 2)
                act.activation(ot[0][:, par, :, :], oT[:, :, bass.ds(t * P, P)], ACT.Copy).then_inc(ot_h_ready, 1)
            ot_high(0, 0)

            def copy_turned(dst, number):
                for h in range(2):
                    act.wait_ge(t_done, 2 * number + h + 1)
                    act.activation(dst[:, h * 512:(h + 1) * 512], t_ps[h][:, :], ACT.Copy).then_inc(t_copied, 1)

            def step(t, par):
                if on(t, -1) and on(t, 0):
                    ot_high(t + 1, 1 - par)
                if on(t, 1):
                    if not known(t) or t >= 2:
                        act.wait_ge(g_done, t - 1)
                    copy_turned(yT, turned_before(t))
                if on(t, 2):
                    if not known(t) or t >= 3:
                        act.wait_ge(gate_done, t - 2)
                    copy_turned(nT, turned_before(t) + (1 if on(t, 1) else 0))
                if on(t, 3):
                    act.wait_ge(gap_ready, t - 2)
                    act.activation(egap[:, :], gap[:, :], ACT.Exp).then_inc(egap_ready, 1)
                if on(t, 1):
                    act.wait_ge(low_ready, t)
                    act.activation(prob[:, :], g_ps[:, 0:SQ], ACT.Exp, bias=low[:, 0:1], scale=-1.0,
                                   accum_out=psum_row[:, :]).then_inc(prob_ready, 1)
                for e, c in halves(t - (NT - 1)) if known(t) else ():
                    act.wait_ge(ot_l_ready, NT)
                    act.wait_ge(chunk_loaded[c], 48 + 16 * e)
                    act.activation(first_experts[e][0][:, c, :], raw[e][:, c, :], ACT.Copy).then_inc(w_h_ready, 1)
            steps(act, step)

        @block.vector
        def _(dve):
            def ot_low(t, par):
                dve.wait_ge(ot_h_ready, t + 1)
                dve.tensor_tensor(ot[1][:, par, :, :], oT[:, :, bass.ds(t * P, P)], ot[0][:, par, :, :].bitcast(F32), ALU.subtract).then_inc(ot_l_ready, 1)
            ot_low(0, 0)
            dve.wait_ge(consts, 11)
            dve.wait_ge(small_loaded, 32)

            def step(t, par):
                if on(t, 1):
                    dve.wait_ge(x_loaded[1 - par], (t - 2 + par) * 8 + 16)
                    if not known(t) or t >= 3:
                        dve.wait_ge(x3_ready, 2 * (t - 3) + 2)
                    for h in range(2):
                        dve.wait_ge(xo_done, 2 * (t - 1) + h + 1)
                        dve.tensor_tensor(x2[:, 1 - par, h * 512:(h + 1) * 512], o_ps[h][:, :], x_in[:, 1 - par, h * 512:(h + 1) * 512], ALU.add).then_inc(x2_ready, 1)
                    dve.wait_ge(x2_ready, 2 * t)
                    norm2.on_vector(dve, t - 1, y[:, 1 - par, :], x2[:, 1 - par, :]).then_inc(y_ready, 1)
                if on(t, 2):
                    if not known(t) or t >= 4:
                        dve.wait_ge(x3_stored[par], (t - 2 - par) * 16)
                    wait_apart(dve, scale_ready, t - 1, passed)
                    for h in range(2):
                        dve.wait_ge(r_done, 2 * (t - 2) + h + 1)
                        dve.scalar_tensor_tensor(out=x3z[:, par, h * 512:(h + 1) * 512], in0=r_ps[h][:, :], scalar=scale[:, par, :],
                                                 in1=y[:, par, h * 512:(h + 1) * 512], op0=ALU.mult, op1=ALU.add).then_inc(z_ready, 1)
                if on(t, 3):
                    route_tile(t - 3)
                if on(t, 2):
                    dve.wait_ge(x3_ready, 2 * (t - 2) + 2)
                    norm3.on_vector(dve, t - 2, n[:, par, :], x3[:, par, :]).then_inc(n_ready, 1)
                if on(t, -1) and on(t, 0):
                    ot_low(t + 1, 1 - par)
                for e, c in halves(t - NT) if known(t) and t <= NT + 1 else ():
                    split_low(dve, sh, e, c)
                if on(t, 3):
                    rank_tile(t - 3)
                if on(t, 1):
                    dve.wait_ge(g_done, t)
                    dve.tensor_reduce(low[:, :], g_ps[:, 0:SQ], AXX, ALU.min).then_inc(low_ready, 1)
                    dve.wait_ge(prob_ready, t)
                    dve.reciprocal(scale[:, 1 - par, :], psum_row[:, :]).then_inc(psr_ready, 1)
                    if not known(t) or t >= 2:
                        dve.wait_ge(r_done, 2 * (t - 1))
                    for b in range(BT):
                        q = slice(b * SQ, (b + 1) * SQ)
                        o = dve.transpose(probT[q, q], prob[q, :])
                    o.then_inc(probT_ready, 1)
                    dve.wait_ge(psr_ready, t)
                    dve.tensor_scalar(scale[:, 1 - par, :], scale[:, 1 - par, :], eta_sb[:, 0:1], None, ALU.mult).then_inc(scale_ready, 1)
            def chain(o, count):
                o.then_inc(route, 1)
                wait_apart(dve, route, count, passed)

            def route_tile(t):
                c = 12 * t
                dve.wait_ge(gate_done, t + 1)
                chain(dve.tensor_copy(logits[:, :], e_ps[:, 0:E]), c + 1)
                chain(dve.max(top[:, :], logits[:, :]), c + 2)
                dve.tensor_tensor(gap[:, :], top[:, 1:2], top[:, 0:1], ALU.subtract).then_inc(gap_ready, 1)
                chain(dve.max_index(top_i[:, :], top[:, :], logits[:, :]), c + 3)
                chain(dve.tensor_copy(chosen_f[:, :], top_i[:, 0:2]), c + 4)
                for k in range(2):
                    chain(dve.tensor_scalar(hot[:, k, :], expert_iota[:, :], chosen_f[:, k:k + 1], None, ALU.is_equal), c + 5 + k)
                dve.tensor_tensor(both[:, :], hot[:, 0, :], hot[:, 1, :], ALU.add).then_inc(both_ready, 1)

            def rank_tile(t):
                c = 12 * t
                dve.wait_ge(egap_ready, t + 1)
                chain(dve.tensor_scalar(chosen_f[:, 0:1], egap[:, :], 1.0, None, ALU.add), c + 7)
                weight = [entries[:, bass.ds(4 * t + 2 * k + 1, 1)].bitcast(F32) for k in range(2)]
                chain(dve.reciprocal(weight[0], chosen_f[:, 0:1]), c + 8)
                dve.tensor_tensor(weight[1], egap[:, :], weight[0], ALU.mult)
                dve.wait_ge(rank_done, t + 1)
                chain(dve.tensor_tensor(ranked[:, :], e_ps[:, 64:64 + E], region[:, :], ALU.add), c + 9)
                dve.tensor_tensor(before[:, :], before[:, :], both[:, :], ALU.add)
                chain(dve.tensor_tensor(row[:, :, :], hot[:, :, :], ranked[:, :].unsqueeze(1).to_broadcast([P, 2, E]), ALU.mult), c + 10)
                chain(dve.tensor_reduce(slot_f[:, :], row[:, :, :], AXX, ALU.add), c + 11)
                chain(dve.tensor_copy(slot[:, bass.ds(2 * t, 2)], slot_f[:, :]), c + 12)
                dve.sem_inc(rows_ready, 1)
            steps(dve, step)

            pc = [0]

            def then(o):
                pc[0] += 1
                o.then_inc(plan, 1)
                dve.wait_ge(plan, pc[0])
            dve.wait_ge(counted, 1)
            then(dve.tensor_copy(counts[:, :], e_ps[:, 0:E]))
            then(dve.tensor_tensor(over[:, :, :], counts[:, :].unsqueeze(2).to_broadcast([P, E, NT]), steps128[:, :, :], ALU.is_gt))
            then(dve.tensor_reduce(n_tiles[:, :], over[:, :, :], AXX, ALU.add))
            then(dve.tensor_scalar(n_tiles1[:, :], n_tiles[:, :], 1.0, None, ALU.max))
            then(dve.tensor_tensor_scan(first[:, :], n_tiles1[:, :], zero8[:, :], 0.0, ALU.add, ALU.add))
            then(dve.tensor_tensor(f_f[:, 0, :], tile_iota[:, :], first[0:1, E - 1:E].to_broadcast([1, COLS]), ALU.is_lt))
            then(dve.tensor_copy(tiles[:, 3, :], f_f[:, 0, :]))
            then(dve.tensor_copy(tiles[:, 4, :], first[0:1, E - 1:E].to_broadcast([1, COLS])))
            then(dve.tensor_tensor(first[:, :], first[:, :], n_tiles1[:, :], ALU.subtract))
            first_b = first[0:1, :].unsqueeze(1).to_broadcast([1, COLS, E])
            then(dve.tensor_tensor(reached[:, :, :], tile_iota[:, :].unsqueeze(2).to_broadcast([1, COLS, E]), first_b, ALU.is_ge))
            then(dve.tensor_tensor(start[:, :, :], reached[:, :, :], first_b, ALU.mult))
            then(dve.tensor_reduce(e_f[:, 0, :], reached[:, :, :], AXX, ALU.add))
            then(dve.tensor_reduce(e_f[:, 1, :], start[:, :, :], AXX, ALU.max))
            then(dve.tensor_scalar(f_f[:, 0, :], e_f[:, 0, :], -1.0, None, ALU.add))
            then(dve.tensor_tensor(f_f[:, 1, :], tile_iota[:, :], e_f[:, 1, :], ALU.subtract))
            then(dve.tensor_copy(tiles[:, 0, :], f_f[:, 0, :]))
            then(dve.tensor_copy(tiles[:, 1, :], f_f[:, 1, :]))
            then(dve.memset(only[:, :], 0.0))
            then(dve.tensor_tensor(only[:, 0:COLS - 1], f_f[:, 0, 1:COLS], f_f[:, 0, 0:COLS - 1], ALU.is_gt))
            then(dve.tensor_scalar(e_f[:, 0, :], f_f[:, 1, :], 0.0, None, ALU.is_equal))
            then(dve.tensor_scalar(e_f[:, 1, :], f_f[:, 0, :], float(E - 1), None, ALU.is_lt))
            then(dve.tensor_scalar(f_f[:, 0, :], f_f[:, 0, :], 0.0, None, ALU.is_gt))
            then(dve.tensor_tensor(e_f[:, 1, :], e_f[:, 1, :], f_f[:, 0, :], ALU.mult))
            then(dve.tensor_tensor(f_f[:, 0, :], e_f[:, 0, :], e_f[:, 1, :], ALU.mult))
            then(dve.tensor_copy(tiles[:, 2, :], f_f[:, 0, :]))
            then(dve.tensor_tensor(only[:, :], only[:, :], f_f[:, 0, :], ALU.mult))
            then(dve.tensor_scalar(e_f[:, 0, :], f_f[:, 1, :], 1.0, None, ALU.is_equal))
            then(dve.tensor_tensor(e_f[:, 0, :], e_f[:, 0, :], e_f[:, 1, :], ALU.mult))
            then(dve.tensor_copy(tiles[:, 5, :], e_f[:, 0, :]))
            then(dve.tensor_copy(tiles[:, 6, :], only[:, :]))
            for c in range(2):
                split_low(dve, sh, 1, c)

        @block.tensor
        def _(pe):
            def product(t, par, unit):
                h = unit // 4
                if unit == 0:
                    pe.wait_ge(ot_l_ready, t + 1)
                if unit % 4 == 0 and (not known(t) or t >= 1):
                    pe.wait_ge(x2_ready, 2 * (t - 1) + h + 1)
                for k in range(unit % 4 * 2, unit % 4 * 2 + 2):
                    for m, (a, b) in enumerate(PASSES):
                        o = pe.matmul(o_ps[h][:, :], ot[a][:, par, k, :], wo_s[b][:, k, h * 512:(h + 1) * 512],
                                      start=(k == 0 and m == 0), stop=(k == KC - 1 and m == 2))
                if unit % 4 == 3:
                    o.then_inc(xo_done, 1)

            def turn(src, number):
                for k in range(KC):
                    if k % 4 == 0 and (not known(number) or number >= 1):
                        pe.wait_ge(t_copied, 2 * (number - 1) + k // 4 + 1)
                    o = pe.transpose(t_ps[k // 4][:, k % 4 * P:(k % 4 + 1) * P], src[:, k * P:(k + 1) * P], ident[:, :])
                    if k % 4 == 3:
                        o.then_inc(t_done, 1)

            def step(t, par):
                if known(t) and t == 1:
                    pe.wait_ge(consts, 11)
                    pe.wait_ge(small_loaded, 32)
                for unit in range(KC):
                    if unit == 7 and on(t, 3):
                        pe.wait_ge(both_ready, t - 2)
                        pe.matmul(e_ps[:, 64:64 + E], earlier[:, :], both[:, :], start=True, stop=False)
                        pe.matmul(e_ps[:, 64:64 + E], ones[:, :], before[:, :], start=False, stop=True).then_inc(rank_done, 1)
                    if unit == 2 and on(t, 2):
                        pe.wait_ge(probT_ready, t - 1)
                        for h in range(2):
                            if not known(t) or t >= 3:
                                pe.wait_ge(z_ready, 2 * (t - 3) + h + 1)
                            pe.matmul(r_ps[h][:, :], probT[:, :], y[:, par, h * 512:(h + 1) * 512], start=True, stop=True).then_inc(r_done, 1)
                    if unit == 4 and on(t, 1):
                        pe.wait_ge(y_ready, t)
                        turn(y[:, 1 - par, :], turned_before(t))
                    if unit == 6 and on(t, 2):
                        pe.wait_ge(n_ready, t - 1)
                        turn(n[:, par, :], turned_before(t) + (1 if on(t, 1) else 0))
                    if unit == 6 and on(t, 1):
                        pe.wait_ge(t_copied, 2 * turned_before(t) + 2)
                        if not known(t) or t >= 2:
                            pe.wait_ge(prob_ready, t - 1)
                        for k in range(KC):
                            for b in range(BT):
                                rows = yT[:, k * P + b * SQ:k * P + (b + 1) * SQ]
                                o = pe.matmul(g_ps[b * SQ:(b + 1) * SQ, 0:SQ], rows, rows, start=(k == 0), stop=(k == KC - 1), skip_group_check=True)
                        o.then_inc(g_done, 1)
                    if on(t, 0):
                        product(t, par, unit)
                if on(t, 2):
                    pe.wait_ge(t_copied, 2 * (turned_before(t) + (1 if on(t, 1) else 0)) + 2)
                    if not known(t) or t >= 3:
                        pe.wait_ge(rows_ready, t - 2)
                    for k in range(KC):
                        o = pe.matmul(e_ps[:, 0:E], nT[:, k * P:(k + 1) * P], gate_sb[:, k, :], start=(k == 0), stop=(k == KC - 1))
                    o.then_inc(gate_done, 1)
            steps(pe, step)
            pe.wait_ge(rows_ready, NT)
            pe.matmul(e_ps[:, 0:E], ones[:, :], before[:, :], start=True, stop=True).then_inc(counted, 1)


def experts(nc, sh, expert_w, n_dram, slot_dram, out):
    with ExitStack() as ctx:
        sb = lambda *a: ctx.enter_context(nc.sbuf_tensor(*a))
        sem = lambda n: ctx.enter_context(nc.semaphore(n))
        ident, banks, w, tiles, chunk_loaded, w_h_ready, w_l_ready = (
            sh.ident, sh.banks, sh.w, sh.tiles, sh.chunk_loaded, sh.w_h_ready, sh.w_l_ready)
        raw = sb("raw", [P, KC, D], F32)
        gT = [sb("gT_h", [P, 2, D], F32R), sb("gT_l", [P, 2, D], F32R)]
        idx, xg, idx_loaded, xg_loaded = sh.idx, sh.xg, sh.idx_loaded, sh.xg_loaded
        idx_out = sb("idx_out", [P, 2, 2], I32)
        acc = sh.at("acc", STAGE + 8 * D, [P, 2, D])
        t_ps, y_ps = banks[0:2], [banks[2:4], banks[4:6]]

        gT_done, gT_h_ready, gT_l_ready = sem("gT_done"), sem("gT_h_ready"), sem("gT_l_ready")
        idx_out_loaded, acc_loaded, y_done, acc_ready, written = (
            sem("idx_out_loaded"), sem("acc_loaded"), sem("y_done"), sem("acc_ready"), sem("written"))
        passed = sem("passed3")

        def entry(eng, i, what, most):
            return eng.value_load(tiles[0:1, what, bass.ds(i, 1)], min_val=0, max_val=most)

        def steps(eng, step):
            def step_if_used(i, par):
                if known(i) and i < E:
                    step(i, par)
                else:
                    with eng.If(entry(eng, i, 3, 1) > 0):
                        step(i, par)
            pipelined(eng, MT, step_if_used, head=3, tail=2)

        block = ctx.enter_context(nc.Block())

        @block.sync
        def _(sp):
            def load_chunk(e, c):
                sp.dma_start(raw[:, c, :], expert_w[bass.ds(e, 1), c * P:(c + 1) * P, :].rearrange("o p n -> p (o n)")).then_inc(chunk_loaded[c], 16)
            sp.wait_ge(xg_loaded, 32)
            for c in range(KC):
                if c >= 2:
                    sp.wait_ge(chunk_loaded[c - 2], 80)
                load_chunk(2, c)
            with sp.Fori(3, E) as e:
                for c in range(KC):
                    sp.wait_ge(w_l_ready, KC * e - KC + c + 1)
                    load_chunk(e, c)

        @block.gpsimd
        def _(pool):
            def first_row(i):
                e = entry(pool, i, 0, E - 1)
                j = entry(pool, i, 1, COLS - E)
                return pool.snap(e * (B * SQ) + j * P, min_val=0, max_val=ROWS - P)

            def load_idx(dst, i, par):
                return pool.dma_start(dst[:, par, :], slot_dram[bass.ds(first_row(i), P), :])

            def gather(i, par):
                wait_apart(pool, idx_loaded, 16 * i + 16, passed)
                pool.indirect_dma_start(xg[:, par, :], None, n_dram, bass.IndirectOffsetOnAxis(ap=idx[:, par, 0:1], axis=0),
                                        bounds_check=B * SQ - 1, oob_is_err=False).then_inc(xg_loaded, 16)

            load_idx(idx, 1, 1).then_inc(idx_loaded, 16)
            pool.wait_ge(xg_loaded, 16)
            gather(1, 1)
            load_idx(idx, 2, 0).then_inc(idx_loaded, 16)
            load_idx(idx_out, 0, 0).then_inc(idx_out_loaded, 16)
            pool.wait_ge(xg_loaded, 32)

            def step(i, par):
                pool.wait_ge(gT_done, 2 * i + 2)
                gather(i + 2, par)
                if not known(i) or i >= 1:
                    wait_apart(pool, written, 16 * i, passed)
                wait_apart(pool, idx_out_loaded, 16 * i + 16, passed)
                pool.indirect_dma_start(acc[:, par, :], None, out, bass.IndirectOffsetOnAxis(ap=idx_out[:, par, 0:1], axis=0),
                                        bounds_check=B * SQ - 1, oob_is_err=False).then_inc(acc_loaded, 16)
                load_idx(idx_out, i + 1, 1 - par).then_inc(idx_out_loaded, 16)
                pool.wait_ge(xg_loaded, 16 * i + 48)
                load_idx(idx, i + 3, 1 - par).then_inc(idx_loaded, 16)
                wait_apart(pool, acc_ready, 2 * i + 2, passed)
                pool.indirect_dma_start(out, bass.IndirectOffsetOnAxis(ap=idx_out[:, par, 0:1], axis=0), acc[:, par, :], None,
                                        bounds_check=B * SQ - 1, oob_is_err=False).then_inc(written, 16)
            steps(pool, step)
            used = pool.value_load(tiles[0:1, 4, 0:1], min_val=E, max_val=MT)
            pool.wait_ge(idx_loaded, used * 16 + 48)
            pool.wait_ge(idx_out_loaded, used * 16 + 16)
            pool.wait_ge(written, used * 16)

        @block.scalar
        def _(act):
            def rows_high(i, par):
                if not known(i) or i >= 2:
                    act.wait_ge(y_done, 2 * i - 2)
                for h in range(2):
                    act.wait_ge(gT_done, 2 * i + h + 1)
                    act.activation(gT[0][:, par, h * 512:(h + 1) * 512], t_ps[h][:, :], ACT.Copy).then_inc(gT_h_ready, 1)

            def split_high(e, slot, half):
                for c in range(half * KC // 2, (half + 1) * KC // 2):
                    act.wait_ge(chunk_loaded[c], 16 * e + 48)
                    act.activation(w[0][:, bass.ds(slot + c * D, D)], raw[:, c, :], ACT.Copy).then_inc(w_h_ready, 1)
            rows_high(0, 0)

            def step(i, par):
                e = entry(act, i, 0, E - 1)
                for half, what in ((1, 5), (0, 2), (1, 6)):
                    if what == 2:
                        rows_high(i + 1, 1 - par)
                    flag = entry(act, i, what, 1)
                    with act.If(flag > 0):
                        if half == 0 and (not known(i) or i >= 1):
                            act.wait_ge(y_done, 2 * i)
                        split_high(e + 1, (e + 1) % 2 * SLOT, half)
            steps(act, step)

        @block.vector
        def _(dve):
            def rows_low(i, par):
                for h in range(2):
                    dve.wait_ge(gT_h_ready, 2 * i + h + 1)
                    dve.tensor_tensor(gT[1][:, par, h * 512:(h + 1) * 512], t_ps[h][:, :],
                                      gT[0][:, par, h * 512:(h + 1) * 512].bitcast(F32), ALU.subtract).then_inc(gT_l_ready, 1)

            def split_lows(e, slot, half):
                for c in range(half * KC // 2, (half + 1) * KC // 2):
                    dve.wait_ge(w_h_ready, KC * e + c + 1)
                    dve.tensor_tensor(w[1][:, bass.ds(slot + c * D, D)], raw[:, c, :],
                                      w[0][:, bass.ds(slot + c * D, D)].bitcast(F32), ALU.subtract).then_inc(w_l_ready, 1)
            rows_low(0, 0)

            def step(i, par):
                e = entry(dve, i, 0, E - 1)
                for half, what in ((1, 5), (0, 2), (1, 6)):
                    if what == 2:
                        rows_low(i + 1, 1 - par)
                        if known(i) and i == 0:
                            for c in range(2, KC):
                                split_low(dve, sh, 1, c)
                    flag = entry(dve, i, what, 1)
                    with dve.If(flag > 0):
                        split_lows(e + 1, (e + 1) % 2 * SLOT, half)
                wait_apart(dve, acc_loaded, 16 * i + 16, passed)
                for h in range(2):
                    wait_apart(dve, y_done, 2 * i + h + 1, passed)
                    cols = slice(h * 512, (h + 1) * 512)
                    dve.scalar_tensor_tensor(out=acc[:, par, cols], in0=y_ps[par][h][:, :], scalar=idx_out[:, par, 1:2].bitcast(F32),
                                             in1=acc[:, par, cols], op0=ALU.mult, op1=ALU.add).then_inc(acc_ready, 1)
            steps(dve, step)

        @block.tensor
        def _(pe):
            def turn(i, par):
                pe.wait_ge(xg_loaded, 16 * i + 16)
                for k in range(KC):
                    if k % 4 == 0 and (not known(i) or i >= 1):
                        pe.wait_ge(gT_l_ready, 2 * i - 1 + k // 4)
                    o = pe.transpose(t_ps[k // 4][:, k % 4 * P:(k % 4 + 1) * P], xg[:, par, k * P:(k + 1) * P], ident[:, :])
                    if k % 4 == 3:
                        o.then_inc(gT_done, 1)
            turn(0, 0)

            def step(i, par):
                e = entry(pe, i, 0, E - 1)
                slot = pe.snap(e % 2 * SLOT, min_val=0, max_val=SLOT)
                pe.wait_ge(w_l_ready, KC * e + KC)
                pe.wait_ge(gT_l_ready, 2 * i + 2)
                if not known(i) or i >= 2:
                    pe.wait_ge(acc_ready, 2 * i - 2)
                for unit in range(KC):
                    h = unit // 4
                    if unit == 4:
                        turn(i + 1, 1 - par)
                    for k in range(unit % 4 * 2, unit % 4 * 2 + 2):
                        for n, (a, b) in enumerate(PASSES):
                            o = pe.matmul(y_ps[par][h][:, :], gT[a][:, par, k * P:(k + 1) * P],
                                          w[b][:, bass.ds(slot + (k * D + h * 512), 512)],
                                          start=(k == 0 and n == 0), stop=(k == KC - 1 and n == 2))
                    if unit % 4 == 3:
                        o.then_inc(y_done, 1)
            steps(pe, step)


def program(nc, x, context, wq, wk, wv, wo, eta, gate, expert_w, out):
    scratch = lambda name, shape, dt: nc.dram_tensor(name, shape, dt, kind="Internal").ap()
    q_dram = scratch("q_scratch", [2, NT, P, D], F32)
    k_dram = scratch("k_scratch", [2, 2, P, 2 * SKP], F32)
    vlast_dram = scratch("vlast_scratch", [B, NG, KV], F32)
    n_dram = scratch("n_scratch", [B * SQ, D], F32)
    slot_dram = scratch("slot_scratch", [ROWS, 2], I32)
    with ExitStack() as ctx:
        sh = Shared(nc, ctx)
        with nc.sbuf_tensor("cl", [B, D], F32) as cl:
            queries(nc, sh, x, wq, wk, wv, context, q_dram, cl)
            cross_attention(nc, sh, context, wo, q_dram, k_dram, vlast_dram, cl)
        mixing(nc, sh, x, eta, gate, expert_w, out, n_dram, slot_dram)
        experts(nc, sh, expert_w, n_dram, slot_dram, out)


def kernel(**inputs):
    import numpy as np
    import concourse.bacc as bacc
    from concourse.bass_utils import run_bass_kernel_spmd as run

    wq = inputs["L0_xattn_Wq"]
    wo = inputs["L0_xattn_Wo"]
    arrays = {
        "x": np.asarray(inputs["x"]).reshape(B * SQ, D),
        "context": np.asarray(inputs["ctx_4096"]),
        "wq": np.ascontiguousarray(np.asarray(wq).reshape(D, 2, 4, REP, DH).transpose(0, 1, 3, 2, 4).reshape(D, D)),
        "wk": np.asarray(inputs["L0_xattn_Wk"]),
        "wv": np.asarray(inputs["L0_xattn_Wv"]),
        "wo": np.ascontiguousarray(np.asarray(wo).reshape(2, 4, REP, DH, D).transpose(0, 2, 1, 3, 4).reshape(D, D)),
        "eta": np.asarray(inputs["L0_attn_eta"]),
        "gate": np.asarray(inputs["L0_ffn_gate_w"]),
        "expert_w": np.asarray(inputs["L0_ffn_expert_w"]),
    }
    nc = bacc.Bacc("TRN2", target_bir_lowering=False, num_devices=1)
    args = [nc.dram_tensor(f"in_{k}", a.shape, mybir.dt.from_np(a.dtype), kind="ExternalInput").ap() for k, a in arrays.items()]
    out = nc.dram_tensor("out_x", (B * SQ, D), F32, kind="ExternalOutput").ap()
    program(nc, *args, out)
    r = run(nc, [{f"in_{k}": a for k, a in arrays.items()}], core_ids=[0])
    return r.results[0]["out_x"].reshape(B, SQ, D)
```
